# Optimizing a Trainium2 kernel written in Bass

```python
import numpy as np
import jax
import jax.numpy as jnp

def _softmax(x, axis=-1):
    return jax.nn.softmax(x, axis=axis)

def _gelu(x):
    return jax.nn.gelu(x, approximate=True)

def _silu(x):
    return jax.nn.silu(x)

def _sigmoid(x):
    return jax.nn.sigmoid(x)

def _layernorm(x, axis=-1, eps=1e-05):
    m = jnp.mean(x, axis=axis, keepdims=True)
    v = jnp.var(x, axis=axis, keepdims=True)
    return (x - m) / jnp.sqrt(v + eps)

def _scatter_add(tgt, idx, src, axis=0):
    return tgt.at[idx].add(src)

def _segment_sum(src, seg, n):
    return jax.ops.segment_sum(src, seg, n)
kernel_name = 'mk_xattn_ffn_d1_seqx_r8_8507f4'

def setup_inputs(seed: int=0):
    np.random.seed(seed)
    _w = jnp.asarray

    def _rec_inputs():
        import jax
        import jax.numpy as jnp
        _rk = jax.random.key(seed)
        x = -0.0002928 + 1 * jax.random.normal(jax.random.fold_in(_rk, 1), (128, 64, 128), jnp.float32)
        _lenS = 64 - jax.random.randint(jax.random.fold_in(_rk, 7), (128,), 0, max(1, 64 // 4) + 1, jnp.int32)
        _lenS2 = 64 - jax.random.randint(jax.random.fold_in(_rk, 8), (128,), 0, max(1, 64 // 4) + 1, jnp.int32)
        _ctx_1024P = jax.random.normal(jax.random.fold_in(_rk, 11), (128, 16, 128), jnp.float32)
        _ctx_1024c = jax.random.dirichlet(jax.random.fold_in(_rk, 511), 0.3 * jnp.ones((16,), jnp.float32), (128, 64))
        _ctx_1024t = jnp.einsum('bsk,bkd->bsd', _ctx_1024c, _ctx_1024P)
        _ctx_1024t = _ctx_1024t * jax.lax.rsqrt(jnp.mean(jnp.square(_ctx_1024t)) + 1e-12) * 0.953939
        ctx_1024 = -1.39393e-06 + 0.999914 * (_ctx_1024t + 0.3 * jax.random.normal(jax.random.fold_in(_rk, 611), (128, 64, 128), jnp.float32))
        return (x, ctx_1024)
    x, ctx_1024 = _rec_inputs()

    def _L0_xattn_setup():
        import jax, jax.numpy as jnp
        import numpy as np
        EPS_BACKEND = 1e-06
        NORM_EPS = 1e-06
        NUM_HEADS = 4

        def _mlstm_forward(q, k, v, ig_kernel, ig_bias, fg_kernel, fg_bias, outnorm_weight):
            B, S, E = q.shape
            NH = ig_bias.shape[0]
            DH = E // NH
            gate_input = jnp.concatenate([q, k, v], axis=-1)
            igate = gate_input @ ig_kernel + ig_bias
            fgate = gate_input @ fg_kernel + fg_bias
            qh = q.reshape(B, S, NH, DH).transpose(0, 2, 1, 3)
            kh = k.reshape(B, S, NH, DH).transpose(0, 2, 1, 3)
            vh = v.reshape(B, S, NH, DH).transpose(0, 2, 1, 3)
            ig = igate.transpose(0, 2, 1)
            fg = fgate.transpose(0, 2, 1)
            log_fg = jax.nn.log_sigmoid(fg)
            cums = jnp.concatenate([jnp.zeros((B, NH, 1), log_fg.dtype), jnp.cumsum(log_fg, axis=-1)], axis=-1)
            fg_mat = cums[..., :, None] - cums[..., None, :]
            mask = jnp.tril(jnp.ones((S + 1, S + 1), bool))
            fg_mat = jnp.where(mask, fg_mat, -jnp.inf)[..., 1:, 1:]
            log_D = fg_mat + ig[..., None, :]
            max_log_D = jnp.max(log_D, axis=-1, keepdims=True)
            D = jnp.exp(log_D - max_log_D)
            qk = jnp.einsum('bnsd,bntd->bnst', qh, kh) / jnp.sqrt(jnp.float32(DH))
            C = qk * D
            normalizer = jnp.maximum(jnp.abs(C.sum(-1, keepdims=True)), jnp.exp(-max_log_D))
            h = jnp.einsum('bnst,bntd->bnsd', C / (normalizer + EPS_BACKEND), vh)
            h = h.transpose(0, 2, 1, 3)
            mean = h.mean(-1, keepdims=True)
            var = h.var(-1, keepdims=True)
            hn = (h - mean) * jax.lax.rsqrt(var + NORM_EPS) * outnorm_weight
            return hn.reshape(B, S, E)
        key = jax.random.key(seed)
        ks = jax.random.split(key, 8)
        B, S, E, NH = (2, 256, 128, NUM_HEADS)
        DH = E // NH
        q = jax.random.normal(ks[0], (B, S, E), jnp.float32)
        k = jax.random.normal(ks[1], (B, S, E), jnp.float32)
        v = jax.random.normal(ks[2], (B, S, E), jnp.float32)
        ig_kernel = jax.random.normal(ks[3], (3 * E, NH), jnp.float32) * 0.02
        fg_kernel = jax.random.normal(ks[4], (3 * E, NH), jnp.float32) * 0.02
        ig_bias = jax.random.normal(ks[5], (NH,), jnp.float32) * 0.1
        fg_bias = jnp.linspace(3.0, 6.0, NH, dtype=jnp.float32)
        outnorm_weight = jnp.ones((NH, DH), jnp.float32)
        return {'q': q, 'k': k, 'v': v, 'ig_kernel': ig_kernel, 'ig_bias': ig_bias, 'fg_kernel': fg_kernel, 'fg_bias': fg_bias, 'outnorm_weight': outnorm_weight}
    _L0_xattn_all = _L0_xattn_setup()
    _L0_xattn_in = {k: v for k, v in _L0_xattn_all.items() if k in ('ig_kernel', 'ig_bias', 'fg_kernel', 'fg_bias', 'outnorm_weight')}
    del _L0_xattn_all

    def _L0_ffn_setup():
        import jax, jax.numpy as jnp
        import numpy as np
        from jax.scipy.linalg import expm
        B, S, D, E, K, NROT = (2, 256, 128, 8, 2, 3)
        EPS = 1e-05

        def _gelu(x):
            return jax.nn.gelu(x, approximate=False)

        def _forward(x, ln_gamma, ln_beta, abel_w, abel_b, moe_gate_w, moe_gate_b, ew1, eb1, ew2, eb2, gens, gc_w, gc_b):
            residual = x
            mu = jnp.mean(x, axis=-1, keepdims=True)
            var = jnp.mean((x - mu) ** 2, axis=-1, keepdims=True)
            xn = (x - mu) * jax.lax.rsqrt(var + EPS) * ln_gamma + ln_beta
            abel_out = _gelu(xn @ abel_w + abel_b)
            logits = xn @ moe_gate_w + moe_gate_b
            topw, topi = jax.lax.top_k(logits, K)
            topw = jax.nn.softmax(topw, axis=-1)
            w_dense = jnp.sum(jax.nn.one_hot(topi, E, dtype=xn.dtype) * topw[..., None], axis=-2)
            h = _gelu(jnp.einsum('bsd,edh->ebsh', xn, ew1) + eb1[:, None, None, :])
            eo = jnp.einsum('ebsh,ehd->ebsd', h, ew2) + eb2[:, None, None, :]
            moe_out = jnp.einsum('ebsd,bse->bsd', eo, w_dense)
            for i in range(NROT):
                moe_out = moe_out @ expm(gens[i])
            combined = jnp.concatenate([abel_out, moe_out], axis=-1)
            gate = jax.nn.sigmoid(combined @ gc_w + gc_b)
            mixed = abel_out * (1.0 - gate) + moe_out * gate
            return residual + mixed
        key = jax.random.key(seed)
        ks = jax.random.split(key, 16)
        sc = 0.02
        x = jax.random.normal(ks[0], (B, S, D), jnp.float32)
        ln_gamma = 1.0 + sc * jax.random.normal(ks[1], (D,), jnp.float32)
        ln_beta = sc * jax.random.normal(ks[2], (D,), jnp.float32)
        abel_w = sc * jax.random.normal(ks[3], (D, D), jnp.float32)
        abel_b = sc * jax.random.normal(ks[4], (D,), jnp.float32)
        moe_gate_w = sc * jax.random.normal(ks[5], (D, E), jnp.float32)
        moe_gate_b = sc * jax.random.normal(ks[6], (E,), jnp.float32)
        ew1 = sc * jax.random.normal(ks[7], (E, D, 2 * D), jnp.float32)
        eb1 = sc * jax.random.normal(ks[8], (E, 2 * D), jnp.float32)
        ew2 = sc * jax.random.normal(ks[9], (E, 2 * D, D), jnp.float32)
        eb2 = sc * jax.random.normal(ks[10], (E, D), jnp.float32)
        g = sc * jax.random.normal(ks[11], (NROT, D, D), jnp.float32)
        gens = 0.5 * (g - jnp.swapaxes(g, -1, -2))
        gc_w = sc * jax.random.normal(ks[12], (2 * D, 1), jnp.float32)
        gc_b = sc * jax.random.normal(ks[13], (1,), jnp.float32)
        return dict(x=x, ln_gamma=ln_gamma, ln_beta=ln_beta, abel_w=abel_w, abel_b=abel_b, moe_gate_w=moe_gate_w, moe_gate_b=moe_gate_b, ew1=ew1, eb1=eb1, ew2=ew2, eb2=eb2, gens=gens, gc_w=gc_w, gc_b=gc_b)
    _L0_ffn_all = _L0_ffn_setup()
    _L0_ffn_in = {k: v for k, v in _L0_ffn_all.items() if k in ('ln_gamma', 'ln_beta', 'abel_w', 'abel_b', 'moe_gate_w', 'moe_gate_b', 'ew1', 'eb1', 'ew2', 'eb2', 'gens', 'gc_w', 'gc_b')}
    del _L0_ffn_all
    return {'x': x, 'ctx_1024': ctx_1024, 'L0_xattn_ig_kernel': _L0_xattn_in['ig_kernel'], 'L0_xattn_ig_bias': _L0_xattn_in['ig_bias'], 'L0_xattn_fg_kernel': _L0_xattn_in['fg_kernel'], 'L0_xattn_fg_bias': _L0_xattn_in['fg_bias'], 'L0_xattn_outnorm_weight': _L0_xattn_in['outnorm_weight'], 'L0_ffn_ln_gamma': _L0_ffn_in['ln_gamma'], 'L0_ffn_ln_beta': _L0_ffn_in['ln_beta'], 'L0_ffn_abel_w': _L0_ffn_in['abel_w'], 'L0_ffn_abel_b': _L0_ffn_in['abel_b'], 'L0_ffn_moe_gate_w': _L0_ffn_in['moe_gate_w'], 'L0_ffn_moe_gate_b': _L0_ffn_in['moe_gate_b'], 'L0_ffn_ew1': _L0_ffn_in['ew1'], 'L0_ffn_eb1': _L0_ffn_in['eb1'], 'L0_ffn_ew2': _L0_ffn_in['ew2'], 'L0_ffn_eb2': _L0_ffn_in['eb2'], 'L0_ffn_gens': _L0_ffn_in['gens'], 'L0_ffn_gc_w': _L0_ffn_in['gc_w'], 'L0_ffn_gc_b': _L0_ffn_in['gc_b']}

def reference(x, ctx_1024, L0_xattn_ig_kernel, L0_xattn_ig_bias, L0_xattn_fg_kernel, L0_xattn_fg_bias, L0_xattn_outnorm_weight, L0_ffn_ln_gamma, L0_ffn_ln_beta, L0_ffn_abel_w, L0_ffn_abel_b, L0_ffn_moe_gate_w, L0_ffn_moe_gate_b, L0_ffn_ew1, L0_ffn_eb1, L0_ffn_ew2, L0_ffn_eb2, L0_ffn_gens, L0_ffn_gc_w, L0_ffn_gc_b):
    import jax
    import jax.numpy as jnp

    def _L0_xattn_ref(q, k, v, ig_kernel, ig_bias, fg_kernel, fg_bias, outnorm_weight):
        import jax, jax.numpy as jnp
        import numpy as np
        EPS_BACKEND = 1e-06
        NORM_EPS = 1e-06
        NUM_HEADS = 4

        def _mlstm_forward(q, k, v, ig_kernel, ig_bias, fg_kernel, fg_bias, outnorm_weight):
            B, S, E = q.shape
            NH = ig_bias.shape[0]
            DH = E // NH
            gate_input = jnp.concatenate([q, k, v], axis=-1)
            igate = gate_input @ ig_kernel + ig_bias
            fgate = gate_input @ fg_kernel + fg_bias
            qh = q.reshape(B, S, NH, DH).transpose(0, 2, 1, 3)
            kh = k.reshape(B, S, NH, DH).transpose(0, 2, 1, 3)
            vh = v.reshape(B, S, NH, DH).transpose(0, 2, 1, 3)
            ig = igate.transpose(0, 2, 1)
            fg = fgate.transpose(0, 2, 1)
            log_fg = jax.nn.log_sigmoid(fg)
            cums = jnp.concatenate([jnp.zeros((B, NH, 1), log_fg.dtype), jnp.cumsum(log_fg, axis=-1)], axis=-1)
            fg_mat = cums[..., :, None] - cums[..., None, :]
            mask = jnp.tril(jnp.ones((S + 1, S + 1), bool))
            fg_mat = jnp.where(mask, fg_mat, -jnp.inf)[..., 1:, 1:]
            log_D = fg_mat + ig[..., None, :]
            max_log_D = jnp.max(log_D, axis=-1, keepdims=True)
            D = jnp.exp(log_D - max_log_D)
            qk = jnp.einsum('bnsd,bntd->bnst', qh, kh) / jnp.sqrt(jnp.float32(DH))
            C = qk * D
            normalizer = jnp.maximum(jnp.abs(C.sum(-1, keepdims=True)), jnp.exp(-max_log_D))
            h = jnp.einsum('bnst,bntd->bnsd', C / (normalizer + EPS_BACKEND), vh)
            h = h.transpose(0, 2, 1, 3)
            mean = h.mean(-1, keepdims=True)
            var = h.var(-1, keepdims=True)
            hn = (h - mean) * jax.lax.rsqrt(var + NORM_EPS) * outnorm_weight
            return hn.reshape(B, S, E)
        return _mlstm_forward(q, k, v, ig_kernel, ig_bias, fg_kernel, fg_bias, outnorm_weight)

    def _L0_ffn_ref(x, ln_gamma, ln_beta, abel_w, abel_b, moe_gate_w, moe_gate_b, ew1, eb1, ew2, eb2, gens, gc_w, gc_b):
        import jax, jax.numpy as jnp
        import numpy as np
        from jax.scipy.linalg import expm
        B, S, D, E, K, NROT = (2, 256, 128, 8, 2, 3)
        EPS = 1e-05

        def _gelu(x):
            return jax.nn.gelu(x, approximate=False)

        def _forward(x, ln_gamma, ln_beta, abel_w, abel_b, moe_gate_w, moe_gate_b, ew1, eb1, ew2, eb2, gens, gc_w, gc_b):
            residual = x
            mu = jnp.mean(x, axis=-1, keepdims=True)
            var = jnp.mean((x - mu) ** 2, axis=-1, keepdims=True)
            xn = (x - mu) * jax.lax.rsqrt(var + EPS) * ln_gamma + ln_beta
            abel_out = _gelu(xn @ abel_w + abel_b)
            logits = xn @ moe_gate_w + moe_gate_b
            topw, topi = jax.lax.top_k(logits, K)
            topw = jax.nn.softmax(topw, axis=-1)
            w_dense = jnp.sum(jax.nn.one_hot(topi, E, dtype=xn.dtype) * topw[..., None], axis=-2)
            h = _gelu(jnp.einsum('bsd,edh->ebsh', xn, ew1) + eb1[:, None, None, :])
            eo = jnp.einsum('ebsh,ehd->ebsd', h, ew2) + eb2[:, None, None, :]
            moe_out = jnp.einsum('ebsd,bse->bsd', eo, w_dense)
            for i in range(NROT):
                moe_out = moe_out @ expm(gens[i])
            combined = jnp.concatenate([abel_out, moe_out], axis=-1)
            gate = jax.nn.sigmoid(combined @ gc_w + gc_b)
            mixed = abel_out * (1.0 - gate) + moe_out * gate
            return residual + mixed
        return _forward(x, ln_gamma, ln_beta, abel_w, abel_b, moe_gate_w, moe_gate_b, ew1, eb1, ew2, eb2, gens, gc_w, gc_b)
    x = x + _L0_xattn_ref(_layernorm(x, axis=-1), ctx_1024, ctx_1024, L0_xattn_ig_kernel, L0_xattn_ig_bias, L0_xattn_fg_kernel, L0_xattn_fg_bias, L0_xattn_outnorm_weight)
    x = x + _L0_ffn_ref(_layernorm(x, axis=-1), L0_ffn_ln_gamma, L0_ffn_ln_beta, L0_ffn_abel_w, L0_ffn_abel_b, L0_ffn_moe_gate_w, L0_ffn_moe_gate_b, L0_ffn_ew1, L0_ffn_eb1, L0_ffn_ew2, L0_ffn_eb2, L0_ffn_gens, L0_ffn_gc_w, L0_ffn_gc_b)
    return x

_drawn_inputs = setup_inputs


def setup_inputs(seed=0):
    import zlib

    import numpy as np

    out = dict(_drawn_inputs(seed))
    spreads = {'L0_xattn_outnorm_weight': (1.0, 0.2)}
    factors = {'L0_xattn_ig_bias': 64.0,
     'L0_xattn_fg_kernel': 4.374,
     'L0_ffn_ln_gamma': 8.0,
     'L0_ffn_ln_beta': 8.0,
     'L0_ffn_abel_b': 30.766,
     'L0_ffn_moe_gate_w': 8.0,
     'L0_ffn_moe_gate_b': 8.0,
     'L0_ffn_ew1': 8.0,
     'L0_ffn_eb1': 8.0,
     'L0_ffn_ew2': 8.0,
     'L0_ffn_eb2': 51.279,
     'L0_ffn_gens': 8.0,
     'L0_ffn_gc_w': 8.0}
    for name, (base, spread) in spreads.items():
        noise = np.random.default_rng([zlib.crc32(name.encode()), seed]).standard_normal(out[name].shape)
        drawn = base * np.exp(spread * noise) if base else spread * noise
        out[name] = jnp.asarray(drawn.astype(out[name].dtype))
    for name, factor in factors.items():
        out[name] = (out[name] * factor).astype(out[name].dtype)
    return out
```

```python
from contextlib import ExitStack

import concourse.bass as bass
from concourse import mybir

F32 = mybir.dt.float32
F32R = mybir.dt.float32r
BF16 = mybir.dt.bfloat16
ALU = mybir.AluOpType
ACT = mybir.ActivationFunctionType
AX_X = mybir.AxisListType.X

P = 128
S = 64
D = 128
NH = 4
DH = D // NH
SEQ = 8
C = 4
T = C * P
E = 8
HID = 256
HF = HID // P
V1 = DH + 1
EPS_NORM = 1e-5
EPS_HEAD = 1e-6
EPS_DEN = 1e-6
QK_SCALE = DH ** -0.5
NEG = -1e30
HALVINGS = 7
DEGREE = 8
NROT = 3

VECTOR_A, VECTOR_B = 37, 1
POOL_A, POOL_B = 6, 1
POOL_STEPS = 14


class Links:

    def __init__(self, eng, sem, per_tile, tile):
        self.eng, self.sem, self.per_tile, self.base, self.n = eng, sem, per_tile, tile * per_tile, 0

    def __call__(self, ins):
        self.n += 1
        ins.then_inc(self.sem, 1)
        self.eng.wait_ge(self.sem, self.base + self.n)

    def end(self):
        assert self.n == self.per_tile, (self.n, self.per_tile)


def after(eng, sem, value):
    if not isinstance(value, int) or value > 0:
        eng.wait_ge(sem, value)


def build(nc, x, ctx_in, ig_w, ig_b, fg_w, fg_b, onorm_w, ln_g, ln_b, abel_w, abel_b, mg_w, mg_b,
          ew1, eb1, ew2, eb2, gens, gc_w, gc_b, out):
    TILES = x.shape[0] // SEQ
    assert TILES % 2 == 0 and TILES >= 6
    xf = x.rearrange("b s d -> (b s) d")
    outf = out.rearrange("b s d -> (b s) d")

    with ExitStack() as stack:
        def sb(name, shape, dt=F32):
            return stack.enter_context(nc.sbuf_tensor(name, shape, dt))

        def sem(name):
            return stack.enter_context(nc.semaphore(name))

        pa = stack.enter_context(nc.psum_tensor("pa", [P, 4, 512], F32))
        pb = stack.enter_context(nc.psum_tensor("pb", [P, 4, 512], F32))

        ident = sb("ident", [P, P])
        ident_b = sb("ident_b", [P, P], BF16)
        eye3 = sb("eye3", [P, NROT, P])
        causal = sb("causal", [P, NH, S], BF16)
        ones_row = sb("ones_row", [32, S])
        mhalf = sb("mhalf", [P, 16])
        rev = sb("rev", [P, E])
        w1f = sb("w1f", [P, E, HID])
        w1h = sb("w1h", [P, E, HID], F32R)
        w1l = sb("w1l", [P, E, HID], F32R)
        w2s = sb("w2s", [P, E * HF, D])
        w2t = sb("w2t", [P, E * HF, P])
        w2r = sb("w2r", [P, E * HF, D])
        b1 = sb("b1", [P, E, HF])
        b1row = sb("b1row", [E * HF, P])
        b2s = sb("b2s", [E, D])
        b2t = sb("b2t", [P, C, E])
        b2m = sb("b2m", [32, C])
        b2b = sb("b2b", [32, C, D])
        wab = sb("wab", [P, D])
        bab = sb("bab", [P, D])
        wmg = sb("wmg", [P, E])
        bmg = sb("bmg", [P, E])
        wgr = sb("wgr", [P, 3, 2, NH])
        wgq = sb("wgq", [P, 2 * NH])
        wgc = sb("wgc", [P, 2 * NH])
        bg = sb("bg", [2 * NH, 1])
        lng = sb("lng", [P, 1])
        lnb = sb("lnb", [P, 1])
        onw = sb("onw", [P, D])
        gc1 = sb("gc1", [P, D])
        gc2 = sb("gc2", [P, D])
        gcb = sb("gcb", [P, 1])
        hgcb = sb("hgcb", [P, 1])
        ga = sb("ga", [P, NROT, P])
        gat = sb("gat", [P, NROT, P])
        tm = sb("tm", [P, 2, NROT, P])
        um = sb("um", [P, 2, NROT, P])
        rot = sb("rot", [P, 2, D])

        xs = sb("xs", [P, 2, C, D])
        cs = sb("cs", [P, 2, C, D])
        st = sb("st", [P, C, 6])
        ssum = sb("ssum", [P, C])
        sdif = sb("sdif", [P, C])
        ssq = sb("ssq", [P, C])
        mean = sb("mean", [P, C])
        vr = sb("vr", [P, C])
        var = sb("var", [P, C])
        rstd = sb("rstd", [P, C])
        carrier = sb("carrier", [1, 1])
        xq = sb("xq", [P, C, D])
        xqT = sb("xqT", [P, T])
        cT = sb("cT", [P, T])
        xbd = sb("xbd", [P, SEQ, NH, S])
        vbd = sb("vbd", [P, C, NH, 2, V1])
        gT = sb("gT", [2 * NH, T])
        gr = sb("gr", [32, 2, S])
        fabs = sb("fabs", [32, S])
        fexp = sb("fexp", [32, S])
        fln = sb("fln", [32, S])
        lf = sb("lf", [32, S])
        cum = sb("cum", [32, S])
        av = sb("av", [32, S])
        mx = sb("mx", [32, S])
        mld = sb("mld", [32, S])
        ah = sb("ah", [32, S], F32R)
        al = sb("al", [32, S], F32R)
        mh = sb("mh", [32, S], F32R)
        ml = sb("ml", [32, S], F32R)
        elc = sb("elc", [12, C, 2, S])
        erc = sb("erc", [12, NH, C, S])
        el = sb("el", [12, C, 2, S], F32R)
        er = sb("er", [12, NH, C, S], F32R)
        dm = sb("dm", [P, C, NH * S])
        ct = sb("ct", [P, C, NH * S])
        enm = sb("enm", [P, 2, 2 * NH])
        den = sb("den", [P, 2, 2 * NH])
        hm = sb("hm", [P, C * NH, DH])
        hsum = sb("hsum", [P, C * NH])
        hmean = sb("hmean", [P, C * NH])
        hc = sb("hc", [P, C * NH, DH])
        hsq = sb("hsq", [P, C * NH, DH])
        hvar = sb("hvar", [P, C * NH])
        hrs = sb("hrs", [P, C * NH])
        ha = sb("ha", [P, C * NH, DH])
        hw = sb("hw", [P, C, D])
        x1 = sb("x1", [P, C, D])
        v2 = sb("v2", [P, C])
        v2e = sb("v2e", [P, C])
        r1 = sb("r1", [P, C])
        r2 = sb("r2", [P, C])
        rr = sb("rr", [P, C])
        p1 = sb("p1", [P, C])
        nm = sb("nm", [P, C])
        yh = sb("yh", [P, C, D])
        base = sb("base", [P, 2, C, D])
        xn = sb("xn", [P, 2, T])
        xnh = sb("xnh", [P, 2, T], F32R)
        xnl = sb("xnl", [P, 2, T], F32R)
        lg = sb("lg", [P, C, E])
        lg2 = sb("lg2", [P, C, E])
        k1 = sb("k1", [P, C, E])
        k2 = sb("k2", [P, C, E])
        o1 = sb("o1", [P, C, E])
        o2 = sb("o2", [P, C, E])
        m1 = sb("m1", [P, C])
        m2 = sb("m2", [P, C])
        kk = sb("kk", [P, C])
        dl = sb("dl", [P, C])
        th = sb("th", [P, C])
        wa = sb("wa", [P, C])
        wb = sb("wb", [P, C])
        wr = sb("wr", [P, 2, C, E])

        hT = sb("hT", [P, 2, HF, T])
        wT = sb("wT", [32, P])
        acc = sb("acc", [P, C, D])
        abp = sb("abp", [P, C, D])
        ab = sb("ab", [P, C, D])
        z1 = sb("z1", [P, C, D])
        z2 = sb("z2", [P, C, D])
        zz = sb("zz", [P, C, D])
        zs = sb("zs", [P, C])
        zt = sb("zt", [P, C])
        gate = sb("gate", [P, C])
        diff = sb("diff", [P, C, D])
        bab2 = sb("bab2", [P, C, D])
        res = sb("res", [P, 2, C, D])

        s_early = sem("s_early")
        s_w1 = sem("s_w1")
        s_w2 = sem("s_w2")
        s_gens = sem("s_gens")
        s_pool = sem("s_pool")
        s_setup_v = sem("s_setup_v")
        s_ready_v = sem("s_ready_v")
        s_gat_ps = sem("s_gat_ps")
        s_exp_ps = sem("s_exp_ps")
        s_exp_t = sem("s_exp_t")
        s_exp_u = sem("s_exp_u")
        s_rot_ps = sem("s_rot_ps")
        s_rot = sem("s_rot")
        s_w2_ps = sem("s_w2_ps")
        s_w2_sb = sem("s_w2_sb")
        s_b1_ps = sem("s_b1_ps")
        s_b1 = sem("s_b1")
        s_x = [sem("s_x0"), sem("s_x1")]
        s_c = [sem("s_c0"), sem("s_c1")]
        s_va = sem("s_va")
        s_vb = sem("s_vb")
        s_ga = sem("s_ga")
        s_gb = sem("s_gb")
        s_xvar = sem("s_xvar")
        s_xrstd = sem("s_xrstd")
        s_xq = sem("s_xq")
        s_xqT_ps = sem("s_xqT_ps")
        s_xqT = sem("s_xqT")
        s_cT_ps = sem("s_cT_ps")
        s_cT = sem("s_cT")
        s_xbd = sem("s_xbd")
        s_vbd = sem("s_vbd")
        s_g_ps = sem("s_g_ps")
        s_gT = sem("s_gT")
        s_gr = sem("s_gr")
        s_fabs = sem("s_fabs")
        s_fexp = sem("s_fexp")
        s_fln = sem("s_fln")
        s_mld = sem("s_mld")
        s_ah = sem("s_ah")
        s_erow = sem("s_erow")
        s_qk = sem("s_qk")
        s_e = sem("s_e")
        s_d = sem("s_d")
        s_ct = sem("s_ct")
        s_pv = sem("s_pv")
        s_enm_ps = sem("s_enm_ps")
        s_enm = sem("s_enm")
        s_hm = sem("s_hm")
        s_hmean = sem("s_hmean")
        s_hsq = sem("s_hsq")
        s_hvar = sem("s_hvar")
        s_hrs = sem("s_hrs")
        s_ha = sem("s_ha")
        s_x1 = sem("s_x1_")
        s_v2 = sem("s_v2")
        s_r1 = sem("s_r1")
        s_v2e = sem("s_v2e")
        s_r2 = sem("s_r2")
        s_yh = sem("s_yh")
        s_base = sem("s_base")
        s_nm = sem("s_nm")
        s_yT_ps = sem("s_yT_ps")
        s_xn = sem("s_xn")
        s_xns = sem("s_xns")
        s_lg_ps = sem("s_lg_ps")
        s_dl = sem("s_dl")
        s_th = sem("s_th")
        s_w = sem("s_w")
        s_h_ps = sem("s_h_ps")
        s_h = sem("s_h")
        s_y_ps = sem("s_y_ps")
        s_y = sem("s_y")
        s_ab = sem("s_ab")
        s_wT_ps = sem("s_wT_ps")
        s_wT = sem("s_wT")
        s_zz = sem("s_zz")
        s_zs = sem("s_zs")
        s_zt = sem("s_zt")
        s_db = sem("s_db")
        s_res = sem("s_res")
        s_out = [sem("s_out0"), sem("s_out1")]

        EXP_STEPS = DEGREE - 1 + HALVINGS
        N_EARLY = 16 * 16

        block = stack.enter_context(nc.Block())

        @block.sync
        def _(sp):
            def load(u, par, first=False):
                row, first_seq = sp.snap(u * T), sp.snap(u * SEQ)
                if not first:
                    sp.wait_ge(s_x1, u - 1)
                    sp.wait_ge(s_cT_ps, u - 1)
                    sp.wait_ge(s_vbd, u - 1)
                sp.dma_start(xs[:, par], xf[bass.ds(row, T), :].rearrange("(c p) d -> p c d", p=P)
                             ).then_inc(s_x[par], 16)
                src = ctx_in[bass.ds(first_seq, SEQ), :, :].rearrange("(q b g) t d -> b q t g d", q=2, b=2)
                for b in range(2):
                    for q in range(2):
                        sp.dma_start(cs[S * b:S * b + S, par, 2 * q:2 * q + 2], src[b, q]).then_inc(s_c[par], 16)

            def gate_rows(u):
                sp.wait_ge(s_gT, u + 1)
                for j in range(2):
                    for b in range(2):
                        sp.dma_start(gr[16 * b:16 * b + 16, j, :],
                                     gT[NH * j:NH * j + NH, 256 * b:256 * b + 256].rearrange(
                                         "h (n t) -> h n t", n=4)).then_inc(s_gr, 16)

            def decay_rows(u):
                sp.wait_ge(s_ah, u + 1)
                for n, (gates, maxima) in enumerate(((ah, mh), (al, ml))):
                    for b in range(2):
                        rows = slice(16 * b, 16 * b + 16)
                        sp.dma_start(el[NH * n:NH * n + NH, :, b].bitcast(F32), gates[rows, :].bitcast(F32)
                                     ).then_inc(s_erow, 16)
                        row = 2 * NH + 2 * n + b
                        sp.dma_start(er[row:row + 1].bitcast(F32), maxima[rows, :].bitcast(F32)
                                     ).then_inc(s_erow, 16)

            def store(t, par):
                row = sp.snap(t * T)
                sp.wait_ge(s_res, t + 1)
                sp.dma_start(outf[bass.ds(row, T), :].rearrange("(c p) d -> p c d", p=P), res[:, par]
                             ).then_inc(s_out[par], 16)

            def bcast(row, n):
                return row.rearrange("(a n) -> a n", a=1).broadcast_to([P, n])

            load(0, 0, True)
            for j, w in enumerate((ig_w, fg_w)):
                sp.dma_start(wgr[:, :, j, :], w.rearrange("(r d) h -> d r h", r=3)).then_inc(s_early, 16)
            sp.dma_start(bg[0:NH, :], ig_b.rearrange("(h a) -> h a", a=1)).then_inc(s_early, 16)
            sp.dma_start(bg[NH:2 * NH, :], fg_b.rearrange("(h a) -> h a", a=1)).then_inc(s_early, 16)
            sp.dma_start(ga[:, :, :], gens.rearrange("r i j -> i r j")).then_inc(s_gens, 16)
            sp.dma_start(onw[:, :], bcast(onorm_w.rearrange("h d -> (h d)"), D)).then_inc(s_early, 16)
            sp.dma_start(lng[:, :], ln_g.rearrange("(d a) -> d a", a=1)).then_inc(s_early, 16)
            sp.dma_start(lnb[:, :], ln_b.rearrange("(d a) -> d a", a=1)).then_inc(s_early, 16)
            sp.dma_start(wmg[:, :], mg_w).then_inc(s_early, 16)
            sp.dma_start(bmg[:, :], bcast(mg_b, E)).then_inc(s_early, 16)
            sp.dma_start(wab[:, :], abel_w).then_inc(s_early, 16)
            sp.dma_start(bab[:, :], bcast(abel_b, D)).then_inc(s_early, 16)
            sp.dma_start(b1row[:, :], eb1.rearrange("e (f p) -> (e f) p", f=HF)).then_inc(s_early, 16)
            sp.dma_start(b2s[:, :], eb2).then_inc(s_early, 16)
            gcv = gc_w.rearrange("d a -> (d a)")
            sp.dma_start(gc1[:, :], bcast(gcv[0:D], D)).then_inc(s_early, 16)
            sp.dma_start(gc2[:, :], bcast(gcv[D:2 * D], D)).then_inc(s_early, 16)
            sp.dma_start(gcb[:, :], bcast(gc_b, 1)).then_inc(s_early, 16)
            sp.dma_start(w2s[:, :, :], ew2.rearrange("e (f p) d -> p (e f) d", f=HF)).then_inc(s_w2, 16)
            sp.dma_start(w1f[:, :, :], ew1.rearrange("e d h -> d e h")).then_inc(s_w1, 16)
            load(1, 1, True)
            gate_rows(0)
            decay_rows(0)

            def body(t, par):
                load(t + 2, par)
                gate_rows(t + 1)
                decay_rows(t + 1)
                store(t, par)

            body(0, 0)
            body(1, 1)
            with sp.Fori(1, TILES // 2 - 1) as i:
                body(2 * i, 0)
                body(2 * i + 1, 1)
            gate_rows(TILES - 1)
            decay_rows(TILES - 1)
            store(TILES - 2, 0)
            store(TILES - 1, 1)
            for par in range(2):
                sp.wait_ge(s_out[par], 16 * (TILES // 2))

        @block.gpsimd
        def _(pool):
            g = nc.gpsimd
            steps = 0

            def step(ins):
                nonlocal steps
                steps += 1
                ins.then_inc(s_pool, 1)
                pool.wait_ge(s_pool, steps)

            step(g.memset(ident[:, :], 0.0))
            step(g.affine_select(out=ident[:, :], in_=ident[:, :], compare_op=ALU.not_equal, fill=1.0,
                                 base=0, pattern=[[-1, P]], channel_multiplier=1))
            for n in range(NROT):
                g.tensor_copy(eye3[:, n, :], ident[:, :])
            g.tensor_copy(ident_b[:, :], ident[:, :])
            g.memset(mhalf[:, :], -0.5)
            g.memset(ones_row[:, :], 1.0)
            for e in range(E):
                g.memset(rev[:, e:e + 1], float(E - e))
            step(g.memset(causal[:, :, :], 0.0))
            for b in range(2):
                half = causal[S * b:S * b + S, :, :]
                step(g.affine_select(out=half, in_=half, compare_op=ALU.is_ge, fill=NEG, base=0,
                                     pattern=[[0, NH], [1, S]], channel_multiplier=-1))
            g.memset(elc[:, :, :, :], 0.0)
            g.memset(erc[:, :, :, :], 0.0)
            g.memset(b2m[:, :], 1.0)
            g.memset(xbd[:, :, :, :], 0.0)
            step(g.memset(vbd[:, :, :, :, :], 0.0))
            for n in range(2):
                step(g.affine_select(out=erc[:, :, :, :], in_=erc[:, :, :, :], compare_op=ALU.not_equal,
                                     fill=1.0, base=-NH * n, pattern=[[-1, NH], [0, C], [0, S]],
                                     channel_multiplier=1))
                step(g.affine_select(out=elc[:, :, :, :], in_=elc[:, :, :, :], compare_op=ALU.not_equal,
                                     fill=1.0, base=-2 * NH - 2 * n, pattern=[[0, C], [-1, 2], [0, S]],
                                     channel_multiplier=1))
            step(g.affine_select(out=b2m[:, :], in_=b2m[:, :], compare_op=ALU.is_ge, fill=0.0,
                                 base=0, pattern=[[-E, C]], channel_multiplier=1))
            step(g.affine_select(out=b2m[:, :], in_=b2m[:, :], compare_op=ALU.is_ge, fill=0.0,
                                 base=E - 1, pattern=[[E, C]], channel_multiplier=-1))
            for b in range(2):
                step(g.memset(vbd[S * b:S * b + S, :, :, b, DH:V1], 1.0))

            def carry():
                g.tensor_tensor(carrier[:, :], mhalf[0:1, 0:1], mhalf[0:1, 0:1], ALU.mult)

            def stage_a1(u, par, link):
                pool.wait_ge(s_xvar, u + 1)
                g.tensor_tensor(rstd[:, :], var[:, :], mhalf[:, 0:C], ALU.pow).then_inc(s_xrstd, 1)
                pool.wait_ge(s_xrstd, u + 1)
                pool.wait_ge(s_c[par], 32 * (u - par) + 64)
                after(pool, s_pv, u)
                halves = [(vbd[S * b:S * b + S, :, :, b, 0:DH],
                           cs[S * b:S * b + S, par].rearrange("t k (h d) -> t k h d", h=NH)) for b in range(2)]
                carry()
                link(g.tensor_copy(*halves[0]))
                carry()
                g.tensor_copy(*halves[1]).then_inc(s_vbd, 1)
                pool.wait_ge(s_vbd, u + 1)
                pool.wait_ge(s_xqT, u + 1)
                after(pool, s_qk, 2 * u)
                for h in range(NH):
                    carry()
                    rows = slice(DH * h, DH * h + DH)
                    ins = g.tensor_copy(xbd[rows, :, h, :], xqT[rows, :].rearrange("d (b s) -> d b s", b=SEQ))
                    if h < NH - 1:
                        link(ins)
                ins.then_inc(s_xbd, 1)
                pool.wait_ge(s_xbd, u + 1)

            def stage_a2(u, par, link):
                pool.wait_ge(s_hmean, u + 1)
                link(g.tensor_tensor(hc[:, :, :], hm[:, :, :],
                                     hmean[:, :].unsqueeze(2).broadcast_to([P, C * NH, DH]), ALU.add))
                g.tensor_tensor(hsq[:, :, :], hc[:, :, :], hc[:, :, :], ALU.mult).then_inc(s_hsq, 1)
                pool.wait_ge(s_hvar, u + 1)
                g.tensor_tensor(hrs[:, :], hvar[:, :], mhalf[:, :], ALU.pow).then_inc(s_hrs, 1)
                pool.wait_ge(s_ha, u + 1)
                link(g.tensor_tensor(hw[:, :, :], ha[:, :, :].rearrange("p (c h) d -> p c (h d)", c=C),
                                     onw[:, :].unsqueeze(1).broadcast_to([P, C, D]), ALU.mult))
                g.tensor_tensor(x1[:, :, :], hw[:, :, :], xs[:, par], ALU.add).then_inc(s_x1, 1)
                pool.wait_ge(s_v2, u + 1)
                g.tensor_tensor(r1[:, :], v2[:, :], mhalf[:, 0:C], ALU.pow).then_inc(s_r1, 1)
                pool.wait_ge(s_v2e, u + 1)
                g.tensor_tensor(r2[:, :], v2e[:, :], mhalf[:, 0:C], ALU.pow).then_inc(s_r2, 1)
                pool.wait_ge(s_nm, u + 1)
                carry()
                for c in range(C):
                    ins = g.tensor_scalar(base[:, par, c, :], x1[:, c, :], p1[:, c:c + 1], nm[:, c:c + 1],
                                          ALU.mult, ALU.add)
                ins.then_inc(s_base, 1)

            def stage_b(t, par):
                link = Links(pool, s_gb, POOL_B, t)
                pool.wait_ge(s_ab, t + 1)
                g.tensor_tensor(z1[:, :, :], ab[:, :, :], gc1[:, :].unsqueeze(1).broadcast_to([P, C, D]), ALU.mult)
                pool.wait_ge(s_y, 10 * t + 10)
                link(g.tensor_tensor(z2[:, :, :], acc[:, :, :],
                                     gc2[:, :].unsqueeze(1).broadcast_to([P, C, D]), ALU.mult))
                g.tensor_tensor(zz[:, :, :], z1[:, :, :], z2[:, :, :], ALU.add).then_inc(s_zz, 1)
                g.tensor_tensor(diff[:, :, :], acc[:, :, :], ab[:, :, :], ALU.subtract)
                g.tensor_tensor(bab2[:, :, :], base[:, par], ab[:, :, :], ALU.add).then_inc(s_db, 1)
                link.end()

            def attend(u, par):
                link = Links(pool, s_ga, POOL_A, u)
                stage_a1(u, par, link)
                stage_a2(u, par, link)
                link.end()

            def body(t, par):
                attend(t + 1, 1 - par)
                stage_b(t, par)

            assert steps == POOL_STEPS
            pool.wait_ge(s_early, N_EARLY)
            attend(0, 0)
            body(0, 0)
            body(1, 1)
            with pool.Fori(1, TILES // 2 - 1) as i:
                body(2 * i, 0)
                body(2 * i + 1, 1)
            body(TILES - 2, 0)
            stage_b(TILES - 1, 1)

        @block.scalar
        def _(act):
            a = nc.scalar

            def gelu(t, e):
                for f in range(HF):
                    act.wait_ge(s_h_ps, 16 * t + 2 * e + f + 1)
                    if e >= 2:
                        act.wait_ge(s_y_ps, 10 * t + 2 + e - 1)
                    else:
                        after(act, s_y_ps, 10 * t)
                    a.activation(hT[:, e % 2, f, :], pb[:, f, :], ACT.Gelu, bias=b1[:, e, f:f + 1]).then_inc(s_h, 1)

            def gelu_abel(t):
                act.wait_ge(s_y, 10 * t + 1)
                after(act, s_res, t)
                a.activation(ab[:, :, :], abp[:, :, :], ACT.Gelu).then_inc(s_ab, 1)

            def query_t(u):
                act.wait_ge(s_xqT_ps, u + 1)
                after(act, s_xbd, u)
                after(act, s_g_ps, u)
                a.activation(xqT[:, :], pa[:, 0, :], ACT.Copy).then_inc(s_xqT, 1)

            def log_sigmoid(u):
                act.wait_ge(s_fabs, u + 1)
                a.activation(fexp[:, :], fabs[:, :], ACT.Exp, scale=-1.0).then_inc(s_fexp, 1)
                act.wait_ge(s_fexp, u + 1)
                a.activation(fln[:, :], fexp[:, :], ACT.Ln, bias=1.0).then_inc(s_fln, 1)

            def decay(u):
                act.wait_ge(s_enm_ps, u + 1)
                a.activation(enm[:, :, :].rearrange("p q n -> p (q n)"), pa[:, 2, 0:16], ACT.Exp,
                             scale=-1.0).then_inc(s_enm, 1)
                for n, q in enumerate((1, 0)):
                    act.wait_ge(s_e, 2 * u + n + 1)
                    a.activation(dm[:, 2 * q:2 * q + 2, :].rearrange("p k n -> p (k n)"), pa[:, 2 + q, :],
                                 ACT.Exp).then_inc(s_d, 1)

            def norm_t(u, par):
                act.wait_ge(s_yT_ps, u + 1)
                a.activation(xn[:, par, :], pa[:, 0, :], ACT.Identity, bias=lnb[:, 0:1],
                             scale=lng[:, 0:1]).then_inc(s_xn, 1)

            def route(u):
                act.wait_ge(s_dl, u + 1)
                a.activation(th[:, :], dl[:, :], ACT.Tanh, scale=0.5).then_inc(s_th, 1)

            def mix(t):
                act.wait_ge(s_zs, t + 1)
                a.activation(zt[:, :], zs[:, :], ACT.Tanh, bias=hgcb[:, 0:1], scale=0.5).then_inc(s_zt, 1)

            for n in range(EXP_STEPS):
                if n >= DEGREE - 1 and n < EXP_STEPS:
                    act.wait_ge(s_exp_ps, n + 1)
                    a.activation(um[:, (n + 1) % 2, :, :].rearrange("p r n -> p (r n)"), pa[:, 1, 0:NROT * P],
                                 ACT.Copy).then_inc(s_exp_u, 1)
            act.wait_ge(s_ready_v, 1)
            query_t(0)
            log_sigmoid(0)
            decay(0)
            norm_t(0, 0)
            route(0)

            def body(t, par):
                u = t + 1
                gelu(t, 0)
                gelu_abel(t)
                gelu(t, 1)
                query_t(u)
                gelu(t, 2)
                log_sigmoid(u)
                gelu(t, 3)
                gelu(t, 4)
                decay(u)
                gelu(t, 5)
                gelu(t, 6)
                gelu(t, 7)
                norm_t(u, 1 - par)
                route(u)
                mix(t)

            body(0, 0)
            body(1, 1)
            with act.Fori(1, TILES // 2 - 1) as i:
                body(2 * i, 0)
                body(2 * i + 1, 1)
            body(TILES - 2, 0)
            gelu(TILES - 1, 0)
            gelu_abel(TILES - 1)
            for e in range(1, E):
                gelu(TILES - 1, e)
            mix(TILES - 1)

        @block.vector
        def _(dve):
            v = nc.vector
            steps = 0

            def step(ins):
                nonlocal steps
                steps += 1
                ins.then_inc(s_setup_v, 1)
                dve.wait_ge(s_setup_v, steps)

            dve.wait_ge(s_gens, 16)
            dve.wait_ge(s_pool, 3)
            dve.wait_ge(s_gat_ps, 1)
            g3 = "p r n -> p (r n)"
            v.tensor_scalar(gat[:, :, :].rearrange(g3), pa[:, 0, 0:NROT * P], 2.0 ** -HALVINGS, None, ALU.mult)
            step(v.tensor_scalar(ga[:, :, :], ga[:, :, :], 2.0 ** -HALVINGS, None, ALU.mult))
            v.scalar_tensor_tensor(out=tm[:, 0], in0=ga[:, :, :], scalar=1.0 / DEGREE, in1=eye3[:, :, :],
                                   op0=ALU.mult, op1=ALU.add).then_inc(s_exp_t, 1)
            v.scalar_tensor_tensor(out=um[:, 0], in0=gat[:, :, :], scalar=1.0 / DEGREE, in1=eye3[:, :, :],
                                   op0=ALU.mult, op1=ALU.add).then_inc(s_exp_u, 1)
            for n in range(EXP_STEPS):
                dve.wait_ge(s_exp_ps, n + 1)
                tn = tm[:, (n + 1) % 2, :, :].rearrange(g3)
                un = um[:, (n + 1) % 2, :, :].rearrange(g3)
                k = DEGREE - 1 - n
                if k > 0:
                    v.scalar_tensor_tensor(out=tn, in0=pa[:, 0, 0:NROT * P], scalar=1.0 / k,
                                           in1=eye3[:, :, :].rearrange(g3), op0=ALU.mult,
                                           op1=ALU.add).then_inc(s_exp_t, 1)
                    v.scalar_tensor_tensor(out=un, in0=pa[:, 1, 0:NROT * P], scalar=1.0 / k,
                                           in1=eye3[:, :, :].rearrange(g3), op0=ALU.mult,
                                           op1=ALU.add).then_inc(s_exp_u, 1)
                else:
                    v.tensor_copy(tn, pa[:, 0, 0:NROT * P]).then_inc(s_exp_t, 1)
            for n in range(2):
                dve.wait_ge(s_rot_ps, n + 1)
                v.tensor_copy(rot[:, n, :], pa[:, 2 + n, 0:D]).then_inc(s_rot, 1)
            for n in range(4):
                dve.wait_ge(s_w2_ps, n + 1)
                v.tensor_copy(w2t[:, 4 * n:4 * n + 4, :].rearrange(g3), pb[:, n, :]).then_inc(s_w2_sb, 1)
            dve.wait_ge(s_b1_ps, 1)
            v.tensor_copy(b1[:, :, :].rearrange("p e f -> p (e f)"), pa[:, 0, 0:E * HF])
            v.tensor_copy(b2t[:, :, :], pa[:, 0, 16:16 + E].unsqueeze(1).broadcast_to([P, C, E])).then_inc(s_b1, 1)
            for n in range(4):
                dve.wait_ge(s_w2_ps, 4 + n + 1)
                v.tensor_copy(w2r[:, 4 * n:4 * n + 4, :].rearrange(g3), pb[:, n, :]).then_inc(s_w2_sb, 1)
            dve.wait_ge(s_b1_ps, 2)
            dve.wait_ge(s_pool, POOL_STEPS)
            v.tensor_tensor(b2b[:, :, :], pa[0:32, 1, 0:D].unsqueeze(1).broadcast_to([32, C, D]),
                            b2m[:, :].unsqueeze(2).broadcast_to([32, C, D]), ALU.mult)
            dve.wait_ge(s_w1, 16)
            step(v.tensor_copy(w1h[:, :, :], w1f[:, :, :]))
            v.tensor_tensor(w1l[:, :, :], w1f[:, :, :], w1h[:, :, :].bitcast(F32), ALU.subtract)
            dve.wait_ge(s_early, N_EARLY)
            v.tensor_copy(wgq[:, :].rearrange("d (j h) -> d j h", j=2), wgr[:, 0])
            v.tensor_tensor(wgc[:, :].rearrange("d (j h) -> d j h", j=2), wgr[:, 1], wgr[:, 2], ALU.add)
            v.tensor_scalar(hgcb[:, :], gcb[:, :], 0.5, None, ALU.mult)
            v.tensor_copy(el[:, :, :, :], elc[:, :, :, :])
            v.tensor_copy(er[:, :, :, :], erc[:, :, :, :]).then_inc(s_ready_v, 1)

            def statistics(src, link):
                for c in range(C):
                    ins = v.bn_stats(st[:, c, :], src[:, c, :])
                link(ins)
                v.tensor_tensor(sdif[:, :], st[:, :, 1], st[:, :, 4], ALU.subtract)
                v.tensor_tensor(ssum[:, :], st[:, :, 1], st[:, :, 4], ALU.add)
                link(v.tensor_tensor(ssq[:, :], st[:, :, 2], st[:, :, 5], ALU.add))
                v.tensor_scalar(mean[:, :], ssum[:, :], 0.5, None, ALU.mult)
                link(v.scalar_tensor_tensor(out=sdif[:, :], in0=sdif[:, :], scalar=0.25, in1=sdif[:, :],
                                            op0=ALU.mult, op1=ALU.mult))
                link(v.scalar_tensor_tensor(out=vr[:, :], in0=ssq[:, :], scalar=1.0 / D, in1=sdif[:, :],
                                            op0=ALU.mult, op1=ALU.add))

            def norm_x(u, par, link):
                dve.wait_ge(s_x[par], 8 * (u - par) + 16)
                statistics(xs[:, par], link)
                v.tensor_scalar(var[:, :], vr[:, :], EPS_NORM, None, ALU.add).then_inc(s_xvar, 1)
                dve.wait_ge(s_xrstd, u + 1)
                after(dve, s_xqT_ps, u)
                for c in range(C):
                    ins = v.tensor_scalar(xq[:, c, :], xs[:, par, c, :], mean[:, c:c + 1], rstd[:, c:c + 1],
                                          ALU.subtract, ALU.mult)
                ins.then_inc(s_xq, 1)

            def context_t(u):
                dve.wait_ge(s_cT_ps, u + 1)
                after(dve, s_qk, 2 * u)
                v.tensor_copy(cT[:, :], pa[:, 1, :]).then_inc(s_cT, 1)

            def gates_out(u):
                dve.wait_ge(s_g_ps, u + 1)
                v.tensor_scalar(gT[:, :], pa[0:2 * NH, 2, :], bg[:, 0:1], None, ALU.add).then_inc(s_gT, 1)
                dve.wait_ge(s_gr, 64 * u + 64)
                v.scalar_tensor_tensor(out=fabs[:, :], in0=gr[:, 1, :], scalar=-1.0, in1=gr[:, 1, :],
                                       op0=ALU.mult, op1=ALU.max).then_inc(s_fabs, 1)

            def decay_rows(u, link):
                dve.wait_ge(s_fln, u + 1)
                link(v.scalar_tensor_tensor(out=lf[:, :], in0=gr[:, 1, :], scalar=0.0, in1=fln[:, :],
                                            op0=ALU.min, op1=ALU.subtract))
                link(v.tensor_tensor_scan(cum[:, :], ones_row[:, :], lf[:, :], 0.0, ALU.mult, ALU.add))
                link(v.tensor_tensor(av[:, :], gr[:, 0, :], cum[:, :], ALU.subtract))
                link(v.tensor_tensor_scan(mx[:, :], av[:, :], av[:, :], -3.0e38, ALU.max, ALU.max))
                v.tensor_tensor(mld[:, :], cum[:, :], mx[:, :], ALU.add).then_inc(s_mld, 1)
                v.tensor_copy(ah[:, :], av[:, :])
                link(v.tensor_scalar(mh[:, :], mx[:, :], -1.0, None, ALU.mult))
                v.tensor_tensor(al[:, :], av[:, :], ah[:, :].bitcast(F32), ALU.subtract)
                v.scalar_tensor_tensor(out=ml[:, :], in0=mx[:, :], scalar=-1.0, in1=mh[:, :].bitcast(F32),
                                       op0=ALU.mult, op1=ALU.subtract).then_inc(s_ah, 1)

            def decayed(u):
                after(dve, s_pv, u)
                for n, q in enumerate((1, 0)):
                    dve.wait_ge(s_qk, 2 * u + n + 1)
                    dve.wait_ge(s_d, 2 * u + n + 1)
                    v.scalar_tensor_tensor(out=ct[:, 2 * q:2 * q + 2, :].rearrange("p k n -> p (k n)"),
                                           in0=pa[:, q, :], scalar=QK_SCALE,
                                           in1=dm[:, 2 * q:2 * q + 2, :].rearrange("p k n -> p (k n)"),
                                           op0=ALU.mult, op1=ALU.mult).then_inc(s_ct, 1)

            def heads(u, link):
                dve.wait_ge(s_pv, u + 1)
                dve.wait_ge(s_enm, u + 1)
                hu = pa[:, 2:4, 0:2 * NH * V1].rearrange("p q (n d) -> p q n d", d=V1)
                link(v.scalar_tensor_tensor(out=den[:, :, :], in0=hu[:, :, :, DH], scalar=-1.0, in1=enm[:, :, :],
                                            op0=ALU.mult, op1=ALU.max))
                link(v.tensor_tensor(den[:, :, :], hu[:, :, :, DH], den[:, :, :], ALU.max))
                link(v.tensor_scalar(den[:, :, :], den[:, :, :], EPS_DEN, None, ALU.add))
                link(v.reciprocal(den[:, :, :], den[:, :, :]))
                for q in range(2):
                    ins = v.tensor_tensor(
                        hm[:, 2 * NH * q:2 * NH * q + 2 * NH, :].rearrange("p (b h) d -> p h b d", b=2),
                        hu[:, q, :, 0:DH].rearrange("p (h b) d -> p h b d", b=2),
                        den[:, q, :].rearrange("p (h b) -> p h b", b=2).unsqueeze(3).broadcast_to([P, NH, 2, DH]),
                        ALU.mult)
                ins.then_inc(s_hm, 1)
                dve.wait_ge(s_hm, u + 1)
                link(v.reduce_sum(hsum[:, :], hm[:, :, :], AX_X))
                v.tensor_scalar(hmean[:, :], hsum[:, :], -1.0 / DH, None, ALU.mult).then_inc(s_hmean, 1)

            def head_norm(u, link):
                dve.wait_ge(s_hsq, u + 1)
                link(v.reduce_sum(hsum[:, :], hsq[:, :, :], AX_X))
                v.tensor_scalar(hvar[:, :], hsum[:, :], 1.0 / DH, EPS_HEAD, ALU.mult, ALU.add).then_inc(s_hvar, 1)
                dve.wait_ge(s_hrs, u + 1)
                v.tensor_tensor(ha[:, :, :], hc[:, :, :], hrs[:, :].unsqueeze(2).broadcast_to([P, C * NH, DH]),
                                ALU.mult).then_inc(s_ha, 1)

            def norm_stats(u, link):
                dve.wait_ge(s_x1, u + 1)
                statistics(x1, link)
                v.tensor_scalar(v2[:, :], vr[:, :], EPS_NORM, None, ALU.add).then_inc(s_v2, 1)
                dve.wait_ge(s_r1, u + 1)
                link(v.tensor_tensor(rr[:, :], r1[:, :], r1[:, :], ALU.mult))
                link(v.tensor_tensor(rr[:, :], rr[:, :], vr[:, :], ALU.mult))
                v.tensor_scalar(v2e[:, :], rr[:, :], EPS_NORM, None, ALU.add).then_inc(s_v2e, 1)

            def norm_apply(u, link):
                v.scalar_tensor_tensor(out=nm[:, :], in0=mean[:, :], scalar=-1.0, in1=r1[:, :],
                                       op0=ALU.mult, op1=ALU.mult)
                v.tensor_scalar(p1[:, :], r1[:, :], 1.0, None, ALU.add).then_inc(s_nm, 1)
                dve.wait_ge(s_r2, u + 1)
                link(v.tensor_tensor(rr[:, :], r1[:, :], r2[:, :], ALU.mult))
                after(dve, s_yT_ps, u)
                for c in range(C):
                    ins = v.tensor_scalar(yh[:, c, :], x1[:, c, :], mean[:, c:c + 1], rr[:, c:c + 1],
                                          ALU.subtract, ALU.mult)
                ins.then_inc(s_yh, 1)

            def norm_split(u, par, link):
                dve.wait_ge(s_xn, u + 1)
                link(v.tensor_copy(xnh[:, par, :], xn[:, par, :]))
                v.tensor_tensor(xnl[:, par, :], xn[:, par, :], xnh[:, par, :].bitcast(F32),
                                ALU.subtract).then_inc(s_xns, 1)

            def top_one(src, key, hot, top, link):
                def row(m):
                    return m[:, :].unsqueeze(2).broadcast_to([P, C, E])
                link(v.reduce_max(top[:, :], src[:, :, :], AX_X))
                link(v.tensor_tensor(key[:, :, :], src[:, :, :], row(top), ALU.is_ge))
                link(v.tensor_tensor(key[:, :, :], key[:, :, :], rev[:, :].unsqueeze(1).broadcast_to([P, C, E]),
                                     ALU.mult))
                link(v.reduce_max(kk[:, :], key[:, :, :], AX_X))
                link(v.tensor_tensor(hot[:, :, :], key[:, :, :], row(kk), ALU.is_equal))

            def routing(u, par, link):
                dve.wait_ge(s_lg_ps, u + 1)
                link(v.tensor_tensor(lg[:, :, :], pa[:, 1, 0:C * E].rearrange("p (c e) -> p c e", c=C),
                                     bmg[:, :].unsqueeze(1).broadcast_to([P, C, E]), ALU.add))
                top_one(lg, k1, o1, m1, link)
                link(v.scalar_tensor_tensor(out=lg2[:, :, :], in0=o1[:, :, :], scalar=-3.0e38, in1=lg[:, :, :],
                                            op0=ALU.mult, op1=ALU.add))
                top_one(lg2, k2, o2, m2, link)
                v.tensor_tensor(dl[:, :], m1[:, :], m2[:, :], ALU.subtract).then_inc(s_dl, 1)
                dve.wait_ge(s_th, u + 1)
                v.tensor_scalar(wa[:, :], th[:, :], 0.5, 0.5, ALU.mult, ALU.add)
                link(v.tensor_scalar(wb[:, :], th[:, :], -0.5, 0.5, ALU.mult, ALU.add))
                v.tensor_tensor(k1[:, :, :], o1[:, :, :], wa[:, :].unsqueeze(2).broadcast_to([P, C, E]), ALU.mult)
                link(v.tensor_tensor(k2[:, :, :], o2[:, :, :], wb[:, :].unsqueeze(2).broadcast_to([P, C, E]),
                                     ALU.mult))
                v.tensor_tensor(wr[:, par], k1[:, :, :], k2[:, :, :], ALU.add).then_inc(s_w, 1)

            def abel_bias(t, link):
                dve.wait_ge(s_wT_ps, t + 1)
                v.tensor_copy(wT[:, :], pa[0:32, 3, 0:P]).then_inc(s_wT, 1)
                dve.wait_ge(s_y_ps, 10 * t + 1)
                after(dve, s_ab, t)
                v.tensor_tensor(abp[:, :, :], pb[:, 2, :].rearrange("p (c d) -> p c d", c=C),
                                bab[:, :].unsqueeze(1).broadcast_to([P, C, D]), ALU.add).then_inc(s_y, 1)
                dve.wait_ge(s_y_ps, 10 * t + 2)
                after(dve, s_db, t)
                v.tensor_copy(acc[:, :, :], pb[:, 3, :].rearrange("p (c d) -> p c d", c=C)).then_inc(s_y, 1)

            def expert(t, par, e):
                dve.wait_ge(s_y, 10 * t + 2 + e)
                dve.wait_ge(s_y_ps, 10 * t + 3 + e)
                for c in range(C):
                    ins = v.scalar_tensor_tensor(out=acc[:, c, :], in0=pb[:, 2 + e % 2, D * c:D * c + D],
                                                 scalar=wr[:, par, c, e:e + 1], in1=acc[:, c, :],
                                                 op0=ALU.mult, op1=ALU.add)
                ins.then_inc(s_y, 1)

            def mix(t, par, link):
                dve.wait_ge(s_zz, t + 1)
                v.reduce_sum(zs[:, :], zz[:, :, :], AX_X).then_inc(s_zs, 1)
                dve.wait_ge(s_zt, t + 1)
                link(v.tensor_scalar(gate[:, :], zt[:, :], 0.5, 0.5, ALU.mult, ALU.add))
                dve.wait_ge(s_db, t + 1)
                after(dve, s_out[par], 8 * (t - par))
                for c in range(C):
                    ins = v.scalar_tensor_tensor(out=res[:, par, c, :], in0=diff[:, c, :], scalar=gate[:, c:c + 1],
                                                 in1=bab2[:, c, :], op0=ALU.mult, op1=ALU.add)
                ins.then_inc(s_res, 1)

            def first_attend(u, par):
                link = Links(dve, s_va, VECTOR_A, u)
                norm_x(u, par, link)
                context_t(u)
                gates_out(u)
                decay_rows(u, link)
                decayed(u)
                heads(u, link)
                head_norm(u, link)
                norm_stats(u, link)
                norm_apply(u, link)
                norm_split(u, par, link)
                routing(u, par, link)
                link.end()

            def body(t, par):
                u, up = t + 1, 1 - par
                link = Links(dve, s_va, VECTOR_A, u)
                link_b = Links(dve, s_vb, VECTOR_B, t)
                norm_x(u, up, link)
                abel_bias(t, link_b)
                expert(t, par, 0)
                context_t(u)
                expert(t, par, 1)
                gates_out(u)
                expert(t, par, 2)
                decay_rows(u, link)
                expert(t, par, 3)
                decayed(u)
                expert(t, par, 4)
                heads(u, link)
                head_norm(u, link)
                expert(t, par, 5)
                norm_stats(u, link)
                norm_apply(u, link)
                expert(t, par, 6)
                norm_split(u, up, link)
                expert(t, par, 7)
                routing(u, up, link)
                mix(t, par, link_b)
                link.end()
                link_b.end()

            first_attend(0, 0)
            body(0, 0)
            body(1, 1)
            with dve.Fori(1, TILES // 2 - 1) as i:
                body(2 * i, 0)
                body(2 * i + 1, 1)
            body(TILES - 2, 0)
            link_b = Links(dve, s_vb, VECTOR_B, TILES - 1)
            abel_bias(TILES - 1, link_b)
            for e in range(E):
                expert(TILES - 1, 1, e)
            mix(TILES - 1, 1, link_b)
            link_b.end()

        @block.tensor
        def _(pe):
            m = nc.tensor

            pe.wait_ge(s_gens, 16)
            pe.wait_ge(s_pool, 2)
            for n in range(NROT):
                ins = m.transpose(pa[:, 0, P * n:P * n + P], ga[:, n, :], ident[:, :])
            ins.then_inc(s_gat_ps, 1)
            for n in range(EXP_STEPS):
                pe.wait_ge(s_exp_t, n + 1)
                pe.wait_ge(s_exp_u, n + 1)
                for r in range(NROT):
                    t_, u_ = tm[:, n % 2, r, :], um[:, n % 2, r, :]
                    squaring = n >= DEGREE - 1
                    m.matmul(pa[:, 0, P * r:P * r + P], u_ if squaring else gat[:, r, :], t_, start=True, stop=True)
                    ins = m.matmul(pa[:, 1, P * r:P * r + P], t_ if squaring else ga[:, r, :], u_,
                                   start=True, stop=True)
                ins.then_inc(s_exp_ps, 1)
            fin = EXP_STEPS % 2
            pe.wait_ge(s_exp_t, EXP_STEPS + 1)
            pe.wait_ge(s_exp_u, EXP_STEPS + 1)
            m.matmul(pa[:, 2, 0:D], um[:, fin, 1, :], tm[:, fin, 2, :], start=True, stop=True).then_inc(s_rot_ps, 1)
            pe.wait_ge(s_rot, 1)
            m.matmul(pa[:, 3, 0:D], um[:, fin, 0, :], rot[:, 0, :], start=True, stop=True).then_inc(s_rot_ps, 1)
            pe.wait_ge(s_w2, 16)
            for n in range(E * HF):
                ins = m.transpose(pb[:, n // 4, P * (n % 4):P * (n % 4) + P], w2s[:, n, :], ident[:, :])
                if n % 4 == 3:
                    ins.then_inc(s_w2_ps, 1)
            pe.wait_ge(s_early, N_EARLY)
            m.transpose(pa[:, 0, 0:E * HF], b1row[:, :], ident[0:E * HF, 0:E * HF])
            m.transpose(pa[:, 0, 16:16 + E], b2s[:, :], ident[0:E, 0:E]).then_inc(s_b1_ps, 1)
            pe.wait_ge(s_rot, 2)
            for n in range(E * HF):
                pe.wait_ge(s_w2_sb, n // 4 + 1)
                ins = m.matmul(pb[:, n // 4, P * (n % 4):P * (n % 4) + P], w2t[:, n, :], rot[:, 1, :],
                               start=True, stop=True)
                if n % 4 == 3:
                    ins.then_inc(s_w2_ps, 1)
            pe.wait_ge(s_b1, 1)
            m.matmul(pa[0:32, 1, 0:D], b2t[:, :, :].rearrange("p c e -> p (c e)"), rot[:, 1, :],
                     start=True, stop=True).then_inc(s_b1_ps, 1)
            pe.wait_ge(s_ready_v, 1)
            pe.wait_ge(s_pool, POOL_STEPS)

            def transposes(u, par):
                pe.wait_ge(s_xq, u + 1)
                after(pe, s_xn, u)
                for c in range(C):
                    ins = m.transpose(pa[:, 0, P * c:P * c + P], xq[:, c, :], ident[:, :])
                ins.then_inc(s_xqT_ps, 1)
                pe.wait_ge(s_c[par], 32 * (u - par) + 64)
                after(pe, s_w, u)
                for k in range(C):
                    ins = m.transpose(pa[:, 1, P * k:P * k + P], cs[:, par, k, :], ident[:, :])
                ins.then_inc(s_cT_ps, 1)

            def gates(u):
                pe.wait_ge(s_xqT, u + 1)
                pe.wait_ge(s_cT, u + 1)
                after(pe, s_hm, u)
                m.matmul(pa[0:2 * NH, 2, :], wgq[:, :], xqT[:, :].rearrange("d (q b n) -> d b q n", q=2, b=2),
                         start=True, stop=False)
                m.matmul(pa[0:2 * NH, 2, :], wgc[:, :], cT[:, :].rearrange("d (k b t) -> d b k t", k=C, b=2),
                         start=False, stop=True).then_inc(s_g_ps, 1)

            def scores(u):
                pe.wait_ge(s_xbd, u + 1)
                for q in (1, 0):
                    for g in range(2):
                        for b in range(2):
                            k = 2 * q + g
                            ins = m.matmul(pa[S * b:S * b + S, q, 256 * g:256 * g + 256],
                                           cT[:, P * k + S * b:P * k + S * b + S],
                                           xbd[:, 4 * q + 2 * b + g, :, :].rearrange("d h s -> d (h s)"),
                                           start=True, stop=True)
                    ins.then_inc(s_qk, 1)

            def exponents(u):
                pe.wait_ge(s_mld, u + 1)
                for g in range(2):
                    pick = ident[0:32, 0:32].rearrange("r (b h q g) -> r g q h b", h=NH, q=2, b=2)[:, g]
                    for q in range(2):
                        ins = m.matmul(pa[S * g:S * g + S, 2, 8 * q:8 * q + 8], mld[:, :], pick[:, q],
                                       start=True, stop=True)
                ins.then_inc(s_enm_ps, 1)
                pe.wait_ge(s_erow, 128 * u + 128)
                for q in (1, 0):
                    if q == 0:
                        pe.wait_ge(s_enm, u + 1)
                    for g in range(2):
                        k = 2 * q + g
                        o = pa[:, 2 + q, 256 * g:256 * g + 256]
                        m.matmul(o, el[:, k].rearrange("r b t -> r (b t)"),
                                 er[:, :, k, :], start=True, stop=False)
                        ins = m.matmul(o, ident_b[:, :], causal[:, :, :].rearrange("p h s -> p (h s)"),
                                       start=False, stop=True)
                    ins.then_inc(s_e, 1)

            def values(u):
                pe.wait_ge(s_vbd, u + 1)
                for n, q in enumerate((1, 0)):
                    pe.wait_ge(s_ct, 2 * u + n + 1)
                    for g in range(2):
                        k = 2 * q + g
                        for h in range(NH):
                            ins = m.matmul(pa[S * g:S * g + S, 2 + q, 2 * V1 * h:2 * V1 * h + 2 * V1],
                                           ct[:, k, S * h:S * h + S],
                                           vbd[:, k, h].rearrange("p b d -> p (b d)"), start=True, stop=True)
                ins.then_inc(s_pv, 1)

            def norm_t(u):
                pe.wait_ge(s_yh, u + 1)
                for c in range(C):
                    ins = m.transpose(pa[:, 0, P * c:P * c + P], yh[:, c, :], ident[:, :])
                ins.then_inc(s_yT_ps, 1)

            def logits(u, par):
                pe.wait_ge(s_xn, u + 1)
                for c in range(C):
                    ins = m.matmul(pa[:, 1, E * c:E * c + E], xn[:, par, P * c:P * c + P], wmg[:, :],
                                   start=True, stop=True)
                ins.then_inc(s_lg_ps, 1)

            def weights_t(t, par):
                pe.wait_ge(s_w, t + 1)
                pe.wait_ge(s_hm, t + 1)
                m.transpose(pa[0:32, 3, 0:P], wr[:, par].rearrange("p c e -> p (c e)"),
                            ident[:, :]).then_inc(s_wT_ps, 1)

            def abel(t, par):
                after(pe, s_y, 10 * t)
                for c in range(C):
                    ins = m.matmul(pb[:, 2, D * c:D * c + D], xn[:, par, P * c:P * c + P], wab[:, :],
                                   start=True, stop=True)
                ins.then_inc(s_y_ps, 1)

            def second_bias(t):
                pe.wait_ge(s_wT, t + 1)
                after(pe, s_y, 10 * t)
                m.matmul(pb[:, 3, :], wT[:, :], b2b[:, :, :].rearrange("r c d -> r (c d)"),
                         start=True, stop=True).then_inc(s_y_ps, 1)

            def hidden(t, par, e):
                if e == 0:
                    pe.wait_ge(s_xns, t + 1)
                for f in range(HF):
                    after(pe, s_h, 16 * t + max(0, 2 * e + f - 1))
                    cols = slice(P * f, P * f + P)
                    m.matmul(pb[:, f, :], w1l[:, e, cols], xnh[:, par, :], start=True, stop=False)
                    m.matmul(pb[:, f, :], w1h[:, e, cols], xnl[:, par, :], start=False, stop=False)
                    m.matmul(pb[:, f, :], w1h[:, e, cols], xnh[:, par, :], start=False,
                             stop=True).then_inc(s_h_ps, 1)

            def output(t, e):
                pe.wait_ge(s_y, 10 * t + 1 + e)
                pe.wait_ge(s_h, 16 * t + 2 * e + 2)
                for c in range(C):
                    for f in range(HF):
                        ins = m.matmul(pb[:, 2 + e % 2, D * c:D * c + D], hT[:, e % 2, f, P * c:P * c + P],
                                       w2r[:, HF * e + f, :], start=(f == 0), stop=(f == HF - 1))
                ins.then_inc(s_y_ps, 1)

            transposes(0, 0)
            gates(0)
            scores(0)
            exponents(0)
            values(0)
            norm_t(0)
            logits(0, 0)

            def body(t, par):
                u, up = t + 1, 1 - par
                weights_t(t, par)
                hidden(t, par, 0)
                abel(t, par)
                hidden(t, par, 1)
                second_bias(t)
                output(t, 0)
                transposes(u, up)
                hidden(t, par, 2)
                output(t, 1)
                gates(u)
                hidden(t, par, 3)
                output(t, 2)
                scores(u)
                hidden(t, par, 4)
                output(t, 3)
                exponents(u)
                hidden(t, par, 5)
                output(t, 4)
                values(u)
                hidden(t, par, 6)
                output(t, 5)
                hidden(t, par, 7)
                output(t, 6)
                norm_t(u)
                output(t, 7)
                logits(u, up)

            body(0, 0)
            body(1, 1)
            with pe.Fori(1, TILES // 2 - 1) as i:
                body(2 * i, 0)
                body(2 * i + 1, 1)
            body(TILES - 2, 0)
            t = TILES - 1
            weights_t(t, 1)
            hidden(t, 1, 0)
            abel(t, 1)
            hidden(t, 1, 1)
            second_bias(t)
            for e in range(E):
                output(t, e)
                if e + 2 < E:
                    hidden(t, 1, e + 2)


_INS = ['x', 'ctx_1024', 'L0_xattn_ig_kernel', 'L0_xattn_ig_bias', 'L0_xattn_fg_kernel', 'L0_xattn_fg_bias',
        'L0_xattn_outnorm_weight', 'L0_ffn_ln_gamma', 'L0_ffn_ln_beta', 'L0_ffn_abel_w', 'L0_ffn_abel_b',
        'L0_ffn_moe_gate_w', 'L0_ffn_moe_gate_b', 'L0_ffn_ew1', 'L0_ffn_eb1', 'L0_ffn_ew2', 'L0_ffn_eb2',
        'L0_ffn_gens', 'L0_ffn_gc_w', 'L0_ffn_gc_b']


def kernel(**inputs):
    import numpy as _np
    import concourse.bacc as _bacc
    from concourse import mybir as _mybir
    from concourse.bass_utils import run_bass_kernel_spmd as _run

    nc = _bacc.Bacc("TRN2", target_bir_lowering=False, num_devices=1)
    arrays, args = {}, []
    for name in _INS:
        a = _np.ascontiguousarray(inputs[name])
        arrays[f"in_{name}_dram"] = a
        args.append(nc.dram_tensor(f"in_{name}_dram", a.shape, _mybir.dt.from_np(a.dtype), kind="ExternalInput").ap())
    shape = inputs["x"].shape
    args.append(nc.dram_tensor("out_0_dram", shape, _mybir.dt.float32, kind="ExternalOutput").ap())
    build(nc, *args)
    r = _run(nc, [arrays], core_ids=[0])
    return r.results[0]["out_0_dram"]
```

```python
from contextlib import ExitStack

import concourse.bass as bass
from concourse import mybir

F32 = mybir.dt.float32
F32R = mybir.dt.float32r
BF16 = mybir.dt.bfloat16
ALU = mybir.AluOpType
ACT = mybir.ActivationFunctionType
AX_X = mybir.AxisListType.X

P = 128
S = 64
D = 128
NH = 4
DH = D // NH
SEQ = 8
C = 4
T = C * P
E = 8
HID = 256
HF = HID // P
WT_COL = 512 - P
V1 = DH + 1
EPS_NORM = 1e-5
EPS_HEAD = 1e-6
EPS_DEN = 1e-6
QK_SCALE = DH ** -0.5
NEG = -1e30
HALVINGS = 7
DEGREE = 8
NROT = 3

VECTOR_ATTEND, VECTOR_NORM, VECTOR_MIX = 9, 28, 1
POOL_ATTEND, POOL_NORM, POOL_MIX = 1, 1, 1
POOL_STEPS = 14


class Links:

    def __init__(self, eng, sem, per_tile, tile):
        self.eng, self.sem, self.per_tile, self.base, self.n = eng, sem, per_tile, tile * per_tile, 0

    def __call__(self, ins):
        self.n += 1
        ins.then_inc(self.sem, 1)
        self.eng.wait_ge(self.sem, self.base + self.n)

    def end(self):
        assert self.n == self.per_tile, (self.n, self.per_tile)


def after(eng, sem, value):
    if not isinstance(value, int) or value > 0:
        eng.wait_ge(sem, value)


def build(nc, x, ctx_in, ig_w, ig_b, fg_w, fg_b, onorm_w, ln_g, ln_b, abel_w, abel_b, mg_w, mg_b,
          ew1, eb1, ew2, eb2, gens, gc_w, gc_b, out):
    TILES = x.shape[0] // SEQ
    assert TILES % 2 == 0 and TILES >= 6
    xf = x.rearrange("b s d -> (b s) d")
    outf = out.rearrange("b s d -> (b s) d")

    with ExitStack() as stack:
        def sb(name, shape, dt=F32):
            return stack.enter_context(nc.sbuf_tensor(name, shape, dt))

        def sem(name):
            return stack.enter_context(nc.semaphore(name))

        pa = stack.enter_context(nc.psum_tensor("pa", [P, 4, 512], F32))
        pb = stack.enter_context(nc.psum_tensor("pb", [P, 4, 512], F32))

        ident = sb("ident", [P, P])
        ident_b = sb("ident_b", [P, P], BF16)
        eye3 = sb("eye3", [P, NROT, P])
        causal = sb("causal", [P, NH, S], BF16)
        ones_row = sb("ones_row", [32, S])
        mhalf = sb("mhalf", [P, 16])
        rev = sb("rev", [P, E])
        w1f = sb("w1f", [P, E, HID])
        w1h = sb("w1h", [P, E, HID], F32R)
        w1l = sb("w1l", [P, E, HID], F32R)
        w2s = sb("w2s", [P, E * HF, D])
        w2t = sb("w2t", [P, E * HF, P])
        w2r = sb("w2r", [P, E * HF, D])
        b1 = sb("b1", [P, E, HF])
        b1row = sb("b1row", [E * HF, P])
        b2s = sb("b2s", [E, D])
        b2t = sb("b2t", [P, C, E])
        b2m = sb("b2m", [32, C])
        b2b = sb("b2b", [32, C, D])
        wab = sb("wab", [P, D])
        bab = sb("bab", [P, D])
        wmg = sb("wmg", [P, E])
        bmg = sb("bmg", [P, E])
        wgr = sb("wgr", [P, 3, 2, NH])
        wgq = sb("wgq", [P, 2 * NH])
        wgc = sb("wgc", [P, 2 * NH])
        bg = sb("bg", [2 * NH, 1])
        lng = sb("lng", [P, 1])
        lnb = sb("lnb", [P, 1])
        onw = sb("onw", [P, D])
        gc1 = sb("gc1", [P, D])
        gc2 = sb("gc2", [P, D])
        gcb = sb("gcb", [P, 1])
        hgcb = sb("hgcb", [P, 1])
        ga = sb("ga", [P, NROT, P])
        gat = sb("gat", [P, NROT, P])
        tm = sb("tm", [P, 2, NROT, P])
        um = sb("um", [P, 2, NROT, P])
        rot = sb("rot", [P, 2, D])

        xs = sb("xs", [P, 2, C, D])
        cs = sb("cs", [P, 2, C, D])
        st = sb("st", [P, C, 6])
        ssum = sb("ssum", [P, C])
        sdif = sb("sdif", [P, C])
        ssq = sb("ssq", [P, C])
        mean = sb("mean", [P, C])
        xmean = sb("xmean", [P, C])
        vr = sb("vr", [P, C])
        var = sb("var", [P, C])
        rstd = sb("rstd", [P, C])
        carrier = sb("carrier", [1, 1])
        xq = sb("xq", [P, C, D])
        xqT = sb("xqT", [P, T])
        cT = sb("cT", [P, T])
        xbd = sb("xbd", [P, SEQ, NH, S])
        vbd = sb("vbd", [P, C, NH, 2, V1])
        gT = sb("gT", [2 * NH, T])
        gr = sb("gr", [32, 2, S])
        fabs = sb("fabs", [32, S])
        fexp = sb("fexp", [32, S])
        fln = sb("fln", [32, S])
        lf = sb("lf", [32, S])
        cum = sb("cum", [32, S])
        av = sb("av", [32, S])
        mx = sb("mx", [32, S])
        mld = sb("mld", [32, S])
        ah = sb("ah", [32, S], F32R)
        al = sb("al", [32, S], F32R)
        mh = sb("mh", [32, S], F32R)
        ml = sb("ml", [32, S], F32R)
        elc = sb("elc", [12, C, 2, S])
        erc = sb("erc", [12, NH, C, S])
        el = sb("el", [12, C, 2, S], F32R)
        er = sb("er", [12, NH, C, S], F32R)
        dm = sb("dm", [P, C, NH * S])
        ct = sb("ct", [P, C, NH * S])
        enm = sb("enm", [P, 2, 2 * NH])
        den = sb("den", [P, 2, 2 * NH])
        hm = sb("hm", [P, C * NH, DH])
        hsum = sb("hsum", [P, C * NH])
        hmean = sb("hmean", [P, C * NH])
        hc = sb("hc", [P, C * NH, DH])
        hsq = sb("hsq", [P, C * NH, DH])
        hvar = sb("hvar", [P, C * NH])
        hrs = sb("hrs", [P, C * NH])
        ha = sb("ha", [P, C * NH, DH])
        hw = sb("hw", [P, C, D])
        x1 = sb("x1", [P, C, D])
        v2 = sb("v2", [P, C])
        v2e = sb("v2e", [P, C])
        r1 = sb("r1", [P, C])
        r2 = sb("r2", [P, C])
        rr = sb("rr", [P, C])
        p1 = sb("p1", [P, C])
        nm = sb("nm", [P, C])
        yh = sb("yh", [P, C, D])
        base = sb("base", [P, 2, C, D])
        xn = sb("xn", [P, 2, T])
        xnh = sb("xnh", [P, 2, T], F32R)
        xnl = sb("xnl", [P, 2, T], F32R)
        lg = sb("lg", [P, C, E])
        lg2 = sb("lg2", [P, C, E])
        k1 = sb("k1", [P, C, E])
        k2 = sb("k2", [P, C, E])
        o1 = sb("o1", [P, C, E])
        o2 = sb("o2", [P, C, E])
        m1 = sb("m1", [P, C])
        m2 = sb("m2", [P, C])
        kk = sb("kk", [P, C])
        dl = sb("dl", [P, C])
        th = sb("th", [P, C])
        wa = sb("wa", [P, C])
        wb = sb("wb", [P, C])
        wr = sb("wr", [P, 2, C, E])

        hT = sb("hT", [P, 2, HF, T])
        wT = sb("wT", [32, P])
        acc = sb("acc", [P, 2, C, D])
        abp = sb("abp", [P, C, D])
        ab = sb("ab", [P, 2, C, D])
        z1 = sb("z1", [P, C, D])
        z2 = sb("z2", [P, C, D])
        zz = sb("zz", [P, C, D])
        zs = sb("zs", [P, C])
        zt = sb("zt", [P, C])
        gate = sb("gate", [P, C])
        diff = sb("diff", [P, C, D])
        bab2 = sb("bab2", [P, C, D])
        res = sb("res", [P, 2, C, D])

        s_early = sem("s_early")
        s_w1 = sem("s_w1")
        s_w2 = sem("s_w2")
        s_gens = sem("s_gens")
        s_pool = sem("s_pool")
        s_setup_v = sem("s_setup_v")
        s_ready_v = sem("s_ready_v")
        s_gat_ps = sem("s_gat_ps")
        s_exp_ps = sem("s_exp_ps")
        s_exp_t = sem("s_exp_t")
        s_exp_u = sem("s_exp_u")
        s_rot_ps = sem("s_rot_ps")
        s_rot = sem("s_rot")
        s_w2_ps = sem("s_w2_ps")
        s_w2_sb = sem("s_w2_sb")
        s_b1_ps = sem("s_b1_ps")
        s_b1 = sem("s_b1")
        s_x = [sem("s_x0"), sem("s_x1")]
        s_c = [sem("s_c0"), sem("s_c1")]
        s_v_attend = sem("s_v_attend")
        s_v_norm = sem("s_v_norm")
        s_v_mix = sem("s_v_mix")
        s_g_attend = sem("s_g_attend")
        s_g_norm = sem("s_g_norm")
        s_g_mix = sem("s_g_mix")
        s_xvar = sem("s_xvar")
        s_xrstd = sem("s_xrstd")
        s_xq = sem("s_xq")
        s_xqT_ps = sem("s_xqT_ps")
        s_xqT = sem("s_xqT")
        s_cT_ps = sem("s_cT_ps")
        s_cT = sem("s_cT")
        s_xbd = sem("s_xbd")
        s_vbd = sem("s_vbd")
        s_g_ps = sem("s_g_ps")
        s_gT = sem("s_gT")
        s_gr = sem("s_gr")
        s_fabs = sem("s_fabs")
        s_fexp = sem("s_fexp")
        s_fln = sem("s_fln")
        s_mld = sem("s_mld")
        s_ah = sem("s_ah")
        s_erow = sem("s_erow")
        s_qk = sem("s_qk")
        s_e = sem("s_e")
        s_d = sem("s_d")
        s_ct = sem("s_ct")
        s_pv = sem("s_pv")
        s_enm_ps = sem("s_enm_ps")
        s_enm = sem("s_enm")
        s_hm = sem("s_hm")
        s_hc = sem("s_hc")
        s_hsq = sem("s_hsq")
        s_hvar = sem("s_hvar")
        s_hrs = sem("s_hrs")
        s_ha = sem("s_ha")
        s_x1 = sem("s_x1_")
        s_v2 = sem("s_v2")
        s_r1 = sem("s_r1")
        s_v2e = sem("s_v2e")
        s_r2 = sem("s_r2")
        s_yh = sem("s_yh")
        s_base = sem("s_base")
        s_nm = sem("s_nm")
        s_yT_ps = sem("s_yT_ps")
        s_xn = sem("s_xn")
        s_xns = sem("s_xns")
        s_lg_ps = sem("s_lg_ps")
        s_lg = sem("s_lg")
        s_dl = sem("s_dl")
        s_th = sem("s_th")
        s_w = sem("s_w")
        s_h_ps = sem("s_h_ps")
        s_h = sem("s_h")
        s_y_ps = sem("s_y_ps")
        s_y = sem("s_y")
        s_ab = sem("s_ab")
        s_wT_ps = sem("s_wT_ps")
        s_wT = sem("s_wT")
        s_zz = sem("s_zz")
        s_zs = sem("s_zs")
        s_zt = sem("s_zt")
        s_db = sem("s_db")
        s_res = sem("s_res")
        s_out = [sem("s_out0"), sem("s_out1")]

        EXP_STEPS = DEGREE - 1 + HALVINGS
        N_EARLY = 16 * 16

        block = stack.enter_context(nc.Block())

        @block.sync
        def _(sp):
            def load(u, par, first=False):
                row, first_seq = sp.snap(u * T), sp.snap(u * SEQ)
                if not first:
                    sp.wait_ge(s_x1, u - 1)
                    sp.wait_ge(s_cT_ps, u - 1)
                    sp.wait_ge(s_vbd, u - 1)
                sp.dma_start(xs[:, par], xf[bass.ds(row, T), :].rearrange("(c p) d -> p c d", p=P)
                             ).then_inc(s_x[par], 16)
                src = ctx_in[bass.ds(first_seq, SEQ), :, :].rearrange("(q b g) t d -> b q t g d", q=2, b=2)
                for b in range(2):
                    for q in range(2):
                        sp.dma_start(cs[S * b:S * b + S, par, 2 * q:2 * q + 2], src[b, q]).then_inc(s_c[par], 16)

            def gate_rows(u):
                sp.wait_ge(s_gT, u + 1)
                for j in range(2):
                    for b in range(2):
                        sp.dma_start(gr[16 * b:16 * b + 16, j, :],
                                     gT[NH * j:NH * j + NH, 256 * b:256 * b + 256].rearrange(
                                         "h (n t) -> h n t", n=4)).then_inc(s_gr, 16)

            def decay_rows(u):
                sp.wait_ge(s_ah, u + 1)
                for n, (gates, maxima) in enumerate(((ah, mh), (al, ml))):
                    for b in range(2):
                        rows = slice(16 * b, 16 * b + 16)
                        sp.dma_start(el[NH * n:NH * n + NH, :, b].bitcast(F32), gates[rows, :].bitcast(F32)
                                     ).then_inc(s_erow, 16)
                        row = 2 * NH + 2 * n + b
                        sp.dma_start(er[row:row + 1].bitcast(F32), maxima[rows, :].bitcast(F32)
                                     ).then_inc(s_erow, 16)

            def store(t, par):
                row = sp.snap(t * T)
                sp.wait_ge(s_res, t + 1)
                sp.dma_start(outf[bass.ds(row, T), :].rearrange("(c p) d -> p c d", p=P), res[:, par]
                             ).then_inc(s_out[par], 16)

            def bcast(row, n):
                return row.rearrange("(a n) -> a n", a=1).broadcast_to([P, n])

            load(0, 0, True)
            for j, w in enumerate((ig_w, fg_w)):
                sp.dma_start(wgr[:, :, j, :], w.rearrange("(r d) h -> d r h", r=3)).then_inc(s_early, 16)
            sp.dma_start(bg[0:NH, :], ig_b.rearrange("(h a) -> h a", a=1)).then_inc(s_early, 16)
            sp.dma_start(bg[NH:2 * NH, :], fg_b.rearrange("(h a) -> h a", a=1)).then_inc(s_early, 16)
            sp.dma_start(ga[:, :, :], gens.rearrange("r i j -> i r j")).then_inc(s_gens, 16)
            sp.dma_start(onw[:, :], bcast(onorm_w.rearrange("h d -> (h d)"), D)).then_inc(s_early, 16)
            sp.dma_start(lng[:, :], ln_g.rearrange("(d a) -> d a", a=1)).then_inc(s_early, 16)
            sp.dma_start(lnb[:, :], ln_b.rearrange("(d a) -> d a", a=1)).then_inc(s_early, 16)
            sp.dma_start(wmg[:, :], mg_w).then_inc(s_early, 16)
            sp.dma_start(bmg[:, :], bcast(mg_b, E)).then_inc(s_early, 16)
            sp.dma_start(wab[:, :], abel_w).then_inc(s_early, 16)
            sp.dma_start(bab[:, :], bcast(abel_b, D)).then_inc(s_early, 16)
            sp.dma_start(b1row[:, :], eb1.rearrange("e (f p) -> (e f) p", f=HF)).then_inc(s_early, 16)
            sp.dma_start(b2s[:, :], eb2).then_inc(s_early, 16)
            gcv = gc_w.rearrange("d a -> (d a)")
            sp.dma_start(gc1[:, :], bcast(gcv[0:D], D)).then_inc(s_early, 16)
            sp.dma_start(gc2[:, :], bcast(gcv[D:2 * D], D)).then_inc(s_early, 16)
            sp.dma_start(gcb[:, :], bcast(gc_b, 1)).then_inc(s_early, 16)
            sp.dma_start(w2s[:, :, :], ew2.rearrange("e (f p) d -> p (e f) d", f=HF)).then_inc(s_w2, 16)
            sp.dma_start(w1f[:, :, :], ew1.rearrange("e d h -> d e h")).then_inc(s_w1, 16)
            load(1, 1, True)
            gate_rows(0)
            decay_rows(0)
            gate_rows(1)

            def body(t, par, stored=True):
                load(t + 2, par)
                decay_rows(t + 1)
                if stored:
                    store(t - 2, par)
                gate_rows(t + 2)

            body(0, 0, stored=False)
            body(1, 1, stored=False)
            with sp.Fori(1, TILES // 2 - 1) as i:
                body(2 * i, 0)
                body(2 * i + 1, 1)
            decay_rows(TILES - 1)
            for t in range(TILES - 4, TILES):
                store(t, t % 2)
            for par in range(2):
                sp.wait_ge(s_out[par], 16 * (TILES // 2))

        @block.gpsimd
        def _(pool):
            g = nc.gpsimd
            steps = 0

            def step(ins):
                nonlocal steps
                steps += 1
                ins.then_inc(s_pool, 1)
                pool.wait_ge(s_pool, steps)

            step(g.memset(ident[:, :], 0.0))
            step(g.affine_select(out=ident[:, :], in_=ident[:, :], compare_op=ALU.not_equal, fill=1.0,
                                 base=0, pattern=[[-1, P]], channel_multiplier=1))
            for n in range(NROT):
                g.tensor_copy(eye3[:, n, :], ident[:, :])
            g.tensor_copy(ident_b[:, :], ident[:, :])
            g.memset(mhalf[:, :], -0.5)
            g.memset(ones_row[:, :], 1.0)
            for e in range(E):
                g.memset(rev[:, e:e + 1], float(E - e))
            step(g.memset(causal[:, :, :], 0.0))
            for b in range(2):
                half = causal[S * b:S * b + S, :, :]
                step(g.affine_select(out=half, in_=half, compare_op=ALU.is_ge, fill=NEG, base=0,
                                     pattern=[[0, NH], [1, S]], channel_multiplier=-1))
            g.memset(elc[:, :, :, :], 0.0)
            g.memset(erc[:, :, :, :], 0.0)
            g.memset(b2m[:, :], 1.0)
            g.memset(xbd[:, :, :, :], 0.0)
            step(g.memset(vbd[:, :, :, :, :], 0.0))
            for n in range(2):
                step(g.affine_select(out=erc[:, :, :, :], in_=erc[:, :, :, :], compare_op=ALU.not_equal,
                                     fill=1.0, base=-NH * n, pattern=[[-1, NH], [0, C], [0, S]],
                                     channel_multiplier=1))
                step(g.affine_select(out=elc[:, :, :, :], in_=elc[:, :, :, :], compare_op=ALU.not_equal,
                                     fill=1.0, base=-2 * NH - 2 * n, pattern=[[0, C], [-1, 2], [0, S]],
                                     channel_multiplier=1))
            step(g.affine_select(out=b2m[:, :], in_=b2m[:, :], compare_op=ALU.is_ge, fill=0.0,
                                 base=0, pattern=[[-E, C]], channel_multiplier=1))
            step(g.affine_select(out=b2m[:, :], in_=b2m[:, :], compare_op=ALU.is_ge, fill=0.0,
                                 base=E - 1, pattern=[[E, C]], channel_multiplier=-1))
            for b in range(2):
                step(g.memset(vbd[S * b:S * b + S, :, :, b, DH:V1], 1.0))

            def carry():
                g.tensor_tensor(carrier[:, :], mhalf[0:1, 0:1], mhalf[0:1, 0:1], ALU.mult)

            def query_rstd(u):
                pool.wait_ge(s_xvar, u + 1)
                g.tensor_tensor(rstd[:, :], var[:, :], mhalf[:, 0:C], ALU.pow).then_inc(s_xrstd, 1)

            def values_split(u, par, link):
                pool.wait_ge(s_c[par], 32 * (u - par) + 64)
                after(pool, s_pv, u)
                halves = [(vbd[S * b:S * b + S, :, :, b, 0:DH],
                           cs[S * b:S * b + S, par].rearrange("t k (h d) -> t k h d", h=NH)) for b in range(2)]
                carry()
                link(g.tensor_copy(*halves[0]))
                carry()
                g.tensor_copy(*halves[1]).then_inc(s_vbd, 1)
                pool.wait_ge(s_vbd, u + 1)

            def head_rstd(u):
                pool.wait_ge(s_hvar, u + 1)
                g.tensor_tensor(hrs[:, :], hvar[:, :], mhalf[:, :], ALU.pow).then_inc(s_hrs, 1)

            def residual(u, par, link):
                pool.wait_ge(s_ha, u + 1)
                link(g.tensor_tensor(hw[:, :, :], ha[:, :, :].rearrange("p (c h) d -> p c (h d)", c=C),
                                     onw[:, :].unsqueeze(1).broadcast_to([P, C, D]), ALU.mult))
                g.tensor_tensor(x1[:, :, :], hw[:, :, :], xs[:, par], ALU.add).then_inc(s_x1, 1)

            def norm_rstd(u):
                pool.wait_ge(s_v2, u + 1)
                g.tensor_tensor(r1[:, :], v2[:, :], mhalf[:, 0:C], ALU.pow).then_inc(s_r1, 1)
                pool.wait_ge(s_v2e, u + 1)
                g.tensor_tensor(r2[:, :], v2e[:, :], mhalf[:, 0:C], ALU.pow).then_inc(s_r2, 1)

            def base_sum(u, par):
                pool.wait_ge(s_nm, u + 1)
                carry()
                for c in range(C):
                    ins = g.tensor_scalar(base[:, par, c, :], x1[:, c, :], p1[:, c:c + 1], nm[:, c:c + 1],
                                          ALU.mult, ALU.add)
                ins.then_inc(s_base, 1)
                pool.wait_ge(s_base, u + 1)

            def gate_abel(t, par):
                after(pool, s_zz, t)
                pool.wait_ge(s_ab, t + 1)
                g.tensor_tensor(z1[:, :, :], ab[:, par], gc1[:, :].unsqueeze(1).broadcast_to([P, C, D]), ALU.mult)

            def gate_sum(t, par, link):
                pool.wait_ge(s_y, 10 * t + 10)
                link(g.tensor_tensor(z2[:, :, :], acc[:, par],
                                     gc2[:, :].unsqueeze(1).broadcast_to([P, C, D]), ALU.mult))
                g.tensor_tensor(zz[:, :, :], z1[:, :, :], z2[:, :, :], ALU.add).then_inc(s_zz, 1)

            def mix_terms(t, par):
                g.tensor_tensor(diff[:, :, :], acc[:, par], ab[:, par], ALU.subtract)
                g.tensor_tensor(bab2[:, :, :], base[:, par], ab[:, par], ALU.add).then_inc(s_db, 1)

            def body(t, par, attend=True, norm=True, experts=True, mix=True):
                other = 1 - par
                link_a = Links(pool, s_g_attend, POOL_ATTEND, t + 2)
                link_n = Links(pool, s_g_norm, POOL_NORM, t + 1)
                link_m = Links(pool, s_g_mix, POOL_MIX, t - 1)
                if attend:
                    query_rstd(t + 2)
                if mix:
                    gate_sum(t - 1, other, link_m)
                if norm:
                    head_rstd(t + 1)
                    residual(t + 1, other, link_n)
                if mix:
                    mix_terms(t - 1, other)
                if norm:
                    norm_rstd(t + 1)
                    base_sum(t + 1, other)
                if attend:
                    values_split(t + 2, par, link_a)
                if experts:
                    gate_abel(t, par)
                for stage, link in ((attend, link_a), (norm, link_n), (mix, link_m)):
                    if stage:
                        link.end()

            assert steps == POOL_STEPS
            pool.wait_ge(s_early, N_EARLY)
            body(-2, 0, norm=False, experts=False, mix=False)
            body(-1, 1, experts=False, mix=False)
            body(0, 0, mix=False)
            body(1, 1)
            with pool.Fori(1, TILES // 2 - 1) as i:
                body(2 * i, 0)
                body(2 * i + 1, 1)
            body(TILES - 2, 0, attend=False)
            body(TILES - 1, 1, attend=False, norm=False)
            link_m = Links(pool, s_g_mix, POOL_MIX, TILES - 1)
            gate_sum(TILES - 1, 1, link_m)
            mix_terms(TILES - 1, 1)

        @block.scalar
        def _(act):
            a = nc.scalar

            def gelu(t, e):
                for f in range(HF):
                    act.wait_ge(s_h_ps, 16 * t + 2 * e + f + 1)
                    if e >= 2:
                        act.wait_ge(s_y_ps, 10 * t + 2 + e - 1)
                    else:
                        after(act, s_y_ps, 10 * t)
                    a.activation(hT[:, e % 2, f, :], pb[:, f, :], ACT.Gelu, bias=b1[:, e, f:f + 1]).then_inc(s_h, 1)

            def gelu_abel(t, par):
                act.wait_ge(s_y, 10 * t + 1)
                after(act, s_db, t - 1)
                a.activation(ab[:, par], abp[:, :, :], ACT.Gelu).then_inc(s_ab, 1)

            def query_t(u):
                act.wait_ge(s_xqT_ps, u + 1)
                after(act, s_g_ps, u)
                a.activation(xqT[:, :], pa[:, 0, :], ACT.Copy).then_inc(s_xqT, 1)
                after(act, s_qk, 2 * u)
                for h in range(NH):
                    rows = slice(DH * h, DH * h + DH)
                    ins = a.activation(xbd[rows, :, h, :], pa[rows, 0, :].rearrange("d (b s) -> d b s", b=SEQ),
                                       ACT.Copy)
                ins.then_inc(s_xbd, 1)

            def head_squares(u):
                act.wait_ge(s_hc, u + 1)
                a.activation(hsq[:, :, :], hc[:, :, :], ACT.Square).then_inc(s_hsq, 1)

            def log_sigmoid(u):
                act.wait_ge(s_gr, 64 * u + 64)
                a.activation(fabs[:, :], gr[:, 1, :], ACT.Abs).then_inc(s_fabs, 1)
                act.wait_ge(s_fabs, u + 1)
                a.activation(fexp[:, :], fabs[:, :], ACT.Exp, scale=-1.0).then_inc(s_fexp, 1)
                act.wait_ge(s_fexp, u + 1)
                a.activation(fln[:, :], fexp[:, :], ACT.Ln, bias=1.0).then_inc(s_fln, 1)

            def decay(u):
                act.wait_ge(s_enm_ps, u + 1)
                a.activation(enm[:, :, :].rearrange("p q n -> p (q n)"), pa[:, 2, 0:16], ACT.Exp,
                             scale=-1.0).then_inc(s_enm, 1)
                for n, q in enumerate((1, 0)):
                    act.wait_ge(s_e, 2 * u + n + 1)
                    a.activation(dm[:, 2 * q:2 * q + 2, :].rearrange("p k n -> p (k n)"), pa[:, 2 + q, :],
                                 ACT.Exp).then_inc(s_d, 1)

            def norm_t(u, par):
                act.wait_ge(s_yT_ps, u + 1)
                a.activation(xn[:, par, :], pa[:, 3, :], ACT.Identity, bias=lnb[:, 0:1],
                             scale=lng[:, 0:1]).then_inc(s_xn, 1)

            def route(u):
                act.wait_ge(s_dl, u + 1)
                a.activation(th[:, :], dl[:, :], ACT.Tanh, scale=0.5).then_inc(s_th, 1)

            def mix_gate(t):
                act.wait_ge(s_zs, t + 1)
                a.activation(zt[:, :], zs[:, :], ACT.Tanh, bias=hgcb[:, 0:1], scale=0.5).then_inc(s_zt, 1)

            for n in range(EXP_STEPS):
                if n >= DEGREE - 1 and n < EXP_STEPS:
                    act.wait_ge(s_exp_ps, n + 1)
                    a.activation(um[:, (n + 1) % 2, :, :].rearrange("p r n -> p (r n)"), pa[:, 1, 0:NROT * P],
                                 ACT.Copy).then_inc(s_exp_u, 1)
            act.wait_ge(s_ready_v, 1)

            def body(t, par, attend=True, norm=True, experts=True, mix=True):
                if experts:
                    gelu(t, 0)
                if norm:
                    head_squares(t + 1)
                if experts:
                    gelu_abel(t, par)
                    gelu(t, 1)
                if attend:
                    query_t(t + 2)
                if experts:
                    gelu(t, 2)
                if mix:
                    mix_gate(t - 1)
                if experts:
                    gelu(t, 3)
                if attend:
                    log_sigmoid(t + 2)
                if experts:
                    gelu(t, 4)
                    gelu(t, 5)
                if norm:
                    norm_t(t + 1, 1 - par)
                if experts:
                    gelu(t, 6)
                    gelu(t, 7)
                if attend:
                    decay(t + 2)
                if norm:
                    route(t + 1)

            body(-2, 0, norm=False, experts=False, mix=False)
            body(-1, 1, experts=False, mix=False)
            body(0, 0, mix=False)
            body(1, 1)
            with act.Fori(1, TILES // 2 - 1) as i:
                body(2 * i, 0)
                body(2 * i + 1, 1)
            body(TILES - 2, 0, attend=False)
            body(TILES - 1, 1, attend=False, norm=False)
            mix_gate(TILES - 1)

        @block.vector
        def _(dve):
            v = nc.vector
            steps = 0

            def step(ins):
                nonlocal steps
                steps += 1
                ins.then_inc(s_setup_v, 1)
                dve.wait_ge(s_setup_v, steps)

            dve.wait_ge(s_gens, 16)
            dve.wait_ge(s_pool, 3)
            dve.wait_ge(s_gat_ps, 1)
            g3 = "p r n -> p (r n)"
            v.tensor_scalar(gat[:, :, :].rearrange(g3), pa[:, 0, 0:NROT * P], 2.0 ** -HALVINGS, None, ALU.mult)
            step(v.tensor_scalar(ga[:, :, :], ga[:, :, :], 2.0 ** -HALVINGS, None, ALU.mult))
            v.scalar_tensor_tensor(out=tm[:, 0], in0=ga[:, :, :], scalar=1.0 / DEGREE, in1=eye3[:, :, :],
                                   op0=ALU.mult, op1=ALU.add).then_inc(s_exp_t, 1)
            v.scalar_tensor_tensor(out=um[:, 0], in0=gat[:, :, :], scalar=1.0 / DEGREE, in1=eye3[:, :, :],
                                   op0=ALU.mult, op1=ALU.add).then_inc(s_exp_u, 1)
            for n in range(EXP_STEPS):
                dve.wait_ge(s_exp_ps, n + 1)
                tn = tm[:, (n + 1) % 2, :, :].rearrange(g3)
                un = um[:, (n + 1) % 2, :, :].rearrange(g3)
                k = DEGREE - 1 - n
                if k > 0:
                    v.scalar_tensor_tensor(out=tn, in0=pa[:, 0, 0:NROT * P], scalar=1.0 / k,
                                           in1=eye3[:, :, :].rearrange(g3), op0=ALU.mult,
                                           op1=ALU.add).then_inc(s_exp_t, 1)
                    v.scalar_tensor_tensor(out=un, in0=pa[:, 1, 0:NROT * P], scalar=1.0 / k,
                                           in1=eye3[:, :, :].rearrange(g3), op0=ALU.mult,
                                           op1=ALU.add).then_inc(s_exp_u, 1)
                else:
                    v.tensor_copy(tn, pa[:, 0, 0:NROT * P]).then_inc(s_exp_t, 1)
            for n in range(2):
                dve.wait_ge(s_rot_ps, n + 1)
                v.tensor_copy(rot[:, n, :], pa[:, 2 + n, 0:D]).then_inc(s_rot, 1)
            for n in range(4):
                dve.wait_ge(s_w2_ps, n + 1)
                v.tensor_copy(w2t[:, 4 * n:4 * n + 4, :].rearrange(g3), pb[:, n, :]).then_inc(s_w2_sb, 1)
            dve.wait_ge(s_b1_ps, 1)
            v.tensor_copy(b1[:, :, :].rearrange("p e f -> p (e f)"), pa[:, 0, 0:E * HF])
            v.tensor_copy(b2t[:, :, :], pa[:, 0, 16:16 + E].unsqueeze(1).broadcast_to([P, C, E])).then_inc(s_b1, 1)
            for n in range(4):
                dve.wait_ge(s_w2_ps, 4 + n + 1)
                v.tensor_copy(w2r[:, 4 * n:4 * n + 4, :].rearrange(g3), pb[:, n, :]).then_inc(s_w2_sb, 1)
            dve.wait_ge(s_b1_ps, 2)
            dve.wait_ge(s_pool, POOL_STEPS)
            v.tensor_tensor(b2b[:, :, :], pa[0:32, 1, 0:D].unsqueeze(1).broadcast_to([32, C, D]),
                            b2m[:, :].unsqueeze(2).broadcast_to([32, C, D]), ALU.mult)
            dve.wait_ge(s_w1, 16)
            step(v.tensor_copy(w1h[:, :, :], w1f[:, :, :]))
            v.tensor_tensor(w1l[:, :, :], w1f[:, :, :], w1h[:, :, :].bitcast(F32), ALU.subtract)
            dve.wait_ge(s_early, N_EARLY)
            v.tensor_copy(wgq[:, :].rearrange("d (j h) -> d j h", j=2), wgr[:, 0])
            v.tensor_tensor(wgc[:, :].rearrange("d (j h) -> d j h", j=2), wgr[:, 1], wgr[:, 2], ALU.add)
            v.tensor_scalar(hgcb[:, :], gcb[:, :], 0.5, None, ALU.mult)
            v.tensor_copy(el[:, :, :, :], elc[:, :, :, :])
            v.tensor_copy(er[:, :, :, :], erc[:, :, :, :]).then_inc(s_ready_v, 1)

            def statistics(src, link):
                for c in range(C):
                    ins = v.bn_stats(st[:, c, :], src[:, c, :])
                link(ins)
                v.tensor_tensor(sdif[:, :], st[:, :, 1], st[:, :, 4], ALU.subtract)
                v.tensor_tensor(ssum[:, :], st[:, :, 1], st[:, :, 4], ALU.add)
                link(v.tensor_tensor(ssq[:, :], st[:, :, 2], st[:, :, 5], ALU.add))
                v.tensor_scalar(mean[:, :], ssum[:, :], 0.5, None, ALU.mult)
                link(v.scalar_tensor_tensor(out=sdif[:, :], in0=sdif[:, :], scalar=0.25, in1=sdif[:, :],
                                            op0=ALU.mult, op1=ALU.mult))
                link(v.scalar_tensor_tensor(out=vr[:, :], in0=ssq[:, :], scalar=1.0 / D, in1=sdif[:, :],
                                            op0=ALU.mult, op1=ALU.add))

            def query_stats(u, par, link):
                dve.wait_ge(s_x[par], 8 * (u - par) + 16)
                statistics(xs[:, par], link)
                v.tensor_copy(xmean[:, :], mean[:, :])
                v.tensor_scalar(var[:, :], vr[:, :], EPS_NORM, None, ALU.add).then_inc(s_xvar, 1)

            def query_norm(u, par):
                dve.wait_ge(s_xrstd, u + 1)
                after(dve, s_xqT_ps, u)
                for c in range(C):
                    ins = v.tensor_scalar(xq[:, c, :], xs[:, par, c, :], xmean[:, c:c + 1], rstd[:, c:c + 1],
                                          ALU.subtract, ALU.mult)
                ins.then_inc(s_xq, 1)

            def context_t(u):
                dve.wait_ge(s_cT_ps, u + 1)
                after(dve, s_qk, 2 * u)
                v.tensor_copy(cT[:, :], pa[:, 1, :]).then_inc(s_cT, 1)

            def gates_out(u):
                dve.wait_ge(s_g_ps, u + 1)
                v.tensor_scalar(gT[:, :], pa[0:2 * NH, 2, :], bg[:, 0:1], None, ALU.add).then_inc(s_gT, 1)

            def decay_rows(u, link):
                dve.wait_ge(s_fln, u + 1)
                link(v.scalar_tensor_tensor(out=lf[:, :], in0=gr[:, 1, :], scalar=0.0, in1=fln[:, :],
                                            op0=ALU.min, op1=ALU.subtract))
                link(v.tensor_tensor_scan(cum[:, :], ones_row[:, :], lf[:, :], 0.0, ALU.mult, ALU.add))
                link(v.tensor_tensor(av[:, :], gr[:, 0, :], cum[:, :], ALU.subtract))
                link(v.tensor_tensor_scan(mx[:, :], av[:, :], av[:, :], -3.0e38, ALU.max, ALU.max))
                v.tensor_tensor(mld[:, :], cum[:, :], mx[:, :], ALU.add).then_inc(s_mld, 1)
                v.tensor_copy(ah[:, :], av[:, :])
                link(v.tensor_scalar(mh[:, :], mx[:, :], -1.0, None, ALU.mult))
                v.tensor_tensor(al[:, :], av[:, :], ah[:, :].bitcast(F32), ALU.subtract)
                v.scalar_tensor_tensor(out=ml[:, :], in0=mx[:, :], scalar=-1.0, in1=mh[:, :].bitcast(F32),
                                       op0=ALU.mult, op1=ALU.subtract).then_inc(s_ah, 1)

            def decayed(u):
                after(dve, s_pv, u)
                for n, q in enumerate((1, 0)):
                    dve.wait_ge(s_qk, 2 * u + n + 1)
                    dve.wait_ge(s_d, 2 * u + n + 1)
                    v.scalar_tensor_tensor(out=ct[:, 2 * q:2 * q + 2, :].rearrange("p k n -> p (k n)"),
                                           in0=pa[:, q, :], scalar=QK_SCALE,
                                           in1=dm[:, 2 * q:2 * q + 2, :].rearrange("p k n -> p (k n)"),
                                           op0=ALU.mult, op1=ALU.mult).then_inc(s_ct, 1)

            def heads(u, link):
                dve.wait_ge(s_pv, u + 1)
                dve.wait_ge(s_enm, u + 1)
                hu = pa[:, 2:4, 0:2 * NH * V1].rearrange("p q (n d) -> p q n d", d=V1)
                link(v.scalar_tensor_tensor(out=den[:, :, :], in0=hu[:, :, :, DH], scalar=-1.0, in1=enm[:, :, :],
                                            op0=ALU.mult, op1=ALU.max))
                link(v.tensor_tensor(den[:, :, :], hu[:, :, :, DH], den[:, :, :], ALU.max))
                link(v.tensor_scalar(den[:, :, :], den[:, :, :], EPS_DEN, None, ALU.add))
                link(v.reciprocal(den[:, :, :], den[:, :, :]))
                for q in range(2):
                    ins = v.tensor_tensor(
                        hm[:, 2 * NH * q:2 * NH * q + 2 * NH, :].rearrange("p (b h) d -> p h b d", b=2),
                        hu[:, q, :, 0:DH].rearrange("p (h b) d -> p h b d", b=2),
                        den[:, q, :].rearrange("p (h b) -> p h b", b=2).unsqueeze(3).broadcast_to([P, NH, 2, DH]),
                        ALU.mult)
                ins.then_inc(s_hm, 1)
                dve.wait_ge(s_hm, u + 1)
                link(v.reduce_sum(hsum[:, :], hm[:, :, :], AX_X))
                link(v.tensor_scalar(hmean[:, :], hsum[:, :], -1.0 / DH, None, ALU.mult))
                v.tensor_tensor(hc[:, :, :], hm[:, :, :], hmean[:, :].unsqueeze(2).broadcast_to([P, C * NH, DH]),
                                ALU.add).then_inc(s_hc, 1)

            def head_variance(u, link):
                dve.wait_ge(s_hsq, u + 1)
                link(v.reduce_sum(hsum[:, :], hsq[:, :, :], AX_X))
                v.tensor_scalar(hvar[:, :], hsum[:, :], 1.0 / DH, EPS_HEAD, ALU.mult, ALU.add).then_inc(s_hvar, 1)

            def head_scale(u):
                dve.wait_ge(s_hrs, u + 1)
                v.tensor_tensor(ha[:, :, :], hc[:, :, :], hrs[:, :].unsqueeze(2).broadcast_to([P, C * NH, DH]),
                                ALU.mult).then_inc(s_ha, 1)

            def norm_stats(u, link):
                dve.wait_ge(s_x1, u + 1)
                statistics(x1, link)
                v.tensor_scalar(v2[:, :], vr[:, :], EPS_NORM, None, ALU.add).then_inc(s_v2, 1)

            def second_variance(u, link):
                dve.wait_ge(s_r1, u + 1)
                link(v.tensor_tensor(rr[:, :], r1[:, :], r1[:, :], ALU.mult))
                link(v.tensor_tensor(rr[:, :], rr[:, :], vr[:, :], ALU.mult))
                v.tensor_scalar(v2e[:, :], rr[:, :], EPS_NORM, None, ALU.add).then_inc(s_v2e, 1)
                v.scalar_tensor_tensor(out=nm[:, :], in0=mean[:, :], scalar=-1.0, in1=r1[:, :],
                                       op0=ALU.mult, op1=ALU.mult)
                v.tensor_scalar(p1[:, :], r1[:, :], 1.0, None, ALU.add).then_inc(s_nm, 1)

            def norm_apply(u, link):
                dve.wait_ge(s_r2, u + 1)
                link(v.tensor_tensor(rr[:, :], r1[:, :], r2[:, :], ALU.mult))
                after(dve, s_yT_ps, u)
                for c in range(C):
                    ins = v.tensor_scalar(yh[:, c, :], x1[:, c, :], mean[:, c:c + 1], rr[:, c:c + 1],
                                          ALU.subtract, ALU.mult)
                ins.then_inc(s_yh, 1)

            def norm_split(u, par, link):
                dve.wait_ge(s_xn, u + 1)
                link(v.tensor_copy(xnh[:, par, :], xn[:, par, :]))
                v.tensor_tensor(xnl[:, par, :], xn[:, par, :], xnh[:, par, :].bitcast(F32),
                                ALU.subtract).then_inc(s_xns, 1)

            def top_one(src, key, hot, top, link):
                def row(m):
                    return m[:, :].unsqueeze(2).broadcast_to([P, C, E])
                link(v.reduce_max(top[:, :], src[:, :, :], AX_X))
                link(v.tensor_tensor(key[:, :, :], src[:, :, :], row(top), ALU.is_ge))
                link(v.tensor_tensor(key[:, :, :], key[:, :, :], rev[:, :].unsqueeze(1).broadcast_to([P, C, E]),
                                     ALU.mult))
                link(v.reduce_max(kk[:, :], key[:, :, :], AX_X))
                link(v.tensor_tensor(hot[:, :, :], key[:, :, :], row(kk), ALU.is_equal))

            def first_expert(u, link):
                dve.wait_ge(s_lg_ps, u + 1)
                v.tensor_tensor(lg[:, :, :], pa[:, 3, 0:C * E].rearrange("p (c e) -> p c e", c=C),
                                bmg[:, :].unsqueeze(1).broadcast_to([P, C, E]), ALU.add).then_inc(s_lg, 1)
                dve.wait_ge(s_lg, u + 1)
                top_one(lg, k1, o1, m1, link)

            def second_expert(u, link):
                link(v.scalar_tensor_tensor(out=lg2[:, :, :], in0=o1[:, :, :], scalar=-3.0e38, in1=lg[:, :, :],
                                            op0=ALU.mult, op1=ALU.add))
                top_one(lg2, k2, o2, m2, link)
                v.tensor_tensor(dl[:, :], m1[:, :], m2[:, :], ALU.subtract).then_inc(s_dl, 1)

            def expert_weights(u, par, link):
                dve.wait_ge(s_th, u + 1)
                v.tensor_scalar(wa[:, :], th[:, :], 0.5, 0.5, ALU.mult, ALU.add)
                link(v.tensor_scalar(wb[:, :], th[:, :], -0.5, 0.5, ALU.mult, ALU.add))
                v.tensor_tensor(k1[:, :, :], o1[:, :, :], wa[:, :].unsqueeze(2).broadcast_to([P, C, E]), ALU.mult)
                link(v.tensor_tensor(k2[:, :, :], o2[:, :, :], wb[:, :].unsqueeze(2).broadcast_to([P, C, E]),
                                     ALU.mult))
                v.tensor_tensor(wr[:, par], k1[:, :, :], k2[:, :, :], ALU.add).then_inc(s_w, 1)

            def weights_t(u):
                dve.wait_ge(s_wT_ps, u + 1)
                v.tensor_copy(wT[:, :], pa[0:32, 3, WT_COL:WT_COL + P]).then_inc(s_wT, 1)

            def abel_bias(t, par):
                dve.wait_ge(s_y_ps, 10 * t + 1)
                after(dve, s_ab, t)
                v.tensor_tensor(abp[:, :, :], pb[:, 2, :].rearrange("p (c d) -> p c d", c=C),
                                bab[:, :].unsqueeze(1).broadcast_to([P, C, D]), ALU.add).then_inc(s_y, 1)
                dve.wait_ge(s_y_ps, 10 * t + 2)
                after(dve, s_db, t - 1)
                v.tensor_copy(acc[:, par], pb[:, 3, :].rearrange("p (c d) -> p c d", c=C)).then_inc(s_y, 1)

            def expert(t, par, e):
                dve.wait_ge(s_y, 10 * t + 2 + e)
                dve.wait_ge(s_y_ps, 10 * t + 3 + e)
                for c in range(C):
                    ins = v.scalar_tensor_tensor(out=acc[:, par, c, :], in0=pb[:, 2 + e % 2, D * c:D * c + D],
                                                 scalar=wr[:, par, c, e:e + 1], in1=acc[:, par, c, :],
                                                 op0=ALU.mult, op1=ALU.add)
                ins.then_inc(s_y, 1)

            def mix_gate(t, link):
                dve.wait_ge(s_zz, t + 1)
                v.reduce_sum(zs[:, :], zz[:, :, :], AX_X).then_inc(s_zs, 1)
                dve.wait_ge(s_zt, t + 1)
                link(v.tensor_scalar(gate[:, :], zt[:, :], 0.5, 0.5, ALU.mult, ALU.add))

            def mixed(t, par):
                dve.wait_ge(s_db, t + 1)
                after(dve, s_out[par], 8 * (t - par))
                for c in range(C):
                    ins = v.scalar_tensor_tensor(out=res[:, par, c, :], in0=diff[:, c, :], scalar=gate[:, c:c + 1],
                                                 in1=bab2[:, c, :], op0=ALU.mult, op1=ALU.add)
                ins.then_inc(s_res, 1)

            def body(t, par, attend=True, norm=True, experts=True, mix=True):
                w, u, other = t + 2, t + 1, 1 - par
                link_a = Links(dve, s_v_attend, VECTOR_ATTEND, w)
                link_n = Links(dve, s_v_norm, VECTOR_NORM, u)
                link_m = Links(dve, s_v_mix, VECTOR_MIX, t - 1)
                if attend:
                    query_stats(w, par, link_a)
                if norm:
                    heads(u, link_n)
                if attend:
                    query_norm(w, par)
                if experts:
                    abel_bias(t, par)
                if norm:
                    head_variance(u, link_n)
                if experts:
                    expert(t, par, 0)
                if attend:
                    context_t(w)
                if norm:
                    head_scale(u)
                if experts:
                    expert(t, par, 1)
                if attend:
                    gates_out(w)
                if norm:
                    norm_stats(u, link_n)
                if mix:
                    mix_gate(t - 1, link_m)
                if experts:
                    expert(t, par, 2)
                if norm:
                    second_variance(u, link_n)
                if experts:
                    expert(t, par, 3)
                if norm:
                    norm_apply(u, link_n)
                if attend:
                    decay_rows(w, link_a)
                if experts:
                    expert(t, par, 4)
                if mix:
                    mixed(t - 1, other)
                if norm:
                    norm_split(u, other, link_n)
                if experts:
                    expert(t, par, 5)
                if norm:
                    first_expert(u, link_n)
                if attend:
                    decayed(w)
                if experts:
                    expert(t, par, 6)
                if norm:
                    second_expert(u, link_n)
                    expert_weights(u, other, link_n)
                if experts:
                    expert(t, par, 7)
                if norm:
                    weights_t(u)
                for stage, link in ((attend, link_a), (norm, link_n), (mix, link_m)):
                    if stage:
                        link.end()

            body(-2, 0, norm=False, experts=False, mix=False)
            body(-1, 1, experts=False, mix=False)
            body(0, 0, mix=False)
            body(1, 1)
            with dve.Fori(1, TILES // 2 - 1) as i:
                body(2 * i, 0)
                body(2 * i + 1, 1)
            body(TILES - 2, 0, attend=False)
            body(TILES - 1, 1, attend=False, norm=False)
            mix_gate(TILES - 1, Links(dve, s_v_mix, VECTOR_MIX, TILES - 1))
            mixed(TILES - 1, 1)

        @block.tensor
        def _(pe):
            m = nc.tensor

            pe.wait_ge(s_gens, 16)
            pe.wait_ge(s_pool, 2)
            for n in range(NROT):
                ins = m.transpose(pa[:, 0, P * n:P * n + P], ga[:, n, :], ident[:, :])
            ins.then_inc(s_gat_ps, 1)
            for n in range(EXP_STEPS):
                pe.wait_ge(s_exp_t, n + 1)
                pe.wait_ge(s_exp_u, n + 1)
                for r in range(NROT):
                    t_, u_ = tm[:, n % 2, r, :], um[:, n % 2, r, :]
                    squaring = n >= DEGREE - 1
                    m.matmul(pa[:, 0, P * r:P * r + P], u_ if squaring else gat[:, r, :], t_, start=True, stop=True)
                    ins = m.matmul(pa[:, 1, P * r:P * r + P], t_ if squaring else ga[:, r, :], u_,
                                   start=True, stop=True)
                ins.then_inc(s_exp_ps, 1)
            fin = EXP_STEPS % 2
            pe.wait_ge(s_exp_t, EXP_STEPS + 1)
            pe.wait_ge(s_exp_u, EXP_STEPS + 1)
            m.matmul(pa[:, 2, 0:D], um[:, fin, 1, :], tm[:, fin, 2, :], start=True, stop=True).then_inc(s_rot_ps, 1)
            pe.wait_ge(s_rot, 1)
            m.matmul(pa[:, 3, 0:D], um[:, fin, 0, :], rot[:, 0, :], start=True, stop=True).then_inc(s_rot_ps, 1)
            pe.wait_ge(s_w2, 16)
            for n in range(E * HF):
                ins = m.transpose(pb[:, n // 4, P * (n % 4):P * (n % 4) + P], w2s[:, n, :], ident[:, :])
                if n % 4 == 3:
                    ins.then_inc(s_w2_ps, 1)
            pe.wait_ge(s_early, N_EARLY)
            m.transpose(pa[:, 0, 0:E * HF], b1row[:, :], ident[0:E * HF, 0:E * HF])
            m.transpose(pa[:, 0, 16:16 + E], b2s[:, :], ident[0:E, 0:E]).then_inc(s_b1_ps, 1)
            pe.wait_ge(s_rot, 2)
            for n in range(E * HF):
                pe.wait_ge(s_w2_sb, n // 4 + 1)
                ins = m.matmul(pb[:, n // 4, P * (n % 4):P * (n % 4) + P], w2t[:, n, :], rot[:, 1, :],
                               start=True, stop=True)
                if n % 4 == 3:
                    ins.then_inc(s_w2_ps, 1)
            pe.wait_ge(s_b1, 1)
            m.matmul(pa[0:32, 1, 0:D], b2t[:, :, :].rearrange("p c e -> p (c e)"), rot[:, 1, :],
                     start=True, stop=True).then_inc(s_b1_ps, 1)
            pe.wait_ge(s_ready_v, 1)
            pe.wait_ge(s_pool, POOL_STEPS)

            def transposes(u, par):
                pe.wait_ge(s_xq, u + 1)
                for c in range(C):
                    ins = m.transpose(pa[:, 0, P * c:P * c + P], xq[:, c, :], ident[:, :])
                ins.then_inc(s_xqT_ps, 1)
                pe.wait_ge(s_c[par], 32 * (u - par) + 64)
                for k in range(C):
                    ins = m.transpose(pa[:, 1, P * k:P * k + P], cs[:, par, k, :], ident[:, :])
                ins.then_inc(s_cT_ps, 1)

            def gates(u):
                pe.wait_ge(s_xqT, u + 1)
                pe.wait_ge(s_cT, u + 1)
                after(pe, s_hm, u)
                m.matmul(pa[0:2 * NH, 2, :], wgq[:, :], xqT[:, :].rearrange("d (q b n) -> d b q n", q=2, b=2),
                         start=True, stop=False)
                m.matmul(pa[0:2 * NH, 2, :], wgc[:, :], cT[:, :].rearrange("d (k b t) -> d b k t", k=C, b=2),
                         start=False, stop=True).then_inc(s_g_ps, 1)

            def scores(u):
                pe.wait_ge(s_xbd, u + 1)
                for q in (1, 0):
                    for g in range(2):
                        for b in range(2):
                            k = 2 * q + g
                            ins = m.matmul(pa[S * b:S * b + S, q, 256 * g:256 * g + 256],
                                           cT[:, P * k + S * b:P * k + S * b + S],
                                           xbd[:, 4 * q + 2 * b + g, :, :].rearrange("d h s -> d (h s)"),
                                           start=True, stop=True)
                    ins.then_inc(s_qk, 1)

            def exponents(u):
                pe.wait_ge(s_mld, u + 1)
                after(pe, s_lg, u)
                for g in range(2):
                    pick = ident[0:32, 0:32].rearrange("r (b h q g) -> r g q h b", h=NH, q=2, b=2)[:, g]
                    for q in range(2):
                        ins = m.matmul(pa[S * g:S * g + S, 2, 8 * q:8 * q + 8], mld[:, :], pick[:, q],
                                       start=True, stop=True)
                ins.then_inc(s_enm_ps, 1)
                pe.wait_ge(s_erow, 128 * u + 128)
                for q in (1, 0):
                    if q == 0:
                        pe.wait_ge(s_enm, u + 1)
                    for g in range(2):
                        k = 2 * q + g
                        o = pa[:, 2 + q, 256 * g:256 * g + 256]
                        m.matmul(o, el[:, k].rearrange("r b t -> r (b t)"),
                                 er[:, :, k, :], start=True, stop=False)
                        ins = m.matmul(o, ident_b[:, :], causal[:, :, :].rearrange("p h s -> p (h s)"),
                                       start=False, stop=True)
                    ins.then_inc(s_e, 1)

            def values(u):
                pe.wait_ge(s_vbd, u + 1)
                for n, q in enumerate((1, 0)):
                    pe.wait_ge(s_ct, 2 * u + n + 1)
                    for g in range(2):
                        k = 2 * q + g
                        for h in range(NH):
                            ins = m.matmul(pa[S * g:S * g + S, 2 + q, 2 * V1 * h:2 * V1 * h + 2 * V1],
                                           ct[:, k, S * h:S * h + S],
                                           vbd[:, k, h].rearrange("p b d -> p (b d)"), start=True, stop=True)
                ins.then_inc(s_pv, 1)

            def norm_t(u):
                pe.wait_ge(s_yh, u + 1)
                for c in range(C):
                    ins = m.transpose(pa[:, 3, P * c:P * c + P], yh[:, c, :], ident[:, :])
                ins.then_inc(s_yT_ps, 1)

            def logits(u, par):
                pe.wait_ge(s_xn, u + 1)
                for c in range(C):
                    ins = m.matmul(pa[:, 3, E * c:E * c + E], xn[:, par, P * c:P * c + P], wmg[:, :],
                                   start=True, stop=True)
                ins.then_inc(s_lg_ps, 1)

            def weights_t(t, par):
                pe.wait_ge(s_w, t + 1)
                m.transpose(pa[0:32, 3, WT_COL:WT_COL + P], wr[:, par].rearrange("p c e -> p (c e)"),
                            ident[:, :]).then_inc(s_wT_ps, 1)

            def abel(t, par):
                after(pe, s_y, 10 * t)
                for c in range(C):
                    ins = m.matmul(pb[:, 2, D * c:D * c + D], xn[:, par, P * c:P * c + P], wab[:, :],
                                   start=True, stop=True)
                ins.then_inc(s_y_ps, 1)

            def second_bias(t):
                pe.wait_ge(s_wT, t + 1)
                after(pe, s_y, 10 * t)
                m.matmul(pb[:, 3, :], wT[:, :], b2b[:, :, :].rearrange("r c d -> r (c d)"),
                         start=True, stop=True).then_inc(s_y_ps, 1)

            def hidden(t, par, e):
                if e == 0:
                    pe.wait_ge(s_xns, t + 1)
                for f in range(HF):
                    after(pe, s_h, 16 * t + max(0, 2 * e + f - 1))
                    cols = slice(P * f, P * f + P)
                    m.matmul(pb[:, f, :], w1l[:, e, cols], xnh[:, par, :], start=True, stop=False)
                    m.matmul(pb[:, f, :], w1h[:, e, cols], xnl[:, par, :], start=False, stop=False)
                    m.matmul(pb[:, f, :], w1h[:, e, cols], xnh[:, par, :], start=False,
                             stop=True).then_inc(s_h_ps, 1)

            def output(t, e):
                pe.wait_ge(s_y, 10 * t + 1 + e)
                pe.wait_ge(s_h, 16 * t + 2 * e + 2)
                for c in range(C):
                    for f in range(HF):
                        ins = m.matmul(pb[:, 2 + e % 2, D * c:D * c + D], hT[:, e % 2, f, P * c:P * c + P],
                                       w2r[:, HF * e + f, :], start=(f == 0), stop=(f == HF - 1))
                ins.then_inc(s_y_ps, 1)

            def body(t, par, attend=True, norm=True, experts=True):
                w, u, other = t + 2, t + 1, 1 - par
                if experts:
                    hidden(t, par, 0)
                    abel(t, par)
                    hidden(t, par, 1)
                    second_bias(t)
                    output(t, 0)
                if attend:
                    transposes(w, par)
                if experts:
                    hidden(t, par, 2)
                    output(t, 1)
                if attend:
                    gates(w)
                if experts:
                    hidden(t, par, 3)
                    output(t, 2)
                    hidden(t, par, 4)
                    output(t, 3)
                if attend:
                    scores(w)
                if experts:
                    hidden(t, par, 5)
                    output(t, 4)
                if norm:
                    norm_t(u)
                if experts:
                    hidden(t, par, 6)
                    output(t, 5)
                if norm:
                    logits(u, other)
                if experts:
                    hidden(t, par, 7)
                if attend:
                    exponents(w)
                if experts:
                    output(t, 6)
                if attend:
                    values(w)
                if experts:
                    output(t, 7)
                if norm:
                    weights_t(u, other)

            body(-2, 0, norm=False, experts=False)
            body(-1, 1, experts=False)
            body(0, 0)
            body(1, 1)
            with pe.Fori(1, TILES // 2 - 1) as i:
                body(2 * i, 0)
                body(2 * i + 1, 1)
            body(TILES - 2, 0, attend=False)
            body(TILES - 1, 1, attend=False, norm=False)


_INS = ['x', 'ctx_1024', 'L0_xattn_ig_kernel', 'L0_xattn_ig_bias', 'L0_xattn_fg_kernel', 'L0_xattn_fg_bias',
        'L0_xattn_outnorm_weight', 'L0_ffn_ln_gamma', 'L0_ffn_ln_beta', 'L0_ffn_abel_w', 'L0_ffn_abel_b',
        'L0_ffn_moe_gate_w', 'L0_ffn_moe_gate_b', 'L0_ffn_ew1', 'L0_ffn_eb1', 'L0_ffn_ew2', 'L0_ffn_eb2',
        'L0_ffn_gens', 'L0_ffn_gc_w', 'L0_ffn_gc_b']


def kernel(**inputs):
    import numpy as _np
    import concourse.bacc as _bacc
    from concourse import mybir as _mybir
    from concourse.bass_utils import run_bass_kernel_spmd as _run

    nc = _bacc.Bacc("TRN2", target_bir_lowering=False, num_devices=1)
    arrays, args = {}, []
    for name in _INS:
        a = _np.ascontiguousarray(inputs[name])
        arrays[f"in_{name}_dram"] = a
        args.append(nc.dram_tensor(f"in_{name}_dram", a.shape, _mybir.dt.from_np(a.dtype), kind="ExternalInput").ap())
    shape = inputs["x"].shape
    args.append(nc.dram_tensor("out_0_dram", shape, _mybir.dt.float32, kind="ExternalOutput").ap())
    build(nc, *args)
    r = _run(nc, [arrays], core_ids=[0])
    return r.results[0]["out_0_dram"]
```

```python
from contextlib import ExitStack

import concourse.bass as bass
from concourse import mybir

F32 = mybir.dt.float32
F32R = mybir.dt.float32r
ALU = mybir.AluOpType
ACT = mybir.ActivationFunctionType
AX_X = mybir.AxisListType.X

P = 128
S = 64
D = 128
NH = 4
DH = D // NH
SEQ = 8
C = 4
T = C * P
E = 8
HID = 256
HF = HID // P
WT_COL = 512 - P
GATE_ROW, EL_ROWS = S, S + 2 * NH + 4
V1 = DH + 1
EPS_NORM = 1e-5
EPS_HEAD = 1e-6
EPS_DEN = 1e-6
QK_SCALE = DH ** -0.5
NEG = -1e30
HALVINGS = 7
DEGREE = 8
NROT = 3

VECTOR_QUERY, VECTOR_ATTEND, VECTOR_NORM, VECTOR_ROUTE, VECTOR_MIX = 4, 5, 14, 14, 1
POOL_ATTEND, POOL_NORM, POOL_MIX = 1, 1, 1
POOL_EYES, POOL_XBD, POOL_STEPS = 3, 4, 15


JOBS, BIAS_JOB = 9, 5


def job_of(e):
    return e + (e > 4)


def job_bank(par, job):
    return 2 + (JOBS * par + job) % 2


class Links:

    def __init__(self, eng, sem, per_tile, tile):
        self.eng, self.sem, self.per_tile, self.base, self.n = eng, sem, per_tile, tile * per_tile, 0

    def __call__(self, ins):
        self.n += 1
        ins.then_inc(self.sem, 1)
        self.eng.wait_ge(self.sem, self.base + self.n)

    def end(self):
        assert self.n == self.per_tile, (self.n, self.per_tile)


def after(eng, sem, value):
    if not isinstance(value, int) or value > 0:
        eng.wait_ge(sem, value)


def build(nc, x, ctx_in, ig_w, ig_b, fg_w, fg_b, onorm_w, ln_g, ln_b, abel_w, abel_b, mg_w, mg_b,
          ew1, eb1, ew2, eb2, gens, gc_w, gc_b, out):
    TILES = x.shape[0] // SEQ
    assert TILES % 2 == 0 and TILES >= 6
    xf = x.rearrange("b s d -> (b s) d")
    outf = out.rearrange("b s d -> (b s) d")

    with ExitStack() as stack:
        def sb(name, shape, dt=F32):
            return stack.enter_context(nc.sbuf_tensor(name, shape, dt))

        def sem(name):
            return stack.enter_context(nc.semaphore(name))

        pa = stack.enter_context(nc.psum_tensor("pa", [P, 4, 512], F32))
        pb = stack.enter_context(nc.psum_tensor("pb", [P, 4, 512], F32))

        ident = sb("ident", [P, P])
        eye3 = sb("eye3", [P, NROT, P])
        ones_row = sb("ones_row", [32, S])
        mhalf = sb("mhalf", [P, 16])
        rev = sb("rev", [P, E])
        w1f = sb("w1f", [P, E, HID])
        w1h = sb("w1h", [P, E, HID], F32R)
        w1l = sb("w1l", [P, E, HID], F32R)
        w2s = sb("w2s", [P, E * HF, D])
        w2t = sb("w2t", [P, E * HF, P])
        w2r = sb("w2r", [P, E * HF, D])
        b1 = sb("b1", [P, E, HF])
        b1row = sb("b1row", [E * HF, P])
        b2s = sb("b2s", [E, D])
        b2t = sb("b2t", [P, C, E])
        b2m = sb("b2m", [32, C])
        b2b = sb("b2b", [32, C, D])
        b2p = sb("b2p", [96, C, D], F32R)
        wabg = sb("wabg", [P, D + E])
        bab = sb("bab", [P, D])
        bmg = sb("bmg", [P, E])
        wgr = sb("wgr", [P, 3, 2, NH])
        wgq = sb("wgq", [P, 2 * NH])
        wgc = sb("wgc", [P, 2 * NH])
        bg = sb("bg", [2 * NH, 1])
        lng = sb("lng", [P, 1])
        lnb = sb("lnb", [P, 1])
        onw = sb("onw", [P, D])
        gc1 = sb("gc1", [P, D])
        gc2 = sb("gc2", [P, D])
        gcb = sb("gcb", [P, 1])
        hgcb = sb("hgcb", [P, 1])
        ga = sb("ga", [P, NROT, P])
        gat = sb("gat", [P, NROT, P])
        tm = sb("tm", [P, 2, NROT, P])
        um = sb("um", [P, 2, NROT, P])
        rot = sb("rot", [P, 2, D])

        xs = sb("xs", [P, 2, C, D])
        cs = sb("cs", [P, 2, C, D])
        st = sb("st", [P, C, 6])
        ssum = sb("ssum", [P, C])
        sdif = sb("sdif", [P, C])
        ssq = sb("ssq", [P, C])
        mean = sb("mean", [P, C])
        vr = sb("vr", [P, C])
        var = sb("var", [P, C])
        rstd = sb("rstd", [P, C])
        carrier = sb("carrier", [1, 1])
        xq = sb("xq", [P, C, D])
        xqT = sb("xqT", [P, T])
        cT = sb("cT", [P, T])
        xbd = sb("xbd", [P, SEQ, NH, S])
        vbd = sb("vbd", [P, C, NH, 2, V1])
        gT = sb("gT", [2 * NH, T])
        gr = sb("gr", [32, 2, S])
        fabs = sb("fabs", [32, S])
        fexp = sb("fexp", [32, S])
        fln = sb("fln", [32, S])
        lf = sb("lf", [32, S])
        cum = sb("cum", [32, S])
        av = sb("av", [32, S])
        mx = sb("mx", [32, S])
        mld = sb("mld", [32, S])
        gs = sb("gs", [64, S], F32R)
        ms = sb("ms", [64, S], F32R)
        elc = sb("elc", [EL_ROWS, C, 2, S])
        erc = sb("erc", [EL_ROWS, NH, C, S])
        el = sb("el", [EL_ROWS, C, 2, S], F32R)
        er = sb("er", [EL_ROWS, NH, C, S], F32R)
        dm = sb("dm", [P, C, NH * S])
        ct = sb("ct", [P, C, NH * S])
        enm = sb("enm", [P, 2, 2 * NH])
        den = sb("den", [P, 2, 2 * NH])
        hm = sb("hm", [P, C * NH, DH])
        hsum = sb("hsum", [P, C * NH])
        hmean = sb("hmean", [P, C * NH])
        hc = sb("hc", [P, C * NH, DH])
        hsq = sb("hsq", [P, C * NH, DH])
        hvar = sb("hvar", [P, C * NH])
        hrs = sb("hrs", [P, C * NH])
        ha = sb("ha", [P, C * NH, DH])
        hw = sb("hw", [P, C, D])
        x1 = sb("x1", [P, C, D])
        v2 = sb("v2", [P, C])
        v2e = sb("v2e", [P, C])
        r1 = sb("r1", [P, C])
        r2 = sb("r2", [P, C])
        rr = sb("rr", [P, C])
        p1 = sb("p1", [P, C])
        nm = sb("nm", [P, C])
        yh = sb("yh", [P, C, D])
        base = sb("base", [P, 2, C, D])
        xn = sb("xn", [P, 2, T])
        xnh = sb("xnh", [P, 2, T], F32R)
        xnl = sb("xnl", [P, 2, T], F32R)
        lg = sb("lg", [P, C, E])
        lg2 = sb("lg2", [P, C, E])
        k1 = sb("k1", [P, C, E])
        k2 = sb("k2", [P, C, E])
        o1 = sb("o1", [P, C, E])
        o2 = sb("o2", [P, C, E])
        m1 = sb("m1", [P, C])
        m2 = sb("m2", [P, C])
        kk = sb("kk", [P, C])
        dl = sb("dl", [P, C])
        th = sb("th", [P, C])
        wa = sb("wa", [P, C])
        wb = sb("wb", [P, C])
        wr = sb("wr", [P, 2, C, E])

        hT = sb("hT", [P, 2, HF, T])
        wT = sb("wT", [96, P], F32R)
        acc = sb("acc", [P, 2, C, D])
        abp = sb("abp", [P, C, D])
        ab = sb("ab", [P, 2, C, D])
        z1 = sb("z1", [P, C, D])
        z2 = sb("z2", [P, C, D])
        zz = sb("zz", [P, C, D])
        zs = sb("zs", [P, C])
        zt = sb("zt", [P, C])
        gate = sb("gate", [P, C])
        diff = sb("diff", [P, C, D])
        bab2 = sb("bab2", [P, C, D])
        res = sb("res", [P, 2, C, D])

        s_early = sem("s_early")
        s_gate_w = sem("s_gate_w")
        s_gates_v = sem("s_gates_v")
        s_w1h = sem("s_w1h")
        s_w1l = sem("s_w1l")
        s_w1 = sem("s_w1")
        s_w2 = sem("s_w2")
        s_gens = sem("s_gens")
        s_pool = sem("s_pool")
        s_setup_v = sem("s_setup_v")
        s_ready_v = sem("s_ready_v")
        s_gat_ps = sem("s_gat_ps")
        s_exp_ps = sem("s_exp_ps")
        s_exp_t = sem("s_exp_t")
        s_exp_u = sem("s_exp_u")
        s_rot_ps = sem("s_rot_ps")
        s_rot = sem("s_rot")
        s_w2_ps = sem("s_w2_ps")
        s_w2t = sem("s_w2t")
        s_w2r = sem("s_w2r")
        s_b1_ps = sem("s_b1_ps")
        s_b1 = sem("s_b1")
        s_b2b = sem("s_b2b")
        s_b2h = sem("s_b2h")
        s_b2l = sem("s_b2l")
        s_x = [sem("s_x0"), sem("s_x1")]
        s_c = [sem("s_c0"), sem("s_c1")]
        s_v_query = sem("s_v_query")
        s_v_attend = sem("s_v_attend")
        s_v_route = sem("s_v_route")
        s_v_norm = sem("s_v_norm")
        s_v_mix = sem("s_v_mix")
        s_g_attend = sem("s_g_attend")
        s_g_norm = sem("s_g_norm")
        s_g_mix = sem("s_g_mix")
        s_xvar = sem("s_xvar")
        s_xrstd = sem("s_xrstd")
        s_xq = sem("s_xq")
        s_xqT_ps = sem("s_xqT_ps")
        s_xqT = sem("s_xqT")
        s_cT_ps = sem("s_cT_ps")
        s_cT = sem("s_cT")
        s_xbd = sem("s_xbd")
        s_vbd = sem("s_vbd")
        s_g_ps = sem("s_g_ps")
        s_gT = sem("s_gT")
        s_gr = sem("s_gr")
        s_fabs = sem("s_fabs")
        s_fexp = sem("s_fexp")
        s_fln = sem("s_fln")
        s_mld = sem("s_mld")
        s_gs = sem("s_gs")
        s_erow = sem("s_erow")
        s_qk = sem("s_qk")
        s_e = sem("s_e")
        s_d = sem("s_d")
        s_ct = sem("s_ct")
        s_pv = sem("s_pv")
        s_enm_ps = sem("s_enm_ps")
        s_enm = sem("s_enm")
        s_hm = sem("s_hm")
        s_hc = sem("s_hc")
        s_hsq = sem("s_hsq")
        s_hvar = sem("s_hvar")
        s_hrs = sem("s_hrs")
        s_ha = sem("s_ha")
        s_x1 = sem("s_x1_")
        s_v2 = sem("s_v2")
        s_r1 = sem("s_r1")
        s_v2e = sem("s_v2e")
        s_r2 = sem("s_r2")
        s_yh = sem("s_yh")
        s_base = sem("s_base")
        s_nm = sem("s_nm")
        s_yT_ps = sem("s_yT_ps")
        s_xn = sem("s_xn")
        s_xns = sem("s_xns")
        s_lg_ps = sem("s_lg_ps")
        s_lg = sem("s_lg")
        s_abp = sem("s_abp")
        s_dl = sem("s_dl")
        s_th = sem("s_th")
        s_w = sem("s_w")
        s_h_ps = sem("s_h_ps")
        s_h = sem("s_h")
        s_y_ps = sem("s_y_ps")
        s_y = sem("s_y")
        s_ab = sem("s_ab")
        s_wT_ps = sem("s_wT_ps")
        s_wTh = sem("s_wTh")
        s_wT = sem("s_wT")
        s_zz = sem("s_zz")
        s_zs = sem("s_zs")
        s_zt = sem("s_zt")
        s_db = sem("s_db")
        s_res = sem("s_res")
        s_out = [sem("s_out0"), sem("s_out1")]

        EXP_STEPS = DEGREE - 1 + HALVINGS
        N_EARLY = 16 * 12

        block = stack.enter_context(nc.Block())

        @block.sync
        def _(sp):
            def load(u, par, first=False):
                row, first_seq = sp.snap(u * T), sp.snap(u * SEQ)
                if not first:
                    sp.wait_ge(s_x1, u - 1)
                    sp.wait_ge(s_cT_ps, u - 1)
                    sp.wait_ge(s_vbd, u - 1)
                sp.dma_start(xs[:, par], xf[bass.ds(row, T), :].rearrange("(c p) d -> p c d", p=P)
                             ).then_inc(s_x[par], 16)
                src = ctx_in[bass.ds(first_seq, SEQ), :, :].rearrange("(q b g) t d -> b q t g d", q=2, b=2)
                for b in range(2):
                    for q in range(2):
                        sp.dma_start(cs[S * b:S * b + S, par, 2 * q:2 * q + 2], src[b, q]).then_inc(s_c[par], 16)

            def gate_rows(u):
                sp.wait_ge(s_gT, u + 1)
                for j in range(2):
                    sp.dma_start(gr[:, j, :], gT[NH * j:NH * j + NH, :].rearrange("h (n t) -> h n t", n=SEQ)
                                 ).then_inc(s_gr, 16)

            def decay_rows(u):
                sp.wait_ge(s_gs, u + 1)
                sp.dma_start(el[GATE_ROW:GATE_ROW + 2 * NH].bitcast(F32), gs[:, :].bitcast(F32)).then_inc(s_erow, 16)
                for b in range(2):
                    sp.dma_start(er[GATE_ROW + 2 * NH + b:EL_ROWS:2].bitcast(F32), ms[b::2, :].bitcast(F32)
                                 ).then_inc(s_erow, 16)

            def store(t, par):
                row = sp.snap(t * T)
                sp.wait_ge(s_res, t + 1)
                sp.dma_start(outf[bass.ds(row, T), :].rearrange("(c p) d -> p c d", p=P), res[:, par]
                             ).then_inc(s_out[par], 16)

            def bcast(row, n):
                return row.rearrange("(a n) -> a n", a=1).broadcast_to([P, n])

            load(0, 0, True)
            sp.dma_start(ga[:, :, :], gens.rearrange("r i j -> i r j")).then_inc(s_gens, 16)
            for j, w in enumerate((ig_w, fg_w)):
                sp.dma_start(wgr[:, :, j, :], w.rearrange("(r d) h -> d r h", r=3)).then_inc(s_gate_w, 16)
            sp.dma_start(bg[0:NH, :], ig_b.rearrange("(h a) -> h a", a=1)).then_inc(s_gate_w, 16)
            sp.dma_start(bg[NH:2 * NH, :], fg_b.rearrange("(h a) -> h a", a=1)).then_inc(s_gate_w, 16)
            load(1, 1, True)
            sp.dma_start(w2s[:, :, :], ew2.rearrange("e (f p) d -> p (e f) d", f=HF)).then_inc(s_w2, 16)
            sp.dma_start(w1f[:, :, :], ew1.rearrange("e d h -> d e h")).then_inc(s_w1, 16)
            sp.dma_start(onw[:, :], bcast(onorm_w.rearrange("h d -> (h d)"), D)).then_inc(s_early, 16)
            sp.dma_start(lng[:, :], ln_g.rearrange("(d a) -> d a", a=1)).then_inc(s_early, 16)
            sp.dma_start(lnb[:, :], ln_b.rearrange("(d a) -> d a", a=1)).then_inc(s_early, 16)
            sp.dma_start(wabg[:, D:D + E], mg_w).then_inc(s_early, 16)
            sp.dma_start(bmg[:, :], bcast(mg_b, E)).then_inc(s_early, 16)
            sp.dma_start(wabg[:, 0:D], abel_w).then_inc(s_early, 16)
            sp.dma_start(bab[:, :], bcast(abel_b, D)).then_inc(s_early, 16)
            sp.dma_start(b1row[:, :], eb1.rearrange("e (f p) -> (e f) p", f=HF)).then_inc(s_early, 16)
            sp.dma_start(b2s[:, :], eb2).then_inc(s_early, 16)
            gcv = gc_w.rearrange("d a -> (d a)")
            sp.dma_start(gc1[:, :], bcast(gcv[0:D], D)).then_inc(s_early, 16)
            sp.dma_start(gc2[:, :], bcast(gcv[D:2 * D], D)).then_inc(s_early, 16)
            sp.dma_start(gcb[:, :], bcast(gc_b, 1)).then_inc(s_early, 16)
            gate_rows(0)
            decay_rows(0)
            gate_rows(1)
            decay_rows(1)

            def body(t, par, stored=True):
                load(t + 2, par)
                if stored:
                    store(t - 2, par)
                gate_rows(t + 2)
                decay_rows(t + 2)

            body(0, 0, stored=False)
            body(1, 1, stored=False)
            with sp.Fori(1, TILES // 2 - 1) as i:
                body(2 * i, 0)
                body(2 * i + 1, 1)
            for t in range(TILES - 4, TILES):
                store(t, t % 2)
            for par in range(2):
                sp.wait_ge(s_out[par], 16 * (TILES // 2))

        @block.gpsimd
        def _(pool):
            g = nc.gpsimd
            steps = 0

            def step(ins):
                nonlocal steps
                steps += 1
                ins.then_inc(s_pool, 1)
                pool.wait_ge(s_pool, steps)

            step(g.memset(ident[:, :], 0.0))
            step(g.affine_select(out=ident[:, :], in_=ident[:, :], compare_op=ALU.not_equal, fill=1.0,
                                 base=0, pattern=[[-1, P]], channel_multiplier=1))
            g.memset(mhalf[:, :], -0.5)
            for n in range(NROT):
                ins = g.tensor_copy(eye3[:, n, :], ident[:, :])
            step(ins)
            assert steps == POOL_EYES
            pool.wait_ge(s_xvar, 1)
            g.tensor_tensor(rstd[:, :], var[:, :], mhalf[:, 0:C], ALU.pow).then_inc(s_xrstd, 1)
            step(g.memset(xbd[:, :, :, :], 0.0))
            assert steps == POOL_XBD
            g.memset(ones_row[:, :], 1.0)
            for e in range(E):
                g.memset(rev[:, e:e + 1], float(E - e))
            g.memset(elc[:, :, :, :], 0.0)
            g.memset(erc[:, :, :, :], 0.0)
            g.memset(b2m[:, :], 1.0)
            step(g.memset(vbd[:, :, :, :, :], 0.0))
            step(g.affine_select(out=elc[0:S], in_=elc[0:S], compare_op=ALU.not_equal, fill=1.0, base=0,
                                 pattern=[[0, C], [0, 2], [-1, S]], channel_multiplier=1))
            step(g.affine_select(out=erc[0:S], in_=erc[0:S], compare_op=ALU.is_ge, fill=NEG, base=0,
                                 pattern=[[0, NH], [0, C], [1, S]], channel_multiplier=-1))
            for n in range(2):
                step(g.affine_select(out=erc[GATE_ROW:], in_=erc[GATE_ROW:], compare_op=ALU.not_equal,
                                     fill=1.0, base=-NH * n, pattern=[[-1, NH], [0, C], [0, S]],
                                     channel_multiplier=1))
                step(g.affine_select(out=elc[GATE_ROW:], in_=elc[GATE_ROW:], compare_op=ALU.not_equal,
                                     fill=1.0, base=-2 * NH - 2 * n, pattern=[[0, C], [-1, 2], [0, S]],
                                     channel_multiplier=1))
            step(g.affine_select(out=b2m[:, :], in_=b2m[:, :], compare_op=ALU.is_ge, fill=0.0,
                                 base=0, pattern=[[-E, C]], channel_multiplier=1))
            step(g.affine_select(out=b2m[:, :], in_=b2m[:, :], compare_op=ALU.is_ge, fill=0.0,
                                 base=E - 1, pattern=[[E, C]], channel_multiplier=-1))
            for b in range(2):
                step(g.memset(vbd[S * b:S * b + S, :, :, b, DH:V1], 1.0))

            def carry():
                g.tensor_tensor(carrier[:, :], mhalf[0:1, 0:1], mhalf[0:1, 0:1], ALU.mult)

            def query_rstd(u):
                pool.wait_ge(s_xvar, u + 1)
                g.tensor_tensor(rstd[:, :], var[:, :], mhalf[:, 0:C], ALU.pow).then_inc(s_xrstd, 1)

            def value_copy(par, b):
                return (vbd[S * b:S * b + S, :, :, b, 0:DH],
                        cs[S * b:S * b + S, par].rearrange("t k (h d) -> t k h d", h=NH))

            def values_first(u, par, link):
                pool.wait_ge(s_c[par], 32 * (u - par) + 64)
                after(pool, s_pv, u)
                carry()
                link(g.tensor_copy(*value_copy(par, 0)))

            def values_second(u, par):
                carry()
                g.tensor_copy(*value_copy(par, 1)).then_inc(s_vbd, 1)
                pool.wait_ge(s_vbd, u + 1)

            def head_rstd(u):
                pool.wait_ge(s_hvar, u + 1)
                g.tensor_tensor(hrs[:, :], hvar[:, :], mhalf[:, :], ALU.pow).then_inc(s_hrs, 1)

            def residual(u, par, link):
                pool.wait_ge(s_ha, u + 1)
                link(g.tensor_tensor(hw[:, :, :], ha[:, :, :].rearrange("p (c h) d -> p c (h d)", c=C),
                                     onw[:, :].unsqueeze(1).broadcast_to([P, C, D]), ALU.mult))
                g.tensor_tensor(x1[:, :, :], hw[:, :, :], xs[:, par], ALU.add).then_inc(s_x1, 1)

            def norm_rstd(u):
                pool.wait_ge(s_v2, u + 1)
                g.tensor_tensor(r1[:, :], v2[:, :], mhalf[:, 0:C], ALU.pow).then_inc(s_r1, 1)
                pool.wait_ge(s_v2e, u + 1)
                g.tensor_tensor(r2[:, :], v2e[:, :], mhalf[:, 0:C], ALU.pow).then_inc(s_r2, 1)

            def base_sum(u, par):
                after(pool, s_db, u - 1)
                pool.wait_ge(s_nm, u + 1)
                carry()
                for c in range(C):
                    ins = g.tensor_scalar(base[:, par, c, :], x1[:, c, :], p1[:, c:c + 1], nm[:, c:c + 1],
                                          ALU.mult, ALU.add)
                ins.then_inc(s_base, 1)
                pool.wait_ge(s_base, u + 1)

            def gate_abel(t, par):
                after(pool, s_zz, t)
                pool.wait_ge(s_ab, t + 1)
                g.tensor_tensor(z1[:, :, :], ab[:, par], gc1[:, :].unsqueeze(1).broadcast_to([P, C, D]), ALU.mult)

            def gate_sum(t, par, link):
                pool.wait_ge(s_y, JOBS * (t + 1))
                link(g.tensor_tensor(z2[:, :, :], acc[:, par],
                                     gc2[:, :].unsqueeze(1).broadcast_to([P, C, D]), ALU.mult))
                g.tensor_tensor(zz[:, :, :], z1[:, :, :], z2[:, :, :], ALU.add).then_inc(s_zz, 1)

            def mix_rest(par):
                return g.tensor_tensor(bab2[:, :, :], base[:, par], ab[:, par], ALU.add)

            def mix_difference(par):
                return g.tensor_tensor(diff[:, :, :], acc[:, par], ab[:, par], ALU.subtract)

            def mix_terms(t, par):
                mix_difference(par)
                mix_rest(par).then_inc(s_db, 1)

            def body(t, par, attend=True, norm=True, mix=True):
                other = 1 - par
                link_a = Links(pool, s_g_attend, POOL_ATTEND, t + 2)
                link_n = Links(pool, s_g_norm, POOL_NORM, t + 1)
                link_m = Links(pool, s_g_mix, POOL_MIX, t - 1)
                if attend:
                    query_rstd(t + 2)
                if mix:
                    gate_sum(t - 1, other, link_m)
                    mix_terms(t - 1, other)
                if norm:
                    head_rstd(t + 1)
                    residual(t + 1, other, link_n)
                if attend:
                    values_first(t + 2, par, link_a)
                if norm:
                    norm_rstd(t + 1)
                if attend:
                    pool.wait_ge(s_r2, t + 2)
                    values_second(t + 2, par)
                if norm:
                    base_sum(t + 1, other)
                gate_abel(t, par)
                for stage, link in ((attend, link_a), (norm, link_n), (mix, link_m)):
                    if stage:
                        link.end()

            assert steps == POOL_STEPS
            values_first(0, 0, Links(pool, s_g_attend, POOL_ATTEND, 0))
            values_second(0, 0)
            query_rstd(1)
            pool.wait_ge(s_w1h, 1)
            g.tensor_tensor(w1l[:, :, :], w1f[:, :, :], w1h[:, :, :].bitcast(F32), ALU.subtract
                            ).then_inc(s_w1l, 1)
            pool.wait_ge(s_early, N_EARLY)
            link_n = Links(pool, s_g_norm, POOL_NORM, 0)
            head_rstd(0)
            residual(0, 0, link_n)
            norm_rstd(0)
            values_first(1, 1, Links(pool, s_g_attend, POOL_ATTEND, 1))
            values_second(1, 1)
            base_sum(0, 0)
            body(0, 0, mix=False)
            body(1, 1)
            with pool.Fori(1, TILES // 2 - 1) as i:
                body(2 * i, 0)
                body(2 * i + 1, 1)
            body(TILES - 2, 0, attend=False)
            body(TILES - 1, 1, attend=False, norm=False)
            link_m = Links(pool, s_g_mix, POOL_MIX, TILES - 1)
            pool.wait_ge(s_res, TILES - 1)
            mix_rest(1)
            gate_sum(TILES - 1, 1, link_m)
            mix_difference(1).then_inc(s_db, 1)

        @block.scalar
        def _(act):
            a = nc.scalar

            def gelu(t, e):
                for f in range(HF):
                    act.wait_ge(s_h_ps, 16 * t + 2 * e + f + 1)
                    if e >= 2:
                        act.wait_ge(s_y_ps, JOBS * t + job_of(e - 2) + 1)
                    else:
                        after(act, s_y_ps, JOBS * (t - 1) + job_of(e + 6) + 1)
                    a.activation(hT[:, e % 2, f, :], pb[:, f, :], ACT.Gelu, bias=b1[:, e, f:f + 1]).then_inc(s_h, 1)

            def gelu_abel(t, par):
                act.wait_ge(s_abp, t + 1)
                after(act, s_db, t - 1)
                a.activation(ab[:, par], abp[:, :, :], ACT.Gelu).then_inc(s_ab, 1)

            def query_t(u):
                act.wait_ge(s_xqT_ps, u + 1)
                after(act, s_g_ps, u)
                a.activation(xqT[:, :], pa[:, 0, :], ACT.Copy).then_inc(s_xqT, 1)

            def query_heads(u):
                act.wait_ge(s_xqT, u + 1)
                after(act, s_qk, 2 * u)
                for h in range(NH):
                    rows = slice(DH * h, DH * h + DH)
                    ins = a.activation(xbd[rows, :, h, :], pa[rows, 0, :].rearrange("d (b s) -> d b s", b=SEQ),
                                       ACT.Copy)
                ins.then_inc(s_xbd, 1)

            def gates_out(u):
                act.wait_ge(s_g_ps, u + 1)
                a.activation(gT[:, :], pa[0:2 * NH, 1, :], ACT.Identity, bias=bg[:, 0:1]).then_inc(s_gT, 1)

            def head_squares(u):
                act.wait_ge(s_hc, u + 1)
                a.activation(hsq[:, :, :], hc[:, :, :], ACT.Square).then_inc(s_hsq, 1)

            def log_sigmoid(u):
                act.wait_ge(s_gr, 32 * u + 32)
                a.activation(fabs[:, :], gr[:, 1, :], ACT.Abs).then_inc(s_fabs, 1)
                act.wait_ge(s_fabs, u + 1)
                a.activation(fexp[:, :], fabs[:, :], ACT.Exp, scale=-1.0).then_inc(s_fexp, 1)
                act.wait_ge(s_fexp, u + 1)
                a.activation(fln[:, :], fexp[:, :], ACT.Ln, bias=1.0).then_inc(s_fln, 1)

            def decay(u):
                act.wait_ge(s_enm_ps, u + 1)
                a.activation(enm[:, :, :].rearrange("p q n -> p (q n)"), pa[:, 2, 0:16], ACT.Exp,
                             scale=-1.0).then_inc(s_enm, 1)
                for n, q in enumerate((1, 0)):
                    act.wait_ge(s_e, 2 * u + n + 1)
                    a.activation(dm[:, 2 * q:2 * q + 2, :].rearrange("p k n -> p (k n)"), pa[:, 2 + q, :],
                                 ACT.Exp).then_inc(s_d, 1)

            def norm_t(u, par):
                act.wait_ge(s_yT_ps, u + 1)
                a.activation(xn[:, par, :], pa[:, 0, :], ACT.Identity, bias=lnb[:, 0:1],
                             scale=lng[:, 0:1]).then_inc(s_xn, 1)

            def route(u):
                act.wait_ge(s_dl, u + 1)
                a.activation(th[:, :], dl[:, :], ACT.Tanh, scale=0.5).then_inc(s_th, 1)

            def mix_gate(t):
                act.wait_ge(s_zs, t + 1)
                a.activation(zt[:, :], zs[:, :], ACT.Tanh, bias=hgcb[:, 0:1], scale=0.5).then_inc(s_zt, 1)

            def exp_square(n):
                act.wait_ge(s_exp_ps, n + 1)
                a.activation(um[:, (n + 1) % 2, :, :].rearrange("p r n -> p (r n)"), pb[:, 1, 0:NROT * P],
                             ACT.Copy).then_inc(s_exp_u, 1)

            def body(t, par, attend=True, norm=True, mix=True, routed=True):
                gelu(t, 0)
                if attend:
                    query_t(t + 2)
                    query_heads(t + 2)
                if routed:
                    route(t)
                gelu(t, 1)
                if attend:
                    gates_out(t + 2)
                gelu(t, 2)
                if norm:
                    head_squares(t + 1)
                gelu(t, 3)
                if attend:
                    log_sigmoid(t + 2)
                gelu(t, 4)
                gelu(t, 5)
                if mix:
                    mix_gate(t - 1)
                gelu_abel(t, par)
                gelu(t, 6)
                if attend:
                    decay(t + 2)
                gelu(t, 7)
                if norm:
                    norm_t(t + 1, 1 - par)

            def second_weights(bank, n, dest, done):
                act.wait_ge(s_w2_ps, n + 1)
                a.activation(dest[:, 4 * (n % 4):4 * (n % 4) + 4, :].rearrange("p r n -> p (r n)"), pb[:, bank, :],
                             ACT.Copy).then_inc(done, 1)

            query_t(0)
            act.wait_ge(s_gate_w, 64)
            gates_out(0)
            act.wait_ge(s_pool, POOL_XBD)
            query_heads(0)
            log_sigmoid(0)
            second_weights(2, 0, w2t, s_w2t)
            second_weights(3, 1, w2t, s_w2t)
            decay(0)
            act.wait_ge(s_w1, 16)
            a.activation(w1h[:, :, :], w1f[:, :, :], ACT.Copy).then_inc(s_w1h, 1)
            query_t(1)
            gates_out(1)
            head_squares(0)
            query_heads(1)
            exp_square(7)
            second_weights(2, 2, w2t, s_w2t)
            second_weights(3, 3, w2t, s_w2t)
            log_sigmoid(1)
            exp_square(8)
            exp_square(9)
            act.wait_ge(s_early, N_EARLY)
            norm_t(0, 0)
            for n in (10, 11, 12, 13):
                exp_square(n)
            decay(1)
            route(0)
            second_weights(2, 6, w2r, s_w2r)
            second_weights(3, 7, w2r, s_w2r)
            act.wait_ge(s_b2b, 1)
            a.activation(b2p[0:32, :, :], b2b[:, :, :], ACT.Copy).then_inc(s_b2h, 1)
            a.activation(b2p[32:64, :, :], b2b[:, :, :], ACT.Copy).then_inc(s_b2h, 1)

            act.wait_ge(s_b1, 1)
            body(0, 0, mix=False, routed=False)
            body(1, 1)
            with act.Fori(1, TILES // 2 - 1) as i:
                body(2 * i, 0)
                body(2 * i + 1, 1)
            body(TILES - 2, 0, attend=False)
            body(TILES - 1, 1, attend=False, norm=False)
            mix_gate(TILES - 1)

        @block.vector
        def _(dve):
            v = nc.vector
            g3 = "p r n -> p (r n)"
            steps = 0

            def step(ins):
                nonlocal steps
                steps += 1
                ins.then_inc(s_setup_v, 1)
                dve.wait_ge(s_setup_v, steps)

            def exp_start():
                dve.wait_ge(s_gens, 16)
                dve.wait_ge(s_pool, POOL_EYES)
                dve.wait_ge(s_gat_ps, 1)
                v.tensor_scalar(gat[:, :, :].rearrange(g3), pb[:, 0, 0:NROT * P], 2.0 ** -HALVINGS, None, ALU.mult)
                step(v.tensor_scalar(ga[:, :, :], ga[:, :, :], 2.0 ** -HALVINGS, None, ALU.mult))
                v.scalar_tensor_tensor(out=tm[:, 0], in0=ga[:, :, :], scalar=1.0 / DEGREE, in1=eye3[:, :, :],
                                       op0=ALU.mult, op1=ALU.add).then_inc(s_exp_t, 1)
                v.scalar_tensor_tensor(out=um[:, 0], in0=gat[:, :, :], scalar=1.0 / DEGREE, in1=eye3[:, :, :],
                                       op0=ALU.mult, op1=ALU.add).then_inc(s_exp_u, 1)

            def exp_step(n):
                dve.wait_ge(s_exp_ps, n + 1)
                tn = tm[:, (n + 1) % 2, :, :].rearrange(g3)
                un = um[:, (n + 1) % 2, :, :].rearrange(g3)
                k = DEGREE - 1 - n
                if k > 0:
                    v.scalar_tensor_tensor(out=tn, in0=pb[:, 0, 0:NROT * P], scalar=1.0 / k,
                                           in1=eye3[:, :, :].rearrange(g3), op0=ALU.mult,
                                           op1=ALU.add).then_inc(s_exp_t, 1)
                    v.scalar_tensor_tensor(out=un, in0=pb[:, 1, 0:NROT * P], scalar=1.0 / k,
                                           in1=eye3[:, :, :].rearrange(g3), op0=ALU.mult,
                                           op1=ALU.add).then_inc(s_exp_u, 1)
                else:
                    v.tensor_copy(tn, pb[:, 0, 0:NROT * P]).then_inc(s_exp_t, 1)

            def rotation(n):
                dve.wait_ge(s_rot_ps, n + 1)
                v.tensor_copy(rot[:, n, :], pb[:, 2 + n, 0:D]).then_inc(s_rot, 1)

            def biases_transposed():
                dve.wait_ge(s_b1_ps, 1)
                v.tensor_copy(b1[:, :, :].rearrange("p e f -> p (e f)"), pb[:, 2, 0:E * HF])
                v.tensor_copy(b2t[:, :, :], pb[:, 2, E * HF:E * HF + E].unsqueeze(1).broadcast_to([P, C, E])
                              ).then_inc(s_b1, 1)

            def expert_weights_turned():
                dve.wait_ge(s_b1_ps, 2)
                v.tensor_tensor(b2b[:, :, :], pa[0:32, 1, 0:D].unsqueeze(1).broadcast_to([32, C, D]),
                                b2m[:, :].unsqueeze(2).broadcast_to([32, C, D]), ALU.mult).then_inc(s_b2b, 1)
                for n in range(2):
                    dve.wait_ge(s_w2_ps, 4 + n + 1)
                    v.tensor_copy(w2r[:, 4 * n:4 * n + 4, :].rearrange(g3), pb[:, n, :]).then_inc(s_ready_v, 1)
                dve.wait_ge(s_b2h, 1)
                v.tensor_tensor(b2p[64:96, :, :], b2b[:, :, :], b2p[0:32, :, :].bitcast(F32), ALU.subtract
                                ).then_inc(s_b2l, 1)

            def gate_weights():
                dve.wait_ge(s_gate_w, 64)
                v.tensor_copy(wgq[:, :].rearrange("d (j h) -> d j h", j=2), wgr[:, 0])
                v.tensor_tensor(wgc[:, :].rearrange("d (j h) -> d j h", j=2), wgr[:, 1], wgr[:, 2],
                                ALU.add).then_inc(s_gates_v, 1)

            def fixed_rows():
                dve.wait_ge(s_pool, POOL_STEPS)
                v.tensor_copy(el[:, :, :, :], elc[:, :, :, :])
                v.tensor_copy(er[:, :, :, :], erc[:, :, :, :])

            def statistics(src, link):
                for c in range(C):
                    ins = v.bn_stats(st[:, c, :], src[:, c, :])
                link(ins)
                v.tensor_tensor(sdif[:, :], st[:, :, 1], st[:, :, 4], ALU.subtract)
                v.tensor_tensor(ssum[:, :], st[:, :, 1], st[:, :, 4], ALU.add)
                link(v.tensor_tensor(ssq[:, :], st[:, :, 2], st[:, :, 5], ALU.add))
                v.tensor_scalar(mean[:, :], ssum[:, :], 0.5, None, ALU.mult)
                link(v.scalar_tensor_tensor(out=sdif[:, :], in0=sdif[:, :], scalar=0.25, in1=sdif[:, :],
                                            op0=ALU.mult, op1=ALU.mult))
                link(v.scalar_tensor_tensor(out=vr[:, :], in0=ssq[:, :], scalar=1.0 / D, in1=sdif[:, :],
                                            op0=ALU.mult, op1=ALU.add))

            def query_stats(u, par, link):
                dve.wait_ge(s_x[par], 8 * (u - par) + 16)
                statistics(xs[:, par], link)
                v.tensor_scalar(var[:, :], vr[:, :], EPS_NORM, None, ALU.add).then_inc(s_xvar, 1)

            def query_norm(u, par):
                dve.wait_ge(s_xrstd, u + 1)
                after(dve, s_xqT_ps, u)
                for c in range(C):
                    ins = v.tensor_scalar(xq[:, c, :], xs[:, par, c, :], mean[:, c:c + 1], rstd[:, c:c + 1],
                                          ALU.subtract, ALU.mult)
                ins.then_inc(s_xq, 1)

            def context_t(u):
                dve.wait_ge(s_cT_ps, u + 1)
                after(dve, s_qk, 2 * u)
                v.tensor_copy(cT[:, :], pa[:, 1, :]).then_inc(s_cT, 1)

            def decay_rows(u, link):
                dve.wait_ge(s_fln, u + 1)
                link(v.scalar_tensor_tensor(out=lf[:, :], in0=gr[:, 1, :], scalar=0.0, in1=fln[:, :],
                                            op0=ALU.min, op1=ALU.subtract))
                link(v.tensor_tensor_scan(cum[:, :], ones_row[:, :], lf[:, :], 0.0, ALU.mult, ALU.add))
                link(v.tensor_tensor(av[:, :], gr[:, 0, :], cum[:, :], ALU.subtract))
                link(v.tensor_tensor_scan(mx[:, :], av[:, :], av[:, :], -3.0e38, ALU.max, ALU.max))
                v.tensor_tensor(mld[:, :], cum[:, :], mx[:, :], ALU.add).then_inc(s_mld, 1)
                v.tensor_copy(gs[0:32, :], av[:, :])
                link(v.tensor_scalar(ms[0:32, :], mx[:, :], -1.0, None, ALU.mult))
                v.tensor_tensor(gs[32:64, :], av[:, :], gs[0:32, :].bitcast(F32), ALU.subtract)
                v.scalar_tensor_tensor(out=ms[32:64, :], in0=mx[:, :], scalar=-1.0, in1=ms[0:32, :].bitcast(F32),
                                       op0=ALU.mult, op1=ALU.subtract).then_inc(s_gs, 1)

            def decayed(u):
                after(dve, s_pv, u)
                for n, q in enumerate((1, 0)):
                    dve.wait_ge(s_qk, 2 * u + n + 1)
                    dve.wait_ge(s_d, 2 * u + n + 1)
                    v.scalar_tensor_tensor(out=ct[:, 2 * q:2 * q + 2, :].rearrange("p k n -> p (k n)"),
                                           in0=pa[:, q, :], scalar=QK_SCALE,
                                           in1=dm[:, 2 * q:2 * q + 2, :].rearrange("p k n -> p (k n)"),
                                           op0=ALU.mult, op1=ALU.mult).then_inc(s_ct, 1)

            def heads(u, link):
                dve.wait_ge(s_pv, u + 1)
                dve.wait_ge(s_enm, u + 1)
                hu = pa[:, 2:4, 0:2 * NH * V1].rearrange("p q (n d) -> p q n d", d=V1)
                link(v.scalar_tensor_tensor(out=den[:, :, :], in0=hu[:, :, :, DH], scalar=-1.0, in1=enm[:, :, :],
                                            op0=ALU.mult, op1=ALU.max))
                link(v.tensor_tensor(den[:, :, :], hu[:, :, :, DH], den[:, :, :], ALU.max))
                link(v.tensor_scalar(den[:, :, :], den[:, :, :], EPS_DEN, None, ALU.add))
                link(v.reciprocal(den[:, :, :], den[:, :, :]))
                for q in range(2):
                    ins = v.tensor_tensor(
                        hm[:, 2 * NH * q:2 * NH * q + 2 * NH, :].rearrange("p (b h) d -> p h b d", b=2),
                        hu[:, q, :, 0:DH].rearrange("p (h b) d -> p h b d", b=2),
                        den[:, q, :].rearrange("p (h b) -> p h b", b=2).unsqueeze(3).broadcast_to([P, NH, 2, DH]),
                        ALU.mult)
                ins.then_inc(s_hm, 1)
                dve.wait_ge(s_hm, u + 1)
                link(v.reduce_sum(hsum[:, :], hm[:, :, :], AX_X))
                link(v.tensor_scalar(hmean[:, :], hsum[:, :], -1.0 / DH, None, ALU.mult))
                v.tensor_tensor(hc[:, :, :], hm[:, :, :], hmean[:, :].unsqueeze(2).broadcast_to([P, C * NH, DH]),
                                ALU.add).then_inc(s_hc, 1)

            def head_variance(u, link):
                dve.wait_ge(s_hsq, u + 1)
                link(v.reduce_sum(hsum[:, :], hsq[:, :, :], AX_X))
                v.tensor_scalar(hvar[:, :], hsum[:, :], 1.0 / DH, EPS_HEAD, ALU.mult, ALU.add).then_inc(s_hvar, 1)

            def head_scale(u):
                dve.wait_ge(s_hrs, u + 1)
                v.tensor_tensor(ha[:, :, :], hc[:, :, :], hrs[:, :].unsqueeze(2).broadcast_to([P, C * NH, DH]),
                                ALU.mult).then_inc(s_ha, 1)

            def norm_stats(u, link):
                dve.wait_ge(s_x1, u + 1)
                statistics(x1, link)
                v.tensor_scalar(v2[:, :], vr[:, :], EPS_NORM, None, ALU.add).then_inc(s_v2, 1)

            def second_variance(u, link):
                dve.wait_ge(s_r1, u + 1)
                link(v.tensor_tensor(rr[:, :], r1[:, :], r1[:, :], ALU.mult))
                link(v.tensor_tensor(rr[:, :], rr[:, :], vr[:, :], ALU.mult))
                v.tensor_scalar(v2e[:, :], rr[:, :], EPS_NORM, None, ALU.add).then_inc(s_v2e, 1)
                v.scalar_tensor_tensor(out=nm[:, :], in0=mean[:, :], scalar=-1.0, in1=r1[:, :],
                                       op0=ALU.mult, op1=ALU.mult)
                v.tensor_scalar(p1[:, :], r1[:, :], 1.0, None, ALU.add).then_inc(s_nm, 1)

            def norm_apply(u, link):
                dve.wait_ge(s_r2, u + 1)
                link(v.tensor_tensor(rr[:, :], r1[:, :], r2[:, :], ALU.mult))
                after(dve, s_yT_ps, u)
                for c in range(C):
                    ins = v.tensor_scalar(yh[:, c, :], x1[:, c, :], mean[:, c:c + 1], rr[:, c:c + 1],
                                          ALU.subtract, ALU.mult)
                ins.then_inc(s_yh, 1)

            def norm_split(u, par, link):
                dve.wait_ge(s_xn, u + 1)
                link(v.tensor_copy(xnh[:, par, :], xn[:, par, :]))
                v.tensor_tensor(xnl[:, par, :], xn[:, par, :], xnh[:, par, :].bitcast(F32),
                                ALU.subtract).then_inc(s_xns, 1)

            def top_one(src, key, hot, top, link):
                def row(m):
                    return m[:, :].unsqueeze(2).broadcast_to([P, C, E])
                link(v.reduce_max(top[:, :], src[:, :, :], AX_X))
                link(v.tensor_tensor(key[:, :, :], src[:, :, :], row(top), ALU.is_ge))
                link(v.tensor_tensor(key[:, :, :], key[:, :, :], rev[:, :].unsqueeze(1).broadcast_to([P, C, E]),
                                     ALU.mult))
                link(v.reduce_max(kk[:, :], key[:, :, :], AX_X))
                link(v.tensor_tensor(hot[:, :, :], key[:, :, :], row(kk), ALU.is_equal))

            def first_expert(u, link):
                dve.wait_ge(s_lg_ps, u + 1)
                parts = [(slice(0, 3), pa[:, 1, 0:3 * (D + E)].rearrange("p (c n) -> p c n", c=3), 3),
                         (slice(3, 4), pa[:, 0, 0:D + E].unsqueeze(1), 1)]
                for blocks, product, n in parts:
                    ins = v.tensor_tensor(lg[:, blocks, :], product[:, :, D:D + E],
                                          bmg[:, :].unsqueeze(1).broadcast_to([P, n, E]), ALU.add)
                ins.then_inc(s_lg, 1)
                after(dve, s_ab, u)
                for blocks, product, n in parts:
                    ins = v.tensor_tensor(abp[:, blocks, :], product[:, :, 0:D],
                                          bab[:, :].unsqueeze(1).broadcast_to([P, n, D]), ALU.add)
                ins.then_inc(s_abp, 1)
                dve.wait_ge(s_lg, u + 1)
                top_one(lg, k1, o1, m1, link)

            def second_expert(u, link):
                link(v.scalar_tensor_tensor(out=lg2[:, :, :], in0=o1[:, :, :], scalar=-3.0e38, in1=lg[:, :, :],
                                            op0=ALU.mult, op1=ALU.add))
                top_one(lg2, k2, o2, m2, link)
                v.tensor_tensor(dl[:, :], m1[:, :], m2[:, :], ALU.subtract).then_inc(s_dl, 1)

            def expert_weights(u, par, link):
                dve.wait_ge(s_th, u + 1)
                v.tensor_scalar(wa[:, :], th[:, :], 0.5, 0.5, ALU.mult, ALU.add)
                link(v.tensor_scalar(wb[:, :], th[:, :], -0.5, 0.5, ALU.mult, ALU.add))
                v.tensor_tensor(k1[:, :, :], o1[:, :, :], wa[:, :].unsqueeze(2).broadcast_to([P, C, E]), ALU.mult)
                link(v.tensor_tensor(k2[:, :, :], o2[:, :, :], wb[:, :].unsqueeze(2).broadcast_to([P, C, E]),
                                     ALU.mult))
                v.tensor_tensor(wr[:, par], k1[:, :, :], k2[:, :, :], ALU.add).then_inc(s_w, 1)

            def weights_t(u):
                dve.wait_ge(s_wT_ps, u + 1)
                weights = pa[0:32, 3, WT_COL:WT_COL + P]
                v.tensor_copy(wT[0:32, :], weights).then_inc(s_wTh, 1)
                v.tensor_copy(wT[64:96, :], weights)
                dve.wait_ge(s_wTh, u + 1)
                v.tensor_tensor(wT[32:64, :], weights, wT[0:32, :].bitcast(F32), ALU.subtract).then_inc(s_wT, 1)

            def second_bias(t, par):
                dve.wait_ge(s_y, JOBS * t + BIAS_JOB)
                dve.wait_ge(s_y_ps, JOBS * t + BIAS_JOB + 1)
                v.tensor_tensor(acc[:, par], pb[:, job_bank(par, BIAS_JOB), :].rearrange("p (c d) -> p c d", c=C),
                                acc[:, par], ALU.add).then_inc(s_y, 1)

            def expert(t, par, e):
                job = job_of(e)
                if e == 0:
                    after(dve, s_db, t - 1)
                    dve.wait_ge(s_w, t + 1)
                else:
                    dve.wait_ge(s_y, JOBS * t + job)
                dve.wait_ge(s_y_ps, JOBS * t + job + 1)
                for c in range(C):
                    product, weight = pb[:, job_bank(par, job), D * c:D * c + D], wr[:, par, c, e:e + 1]
                    if e == 0:
                        ins = v.tensor_scalar(acc[:, par, c, :], product, weight, None, ALU.mult)
                    else:
                        ins = v.scalar_tensor_tensor(out=acc[:, par, c, :], in0=product, scalar=weight,
                                                     in1=acc[:, par, c, :], op0=ALU.mult, op1=ALU.add)
                ins.then_inc(s_y, 1)

            def mix_gate(t):
                dve.wait_ge(s_zz, t + 1)
                v.reduce_sum(zs[:, :], zz[:, :, :], AX_X).then_inc(s_zs, 1)

            def mixed(t, par, link):
                dve.wait_ge(s_zt, t + 1)
                link(v.tensor_scalar(gate[:, :], zt[:, :], 0.5, 0.5, ALU.mult, ALU.add))
                dve.wait_ge(s_db, t + 1)
                after(dve, s_out[par], 8 * (t - par))
                for c in range(C):
                    ins = v.scalar_tensor_tensor(out=res[:, par, c, :], in0=diff[:, c, :], scalar=gate[:, c:c + 1],
                                                 in1=bab2[:, c, :], op0=ALU.mult, op1=ALU.add)
                ins.then_inc(s_res, 1)

            def turn(t, par, attend=True, route=True):
                link_q = Links(dve, s_v_query, VECTOR_QUERY, t + 2)
                link_r = Links(dve, s_v_route, VECTOR_ROUTE, t)
                if attend:
                    query_stats(t + 2, par, link_q)
                    link_q.end()
                if route:
                    norm_split(t, par, link_r)
                if attend:
                    query_norm(t + 2, par)
                if route:
                    first_expert(t, link_r)
                expert(t - 1, 1 - par, 6)
                if attend:
                    context_t(t + 2)
                if route:
                    second_expert(t, link_r)
                expert(t - 1, 1 - par, 7)
                if route:
                    expert_weights(t, par, link_r)
                    link_r.end()

            def main(t, par, attend=True, norm=True, mix=True):
                w, u, other = t + 2, t + 1, 1 - par
                link_a = Links(dve, s_v_attend, VECTOR_ATTEND, w)
                link_n = Links(dve, s_v_norm, VECTOR_NORM, u)
                link_m = Links(dve, s_v_mix, VECTOR_MIX, t - 1)
                if norm:
                    heads(u, link_n)
                expert(t, par, 0)
                if norm:
                    head_variance(u, link_n)
                expert(t, par, 1)
                expert(t, par, 2)
                if norm:
                    head_scale(u)
                weights_t(t)
                if attend:
                    decay_rows(w, link_a)
                expert(t, par, 3)
                if norm:
                    norm_stats(u, link_n)
                if mix:
                    mix_gate(t - 1)
                expert(t, par, 4)
                if norm:
                    second_variance(u, link_n)
                second_bias(t, par)
                if norm:
                    norm_apply(u, link_n)
                if attend:
                    decayed(w)
                expert(t, par, 5)
                if mix:
                    mixed(t - 1, other, link_m)
                for stage, link in ((attend, link_a), (norm, link_n), (mix, link_m)):
                    if stage:
                        link.end()

            link_a = Links(dve, s_v_attend, VECTOR_ATTEND, 0)
            query_stats(0, 0, Links(dve, s_v_query, VECTOR_QUERY, 0))
            query_norm(0, 0)
            gate_weights()
            context_t(0)
            exp_start()
            exp_step(0)
            exp_step(1)
            fixed_rows()
            decay_rows(0, link_a)
            exp_step(2)
            exp_step(3)
            query_stats(1, 1, Links(dve, s_v_query, VECTOR_QUERY, 1))
            query_norm(1, 1)
            decayed(0)
            exp_step(4)
            link_a.end()
            link_a = Links(dve, s_v_attend, VECTOR_ATTEND, 1)
            link_n = Links(dve, s_v_norm, VECTOR_NORM, 0)
            context_t(1)
            heads(0, link_n)
            exp_step(5)
            head_variance(0, link_n)
            exp_step(6)
            head_scale(0)
            exp_step(7)
            norm_stats(0, link_n)
            exp_step(8)
            second_variance(0, link_n)
            exp_step(9)
            norm_apply(0, link_n)
            decay_rows(1, link_a)
            exp_step(10)
            link_r = Links(dve, s_v_route, VECTOR_ROUTE, 0)
            norm_split(0, 0, link_r)
            exp_step(11)
            dve.wait_ge(s_early, N_EARLY)
            v.tensor_scalar(hgcb[:, :], gcb[:, :], 0.5, None, ALU.mult)
            first_expert(0, link_r)
            exp_step(12)
            exp_step(13)
            biases_transposed()
            rotation(0)
            decayed(1)
            rotation(1)
            query_stats(2, 0, Links(dve, s_v_query, VECTOR_QUERY, 2))
            second_expert(0, link_r)
            query_norm(2, 0)
            expert_weights(0, 0, link_r)
            expert_weights_turned()
            context_t(2)
            link_a.end()
            link_n.end()
            link_r.end()

            main(0, 0, mix=False)
            turn(1, 1)
            main(1, 1)
            with dve.Fori(1, TILES // 2 - 1) as i:
                for par in range(2):
                    turn(2 * i + par, par)
                    main(2 * i + par, par)
            turn(TILES - 2, 0, attend=False)
            main(TILES - 2, 0, attend=False)
            turn(TILES - 1, 1, attend=False)
            main(TILES - 1, 1, attend=False, norm=False)
            turn(TILES, 0, attend=False, route=False)
            mix_gate(TILES - 1)
            mixed(TILES - 1, 1, Links(dve, s_v_mix, VECTOR_MIX, TILES - 1))

        @block.tensor
        def _(pe):
            m = nc.tensor

            def exp_start():
                pe.wait_ge(s_gens, 16)
                pe.wait_ge(s_pool, 2)
                for n in range(NROT):
                    ins = m.transpose(pb[:, 0, P * n:P * n + P], ga[:, n, :], ident[:, :])
                ins.then_inc(s_gat_ps, 1)

            def exp_step(n):
                pe.wait_ge(s_exp_t, n + 1)
                pe.wait_ge(s_exp_u, n + 1)
                for r in range(NROT):
                    t_, u_ = tm[:, n % 2, r, :], um[:, n % 2, r, :]
                    squaring = n >= DEGREE - 1
                    m.matmul(pb[:, 0, P * r:P * r + P], u_ if squaring else gat[:, r, :], t_, start=True, stop=True)
                    ins = m.matmul(pb[:, 1, P * r:P * r + P], t_ if squaring else ga[:, r, :], u_,
                                   start=True, stop=True)
                ins.then_inc(s_exp_ps, 1)

            def rotation(n):
                fin = EXP_STEPS % 2
                if n == 0:
                    pe.wait_ge(s_b1, 1)
                    pe.wait_ge(s_exp_t, EXP_STEPS + 1)
                    pe.wait_ge(s_exp_u, EXP_STEPS + 1)
                    right = tm[:, fin, 2, :]
                else:
                    pe.wait_ge(s_rot, 1)
                    right = rot[:, 0, :]
                m.matmul(pb[:, 2 + n, 0:D], um[:, fin, 1 - n, :], right, start=True, stop=True).then_inc(s_rot_ps, 1)

            def second_weights_t(half):
                pe.wait_ge(s_w2, 16)
                if half == 1:
                    pe.wait_ge(s_w2t, 2)
                for n in range(E):
                    ins = m.transpose(pb[:, 2 + n // 4, P * (n % 4):P * (n % 4) + P], w2s[:, E * half + n, :],
                                      ident[:, :])
                    if n % 4 == 3:
                        ins.then_inc(s_w2_ps, 1)

            def biases_t():
                pe.wait_ge(s_early, N_EARLY)
                pe.wait_ge(s_w2t, 4)
                m.transpose(pb[:, 2, 0:E * HF], b1row[:, :], ident[0:E * HF, 0:E * HF])
                m.transpose(pb[:, 2, E * HF:E * HF + E], b2s[:, :], ident[0:E, 0:E]).then_inc(s_b1_ps, 1)

            def expert_weights_turned():
                pe.wait_ge(s_rot, 2)
                m.matmul(pa[0:32, 1, 0:D], b2t[:, :, :].rearrange("p c e -> p (c e)"), rot[:, 1, :],
                         start=True, stop=True).then_inc(s_b1_ps, 1)
                for n in range(E * HF):
                    ins = m.matmul(pb[:, n // 4, P * (n % 4):P * (n % 4) + P], w2t[:, n, :], rot[:, 1, :],
                                   start=True, stop=True)
                    if n % 4 == 3:
                        ins.then_inc(s_w2_ps, 1)

            def transposes(u, par):
                pe.wait_ge(s_xq, u + 1)
                after(pe, s_ct, 2 * u)
                after(pe, s_abp, u - 1)
                for c in range(C):
                    ins = m.transpose(pa[:, 0, P * c:P * c + P], xq[:, c, :], ident[:, :])
                ins.then_inc(s_xqT_ps, 1)
                pe.wait_ge(s_c[par], 32 * (u - par) + 64)
                for k in range(C):
                    ins = m.transpose(pa[:, 1, P * k:P * k + P], cs[:, par, k, :], ident[:, :])
                ins.then_inc(s_cT_ps, 1)

            def gates(u):
                pe.wait_ge(s_xqT, u + 1)
                pe.wait_ge(s_cT, u + 1)
                for q in range(2):
                    cols = slice(256 * q, 256 * q + 256)
                    m.matmul(pa[0:2 * NH, 1, cols], wgq[:, :],
                             xqT[:, cols].rearrange("d (b g s) -> d g b s", b=2, g=2), start=True, stop=False)
                    ins = m.matmul(pa[0:2 * NH, 1, cols], wgc[:, :], cT[:, cols], start=False, stop=True)
                ins.then_inc(s_g_ps, 1)

            def scores(u):
                pe.wait_ge(s_xbd, u + 1)
                pe.wait_ge(s_gT, u + 1)
                for q in (1, 0):
                    for g in range(2):
                        for b in range(2):
                            k = 2 * q + g
                            ins = m.matmul(pa[S * b:S * b + S, q, 256 * g:256 * g + 256],
                                           cT[:, P * k + S * b:P * k + S * b + S],
                                           xbd[:, 4 * q + 2 * b + g, :, :].rearrange("d h s -> d (h s)"),
                                           start=True, stop=True)
                    ins.then_inc(s_qk, 1)

            def exponents(u, q):
                if q == 1:
                    pe.wait_ge(s_mld, u + 1)
                    after(pe, s_hm, u)
                    for g in range(2):
                        pick = ident[0:32, 0:32].rearrange("r (h q g b) -> r g q h b", h=NH, q=2, g=2)[:, g]
                        for n in range(2):
                            ins = m.matmul(pa[S * g:S * g + S, 2, 8 * n:8 * n + 8], mld[:, :], pick[:, n],
                                           start=True, stop=True)
                    ins.then_inc(s_enm_ps, 1)
                    pe.wait_ge(s_erow, 48 * u + 48)
                else:
                    pe.wait_ge(s_enm, u + 1)
                for g in range(2):
                    k = 2 * q + g
                    ins = m.matmul(pa[:, 2 + q, 256 * g:256 * g + 256], el[:, k].rearrange("r b t -> r (b t)"),
                                   er[:, :, k, :], start=True, stop=True)
                ins.then_inc(s_e, 1)

            def values(u):
                pe.wait_ge(s_vbd, u + 1)
                for n, q in enumerate((1, 0)):
                    pe.wait_ge(s_ct, 2 * u + n + 1)
                    for g in range(2):
                        k = 2 * q + g
                        for h in range(NH):
                            ins = m.matmul(pa[S * g:S * g + S, 2 + q, 2 * V1 * h:2 * V1 * h + 2 * V1],
                                           ct[:, k, S * h:S * h + S],
                                           vbd[:, k, h].rearrange("p b d -> p (b d)"), start=True, stop=True)
                ins.then_inc(s_pv, 1)

            def norm_t(u):
                pe.wait_ge(s_yh, u + 1)
                for c in range(C):
                    ins = m.transpose(pa[:, 0, P * c:P * c + P], yh[:, c, :], ident[:, :])
                ins.then_inc(s_yT_ps, 1)

            def logits(u, par):
                pe.wait_ge(s_xn, u + 1)
                for c in range(C):
                    bank, col = (1, (D + E) * c) if c < 3 else (0, 0)
                    ins = m.matmul(pa[:, bank, col:col + D + E], xn[:, par, P * c:P * c + P], wabg[:, :],
                                   start=True, stop=True)
                ins.then_inc(s_lg_ps, 1)

            def weights_t(t, par):
                pe.wait_ge(s_w, t + 1)
                m.transpose(pa[0:32, 3, WT_COL:WT_COL + P], wr[:, par].rearrange("p c e -> p (c e)"),
                            ident[:, :]).then_inc(s_wT_ps, 1)

            def second_bias(t, par):
                pe.wait_ge(s_b2h, 2)
                pe.wait_ge(s_b2l, 1)
                pe.wait_ge(s_wT, t + 1)
                pe.wait_ge(s_y, JOBS * t + BIAS_JOB - 1)
                m.matmul(pb[:, job_bank(par, BIAS_JOB), :], wT[:, :], b2p[:, :, :].rearrange("r c d -> r (c d)"),
                         start=True, stop=True).then_inc(s_y_ps, 1)

            def hidden(t, par, e):
                if e == 0:
                    pe.wait_ge(s_xns, t + 1)
                for f in range(HF):
                    after(pe, s_h, 16 * t + max(0, 2 * e + f - 1))
                    cols = slice(P * f, P * f + P)
                    m.matmul(pb[:, f, :], w1l[:, e, cols], xnh[:, par, :], start=True, stop=False)
                    m.matmul(pb[:, f, :], w1h[:, e, cols], xnl[:, par, :], start=False, stop=False)
                    m.matmul(pb[:, f, :], w1h[:, e, cols], xnh[:, par, :], start=False,
                             stop=True).then_inc(s_h_ps, 1)

            def output(t, par, e):
                job = job_of(e)
                after(pe, s_y, JOBS * t + job - 1)
                pe.wait_ge(s_h, 16 * t + 2 * e + 2)
                for c in range(C):
                    for f in range(HF):
                        ins = m.matmul(pb[:, job_bank(par, job), D * c:D * c + D], hT[:, e % 2, f, P * c:P * c + P],
                                       w2r[:, HF * e + f, :], start=(f == 0), stop=(f == HF - 1))
                ins.then_inc(s_y_ps, 1)

            def body(t, par, attend=True, norm=True):
                w, u, other = t + 2, t + 1, 1 - par
                hidden(t, par, 0)
                if attend:
                    transposes(w, par)
                hidden(t, par, 1)
                output(t, par, 0)
                if attend:
                    gates(w)
                hidden(t, par, 2)
                output(t, par, 1)
                hidden(t, par, 3)
                output(t, par, 2)
                weights_t(t, par)
                hidden(t, par, 4)
                output(t, par, 3)
                if attend:
                    scores(w)
                hidden(t, par, 5)
                output(t, par, 4)
                hidden(t, par, 6)
                second_bias(t, par)
                if attend:
                    exponents(w, 1)
                output(t, par, 5)
                if attend:
                    exponents(w, 0)
                hidden(t, par, 7)
                if attend:
                    values(w)
                if norm:
                    norm_t(u)
                output(t, par, 6)
                if norm:
                    logits(u, other)
                output(t, par, 7)

            pe.wait_ge(s_pool, 2)
            transposes(0, 0)
            exp_start()
            pe.wait_ge(s_gates_v, 1)
            gates(0)
            exp_step(0)
            exp_step(1)
            scores(0)
            exp_step(2)
            second_weights_t(0)
            exp_step(3)
            pe.wait_ge(s_pool, POOL_STEPS)
            exponents(0, 1)
            exponents(0, 0)
            exp_step(4)
            values(0)
            transposes(1, 1)
            gates(1)
            exp_step(5)
            exp_step(6)
            second_weights_t(1)
            exp_step(7)
            exp_step(8)
            exp_step(9)
            exp_step(10)
            pe.wait_ge(s_xbd, 2)
            pe.wait_ge(s_gT, 2)
            norm_t(0)
            exp_step(11)
            pe.wait_ge(s_early, N_EARLY)
            logits(0, 0)
            exp_step(12)
            pe.wait_ge(s_abp, 1)
            scores(1)
            exp_step(13)
            biases_t()
            exponents(1, 1)
            rotation(0)
            exponents(1, 0)
            rotation(1)
            expert_weights_turned()
            values(1)
            pe.wait_ge(s_b2b, 1)
            pe.wait_ge(s_ready_v, 2)
            pe.wait_ge(s_w2r, 2)
            pe.wait_ge(s_w1l, 1)

            body(0, 0)
            body(1, 1)
            with pe.Fori(1, TILES // 2 - 1) as i:
                body(2 * i, 0)
                body(2 * i + 1, 1)
            body(TILES - 2, 0, attend=False)
            body(TILES - 1, 1, attend=False, norm=False)


_INS = ['x', 'ctx_1024', 'L0_xattn_ig_kernel', 'L0_xattn_ig_bias', 'L0_xattn_fg_kernel', 'L0_xattn_fg_bias',
        'L0_xattn_outnorm_weight', 'L0_ffn_ln_gamma', 'L0_ffn_ln_beta', 'L0_ffn_abel_w', 'L0_ffn_abel_b',
        'L0_ffn_moe_gate_w', 'L0_ffn_moe_gate_b', 'L0_ffn_ew1', 'L0_ffn_eb1', 'L0_ffn_ew2', 'L0_ffn_eb2',
        'L0_ffn_gens', 'L0_ffn_gc_w', 'L0_ffn_gc_b']


def kernel(**inputs):
    import numpy as _np
    import concourse.bacc as _bacc
    from concourse import mybir as _mybir
    from concourse.bass_utils import run_bass_kernel_spmd as _run

    nc = _bacc.Bacc("TRN2", target_bir_lowering=False, num_devices=1)
    arrays, args = {}, []
    for name in _INS:
        a = _np.ascontiguousarray(inputs[name])
        arrays[f"in_{name}_dram"] = a
        args.append(nc.dram_tensor(f"in_{name}_dram", a.shape, _mybir.dt.from_np(a.dtype), kind="ExternalInput").ap())
    shape = inputs["x"].shape
    args.append(nc.dram_tensor("out_0_dram", shape, _mybir.dt.float32, kind="ExternalOutput").ap())
    build(nc, *args)
    r = _run(nc, [arrays], core_ids=[0])
    return r.results[0]["out_0_dram"]
```
